# Optimizing a Trainium2 kernel written in Bass

```python
import numpy as np
import jax
import jax.numpy as jnp

def _softmax(x, axis=-1):
    return jax.nn.softmax(x, axis=axis)

def _gelu(x):
    return jax.nn.gelu(x, approximate=True)

def _silu(x):
    return jax.nn.silu(x)

def _sigmoid(x):
    return jax.nn.sigmoid(x)

def _layernorm(x, axis=-1, eps=1e-05):
    m = jnp.mean(x, axis=axis, keepdims=True)
    v = jnp.var(x, axis=axis, keepdims=True)
    return (x - m) / jnp.sqrt(v + eps)

def _scatter_add(tgt, idx, src, axis=0):
    return tgt.at[idx].add(src)

def _segment_sum(src, seg, n):
    return jax.ops.segment_sum(src, seg, n)
kernel_name = 'mk_macaron_d1_jaxref_r4_f9b17d'

def setup_inputs(seed: int=0):
    np.random.seed(seed)
    _w = jnp.asarray

    def _L0_attn_setup():
        import jax, jax.numpy as jnp
        from jax import lax
        import numpy as np
        B, T, HID = (1, 512, 512)
        H, DQ, DV, K = (16, 128, 128, 4)
        SCALE = DQ ** (-0.5)
        LN_EPS = 1e-05

        def _causal_depthwise_conv(x, w, b):
            C = w.shape[0]
            out = lax.conv_general_dilated(x.transpose(0, 2, 1), w[:, None, :], window_strides=(1,), padding=[(K - 1, 0)], feature_group_count=C, dimension_numbers=('NCH', 'OIH', 'NCH'))
            return (out + b[None, :, None]).transpose(0, 2, 1)

        def _delta_scan(q, k, v, a, beta):
            N = q.shape[0]

            def step(S, inp):
                q_t, k_t, v_t, a_t, b_t = inp
                sk = jnp.einsum('ndq,nq->nd', S, k_t)
                err = sk - v_t
                S = S * a_t[:, :, None] - (b_t[:, None] * err)[:, :, None] * k_t[:, None, :]
                o_t = jnp.einsum('ndq,nq->nd', S, q_t)
                return (S, o_t)
            S0 = jnp.zeros((N, DV, DQ), dtype=q.dtype)
            xs = (q.transpose(1, 0, 2), k.transpose(1, 0, 2), v.transpose(1, 0, 2), a.transpose(1, 0, 2), beta.transpose(1, 0))
            _, o = lax.scan(step, S0, xs)
            return o.transpose(1, 0, 2)
        key = jax.random.key(seed)
        ks = jax.random.split(key, 16)
        s = HID ** (-0.5)
        sc = K ** (-0.5)
        return {'x': jax.random.normal(ks[0], (B, T, HID), jnp.float32), 'Wq': jax.random.normal(ks[1], (H * DQ, HID), jnp.float32) * s, 'Wk': jax.random.normal(ks[2], (H * DQ, HID), jnp.float32) * s, 'Wv': jax.random.normal(ks[3], (H * DV, HID), jnp.float32) * s, 'Wa': jax.random.normal(ks[4], (H * DV, HID), jnp.float32) * s, 'ba': jnp.zeros((H * DV,), jnp.float32), 'Wb': jax.random.normal(ks[5], (H, HID), jnp.float32) * s, 'bb': jnp.zeros((H,), jnp.float32), 'qconv_w': jax.random.normal(ks[6], (H * DQ, K), jnp.float32) * sc, 'qconv_b': jnp.zeros((H * DQ,), jnp.float32), 'kconv_w': jax.random.normal(ks[7], (H * DQ, K), jnp.float32) * sc, 'kconv_b': jnp.zeros((H * DQ,), jnp.float32), 'vconv_w': jax.random.normal(ks[8], (H * DV, K), jnp.float32) * sc, 'vconv_b': jnp.zeros((H * DV,), jnp.float32), 'Wg': jax.random.normal(ks[9], (H * DV, HID), jnp.float32) * s, 'Wo': jax.random.normal(ks[10], (HID, H * DV), jnp.float32) * s, 'ln_w': jnp.ones((DV,), jnp.float32), 'ln_b': jnp.zeros((DV,), jnp.float32)}
    _L0_attn_in = _L0_attn_setup()

    def _L0_ffn_setup():
        import jax, jax.numpy as jnp
        import numpy as np
        HIDDEN = 512
        INTER = 1376
        LUT_SIZE = 16

        def _ghost_linear(x, idx, lut):
            w = lut[idx]
            return jnp.einsum('bsh,oh->bso', x, w)
        key = jax.random.key(seed)
        k_x, k_lut, k_g, k_u, k_d = jax.random.split(key, 5)
        x = jax.random.normal(k_x, (2, 1024, HIDDEN), dtype=jnp.float32)
        lut = jax.random.normal(k_lut, (LUT_SIZE,), dtype=jnp.float32) * 0.02
        gate_idx = jax.random.randint(k_g, (INTER, HIDDEN), 0, LUT_SIZE, dtype=jnp.int32)
        up_idx = jax.random.randint(k_u, (INTER, HIDDEN), 0, LUT_SIZE, dtype=jnp.int32)
        down_idx = jax.random.randint(k_d, (HIDDEN, INTER), 0, LUT_SIZE, dtype=jnp.int32)
        return {'x': x, 'lut': lut, 'gate_idx': gate_idx, 'up_idx': up_idx, 'down_idx': down_idx}
    _L0_ffn_in = _L0_ffn_setup()
    _d = {'L0_attn_x': _L0_attn_in['x'], 'L0_attn_Wq': _L0_attn_in['Wq'], 'L0_attn_Wk': _L0_attn_in['Wk'], 'L0_attn_Wv': _L0_attn_in['Wv'], 'L0_attn_Wa': _L0_attn_in['Wa'], 'L0_attn_ba': _L0_attn_in['ba'], 'L0_attn_Wb': _L0_attn_in['Wb'], 'L0_attn_bb': _L0_attn_in['bb'], 'L0_attn_qconv_w': _L0_attn_in['qconv_w'], 'L0_attn_qconv_b': _L0_attn_in['qconv_b'], 'L0_attn_kconv_w': _L0_attn_in['kconv_w'], 'L0_attn_kconv_b': _L0_attn_in['kconv_b'], 'L0_attn_vconv_w': _L0_attn_in['vconv_w'], 'L0_attn_vconv_b': _L0_attn_in['vconv_b'], 'L0_attn_Wg': _L0_attn_in['Wg'], 'L0_attn_Wo': _L0_attn_in['Wo'], 'L0_attn_ln_w': _L0_attn_in['ln_w'], 'L0_attn_ln_b': _L0_attn_in['ln_b'], 'L0_ffn_lut': _L0_ffn_in['lut'], 'L0_ffn_gate_idx': _L0_ffn_in['gate_idx'], 'L0_ffn_up_idx': _L0_ffn_in['up_idx'], 'L0_ffn_down_idx': _L0_ffn_in['down_idx']}
    _x0 = _d['L0_attn_x']
    _d['L0_attn_x'] = jax.random.normal(jax.random.fold_in(jax.random.key(seed), 1), (4, 512, 512), dtype=_x0.dtype)
    del _x0
    return _d

def reference(L0_attn_x, L0_attn_Wq, L0_attn_Wk, L0_attn_Wv, L0_attn_Wa, L0_attn_ba, L0_attn_Wb, L0_attn_bb, L0_attn_qconv_w, L0_attn_qconv_b, L0_attn_kconv_w, L0_attn_kconv_b, L0_attn_vconv_w, L0_attn_vconv_b, L0_attn_Wg, L0_attn_Wo, L0_attn_ln_w, L0_attn_ln_b, L0_ffn_lut, L0_ffn_gate_idx, L0_ffn_up_idx, L0_ffn_down_idx):

    def _L0_attn_ref(x, Wq, Wk, Wv, Wa, ba, Wb, bb, qconv_w, qconv_b, kconv_w, kconv_b, vconv_w, vconv_b, Wg, Wo, ln_w, ln_b):
        import jax, jax.numpy as jnp
        from jax import lax
        import numpy as np
        B, T, HID = (1, 512, 512)
        H, DQ, DV, K = (16, 128, 128, 4)
        SCALE = DQ ** (-0.5)
        LN_EPS = 1e-05

        def _causal_depthwise_conv(x, w, b):
            C = w.shape[0]
            out = lax.conv_general_dilated(x.transpose(0, 2, 1), w[:, None, :], window_strides=(1,), padding=[(K - 1, 0)], feature_group_count=C, dimension_numbers=('NCH', 'OIH', 'NCH'))
            return (out + b[None, :, None]).transpose(0, 2, 1)

        def _delta_scan(q, k, v, a, beta):
            N = q.shape[0]

            def step(S, inp):
                q_t, k_t, v_t, a_t, b_t = inp
                sk = jnp.einsum('ndq,nq->nd', S, k_t)
                err = sk - v_t
                S = S * a_t[:, :, None] - (b_t[:, None] * err)[:, :, None] * k_t[:, None, :]
                o_t = jnp.einsum('ndq,nq->nd', S, q_t)
                return (S, o_t)
            S0 = jnp.zeros((N, DV, DQ), dtype=q.dtype)
            xs = (q.transpose(1, 0, 2), k.transpose(1, 0, 2), v.transpose(1, 0, 2), a.transpose(1, 0, 2), beta.transpose(1, 0))
            _, o = lax.scan(step, S0, xs)
            return o.transpose(1, 0, 2)
        b, t, _ = x.shape
        q = x @ Wq.T
        k = x @ Wk.T
        v = x @ Wv.T
        q = jax.nn.silu(_causal_depthwise_conv(q, qconv_w, qconv_b))
        k = jax.nn.silu(_causal_depthwise_conv(k, kconv_w, kconv_b))
        v = jax.nn.silu(_causal_depthwise_conv(v, vconv_w, vconv_b))
        q = q.reshape(b, t, H, DQ)
        k = k.reshape(b, t, H, DQ) * SCALE
        v = v.reshape(b, t, H, DV)
        a = jax.nn.sigmoid(x @ Wa.T + ba).reshape(b, t, H, DV)
        beta = jax.nn.sigmoid(x @ Wb.T + bb)
        to_n = lambda z: z.transpose(0, 2, 1, 3).reshape(b * H, t, -1)
        o = _delta_scan(to_n(q), to_n(k), to_n(v), to_n(a), beta.transpose(0, 2, 1).reshape(b * H, t))
        o = o.reshape(b, H, t, DV).transpose(0, 2, 1, 3)
        mu = o.mean(-1, keepdims=True)
        var = ((o - mu) ** 2).mean(-1, keepdims=True)
        o = (o - mu) * lax.rsqrt(var + LN_EPS) * ln_w + ln_b
        g = jax.nn.sigmoid(x @ Wg.T).reshape(b, t, H, DV)
        o = (o * g).reshape(b, t, H * DV)
        return o @ Wo.T

    def _L0_ffn_ref(x, lut, gate_idx, up_idx, down_idx):
        import jax, jax.numpy as jnp
        import numpy as np
        HIDDEN = 512
        INTER = 1376
        LUT_SIZE = 16

        def _ghost_linear(x, idx, lut):
            w = lut[idx]
            return jnp.einsum('bsh,oh->bso', x, w)
        gate = _ghost_linear(x, gate_idx, lut)
        up = _ghost_linear(x, up_idx, lut)
        h = jax.nn.silu(gate) * up
        return _ghost_linear(h, down_idx, lut)
    x = L0_attn_x
    x = x + 0.5 * _L0_ffn_ref(_layernorm(x, axis=-1), L0_ffn_lut, L0_ffn_gate_idx, L0_ffn_up_idx, L0_ffn_down_idx)
    x = x + _L0_attn_ref(_layernorm(x, axis=-1), L0_attn_Wq, L0_attn_Wk, L0_attn_Wv, L0_attn_Wa, L0_attn_ba, L0_attn_Wb, L0_attn_bb, L0_attn_qconv_w, L0_attn_qconv_b, L0_attn_kconv_w, L0_attn_kconv_b, L0_attn_vconv_w, L0_attn_vconv_b, L0_attn_Wg, L0_attn_Wo, L0_attn_ln_w, L0_attn_ln_b)
    x = x + 0.5 * _L0_ffn_ref(_layernorm(x, axis=-1), L0_ffn_lut, L0_ffn_gate_idx, L0_ffn_up_idx, L0_ffn_down_idx)
    return x

_drawn_inputs = setup_inputs


def setup_inputs(seed=0):
    import zlib

    import numpy as np

    out = dict(_drawn_inputs(seed))
    spreads = {'L0_attn_ba': (0.0, 0.1),
     'L0_attn_bb': (0.0, 0.657),
     'L0_attn_qconv_b': (0.0, 0.1),
     'L0_attn_kconv_b': (0.0, 0.1),
     'L0_attn_vconv_b': (0.0, 0.1),
     'L0_attn_ln_w': (1.0, 0.2),
     'L0_attn_ln_b': (0.0, 0.1)}
    factors = {}
    for name, (base, spread) in spreads.items():
        noise = np.random.default_rng([zlib.crc32(name.encode()), seed]).standard_normal(out[name].shape)
        drawn = base * np.exp(spread * noise) if base else spread * noise
        out[name] = jnp.asarray(drawn.astype(out[name].dtype))
    for name, factor in factors.items():
        out[name] = (out[name] * factor).astype(out[name].dtype)
    return out
```

```python
from contextlib import ExitStack

import concourse.bass as bass
from concourse import mybir

F32 = mybir.dt.float32
BF16 = mybir.dt.bfloat16
I32 = mybir.dt.int32
ALU = mybir.AluOpType
ACT = mybir.ActivationFunctionType
AX = mybir.AxisListType

P = 128
B, T, HID = 4, 512, 512
TOK = B * T
H, D, K = 16, 128, 4
C = H * D
N = B * H
INTER, LUT = 1376, 16
KH = HID // P
OT = (INTER + P - 1) // P
OLAST = INTER - (OT - 1) * P
BLK = 512
NBLK = TOK // BLK
TT = BLK // P
EPS = 1e-5
S2 = 1.0 / D

CH = 16
SUP = 64
CPS = SUP // CH
NCH = T // CH
DH = 64
NP = N * D // DH
SBLK = 512
NSB = N * D // SBLK
NPB = SBLK // D


def mid(ap, axis, n):
    a = ap.unsqueeze(axis)
    shape = list(a.shape)
    shape[axis] = n
    return a.broadcast_to(shape)


class Steps:

    def __init__(self, sem, per, turn):
        self.sem, self.per, self.turn, self.n = sem, per, turn, 0

    def mark(self, ins):
        ins.then_inc(self.sem, 1)
        self.n += 1
        return self.n

    def wait(self, eng, n):
        eng.wait_ge(self.sem, self.turn * self.per + n)

    def end(self):
        assert self.n == self.per, (self.n, self.per)


class Space:

    def __init__(self, nc, ctx, tag):
        self.nc, self.ctx, self.tag = nc, ctx, tag

    def sb(self, name, shape, dt=F32):
        return self.ctx.enter_context(self.nc.sbuf_tensor(f"{self.tag}_{name}", shape, dt))

    def ps(self, name, n=1, shape=(P, 512), dt=F32):
        t = [self.ctx.enter_context(self.nc.psum_tensor(f"{self.tag}_{name}{j}", list(shape), dt)) for j in range(n)]
        return t if n > 1 else t[0]

    def sem(self, name):
        return self.ctx.enter_context(self.nc.semaphore(f"{self.tag}_{name}"))

    def sems(self, name, n):
        return [self.sem(f"{name}{j}") for j in range(n)]


def identity_step(pool, ident, sem):
    pool.memset(ident[:, :], 0.0).then_inc(sem, 1)
    pool.wait_ge(sem, 1)
    pool.affine_select(out=ident[:, :], in_=ident[:, :], compare_op=ALU.not_equal, fill=1.0, base=0,
                       pattern=[[-1, P]], channel_multiplier=1).then_inc(sem, 1)


def dequantise(nc, wg, wu, wd, lut, gate_idx, up_idx, down_idx, wg_d, wu_d, wd_d):
    with ExitStack() as ctx:
        sp_ = Space(nc, ctx, "dq")
        idx = [sp_.sb(f"idx{j}", [P, KH * INTER + P], I32) for j in range(2)]
        lut_sb = sp_.sb("lut", [P, LUT])
        idxb = [sp_.sb(f"idxb{j}", [P, 1408], BF16) for j in range(2)]
        hot = [sp_.sb(f"hot{j}", [P, 1408], BF16) for j in range(2)]
        lut_in = sp_.sem("lut_in")
        idx_in = sp_.sems("idx_in", 3)
        pad_done = sp_.sem("pad_done")
        cast_done = sp_.sem("cast_done")
        hot_done = sp_.sem("hot_done")
        acc_done = sp_.sem("acc_done")
        stored = sp_.sem("stored")
        nd = OT * HID
        pieces = [(m, idx[m % 2][:, j * INTER:(j + 1) * INTER], w[:, j, :])
                  for m, w in ((0, wg), (1, wu)) for j in range(KH)]
        wdf = wd[:, :, :].rearrange("p a h -> p (a h)")
        pieces += [(2, idx[0][:, j * (nd // 4):(j + 1) * (nd // 4)], wdf[:, j * (nd // 4):(j + 1) * (nd // 4)])
                   for j in range(4)]
        block = ctx.enter_context(nc.Block())

        @block.sync
        def _(sp):
            sp.dma_start(lut_sb[:, :], lut.rearrange("(o k) -> o k", o=1).broadcast_to([P, LUT])).then_inc(lut_in, 16)
            sp.dma_start(idx[0][:, 0:KH * INTER].rearrange("p (k o) -> p k o", k=KH),
                         gate_idx.rearrange("(k p) o -> p k o", p=P)).then_inc(idx_in[0], 16)
            sp.dma_start(idx[1][:, 0:KH * INTER].rearrange("p (k o) -> p k o", k=KH),
                         up_idx.rearrange("(k p) o -> p k o", p=P)).then_inc(idx_in[1], 16)
            sp.wait_ge(cast_done, 4)
            sp.dma_start(idx[0][:, 0:(OT - 1) * HID].rearrange("p (a h) -> p a h", h=HID),
                         down_idx[0:(OT - 1) * P, :].rearrange("(a p) h -> p a h", p=P)).then_inc(idx_in[2], 16)
            sp.dma_start(idx[0][0:OLAST, (OT - 1) * HID:nd], down_idx[(OT - 1) * P:INTER, :]).then_inc(idx_in[2], 16)
            for m, (w, d) in enumerate(((wg, wg_d), (wu, wu_d), (wd, wd_d))):
                sp.wait_ge(acc_done, 4 * LUT * (m + 1))
                sp.dma_start(d, w[:, :, :]).then_inc(stored, 16)
            sp.wait_ge(stored, 48)

        @block.gpsimd
        def _(pool):
            pool.wait_ge(cast_done, 4)
            pool.memset(idx[0][OLAST:P, (OT - 1) * HID:nd], 0).then_inc(pad_done, 1)

        @block.scalar
        def _(act):
            for n, (m, src, dst) in enumerate(pieces):
                act.wait_ge(idx_in[m], 32 if m == 2 else 16)
                if m == 2:
                    act.wait_ge(pad_done, 1)
                if n >= 2:
                    act.wait_ge(hot_done, LUT * (n - 1))
                w = src.shape[1]
                act.activation(idxb[n % 2][:, 0:w], src, ACT.Copy).then_inc(cast_done, 1)

        @block.vector
        def _(dve):
            dve.wait_ge(lut_in, 16)
            for n, (m, src, dst) in enumerate(pieces):
                w = src.shape[1]
                dve.wait_ge(cast_done, n + 1)
                for k in range(LUT):
                    dve.tensor_scalar(hot[k % 2][:, 0:w], idxb[n % 2][:, 0:w], float(k), None,
                                      ALU.is_equal).then_inc(hot_done, 1)
                    dve.wait_ge(hot_done, LUT * n + k + 1)
                    if k == 0:
                        dve.tensor_scalar(dst, hot[0][:, 0:w], lut_sb[:, 0:1], None, ALU.mult).then_inc(acc_done, 1)
                    else:
                        dve.wait_ge(acc_done, LUT * n + k)
                        dve.scalar_tensor_tensor(dst, hot[k % 2][:, 0:w], lut_sb[:, k:k + 1], dst,
                                                 ALU.mult, ALU.add).then_inc(acc_done, 1)


def ffn(nc, tag, wg, wu, wd, src, dst, load=None):
    with ExitStack() as ctx:
        s_ = Space(nc, ctx, tag)
        x = [s_.sb(f"x{j}", [P, TT, HID]) for j in range(2)]
        y = [s_.sb(f"y{j}", [P, TT, HID]) for j in range(2)]
        xn = s_.sb("xn", [P, TT, HID])
        xnT = s_.sb("xnT", [P, KH, BLK])
        hT = s_.sb("hT", [P, OT, BLK])
        sil = [s_.sb(f"sil{j}", [P, BLK]) for j in range(2)]
        st = s_.sb("st", [P, TT, 6])
        mv = s_.sb("mv", [P, TT, 2])
        ve = s_.sb("ve", [P, TT])
        half = s_.sb("half", [P, TT])
        rstd = s_.sb("rstd", [P, TT])
        hold = s_.sb("hold", [P, 1])
        ident = s_.sb("ident", [P, P])
        tp = s_.ps("tp", 2)
        pg = s_.ps("pg", 2)
        pu = s_.ps("pu", 2)
        po = s_.ps("po", 2)
        w_in = s_.sem("w_in")
        ident_done = s_.sem("ident_done")
        half_done = s_.sem("half_done")
        x_in = s_.sems("x_in", 2)
        y_out = s_.sems("y_out", 2)
        stats = s_.sem("stats")
        rstd_done = s_.sem("rstd_done")
        xn_done = s_.sem("xn_done")
        tp_done = s_.sem("tp_done")
        tp_free = s_.sem("tp_free")
        gate_done = s_.sem("gate_done")
        up_done = s_.sem("up_done")
        sil_done = s_.sem("sil_done")
        h_done = s_.sem("h_done")
        o_done = s_.sem("o_done")
        y_done = s_.sem("y_done")
        xv = src.rearrange("(b t p) h -> b p t h", t=TT, p=P)
        yv = dst.rearrange("(b t p) h -> b p t h", t=TT, p=P)
        BANKS = 2
        block = ctx.enter_context(nc.Block())

        @block.sync
        def _(sp):
            if load:
                for w, d in load:
                    sp.dma_start(w[:, :, :], d).then_inc(w_in, 16)
            with sp.Fori(0, NBLK // 2) as i:
                for u in range(2):
                    sp.wait_ge(y_out[u], i * 16)
                    sp.dma_start(x[u][:, :, :], xv[i * 2 + u]).then_inc(x_in[u], 16)

        @block.gpsimd
        def _(pool):
            identity_step(pool, ident, ident_done)
            pool.memset(half[:, :], -0.5).then_inc(half_done, 1)
            pool.wait_ge(half_done, 1)
            with pool.Fori(0, NBLK // 2) as i:
                for u in range(2):
                    pool.wait_ge(stats, (i * 2 + u + 1) * (2 * TT + 1))
                    pool.tensor_tensor(rstd[:, :], ve[:, :], half[:, :], ALU.pow).then_inc(rstd_done, 1)
                    pool.wait_ge(y_done, (i * 2 + u + 1) * TT)
                    pool.dma_start(yv[i * 2 + u], y[u][:, :, :]).then_inc(y_out[u], 16)
            for u in range(2):
                pool.wait_ge(y_out[u], 16 * NBLK // 2)

        @block.tensor
        def _(pe):
            pe.sem_inc(tp_free, BANKS)
            pe.sem_inc(h_done, BANKS)
            pe.wait_ge(ident_done, 2)
            if load:
                pe.wait_ge(w_in, 16 * len(load))
            with pe.Fori(0, NBLK // 2) as i:
                for u in range(2):
                    blk = i * 2 + u
                    pe.wait_ge(xn_done, (blk + 1) * TT)
                    for k in range(KH):
                        pe.wait_ge(tp_free, blk * KH + k + 1)
                        for t in range(TT):
                            last = pe.transpose(tp[k % 2][:, t * P:(t + 1) * P], xn[:, t, k * P:(k + 1) * P], ident[:, :])
                        last.then_inc(tp_done, 1)
                    pe.wait_ge(tp_free, blk * KH + KH + BANKS)
                    for o in range(OT):
                        m = P if o < OT - 1 else OLAST
                        bank = (u * OT + o) % 2
                        pe.wait_ge(h_done, blk * OT + o + 1)
                        for k in range(KH):
                            last = pe.matmul(pg[bank][0:m, :], wg[:, k, o * P:o * P + m], xnT[:, k, :],
                                             start=(k == 0), stop=(k == KH - 1))
                        last.then_inc(gate_done, 1)
                        for k in range(KH):
                            last = pe.matmul(pu[bank][0:m, :], wu[:, k, o * P:o * P + m], xnT[:, k, :],
                                             start=(k == 0), stop=(k == KH - 1))
                        last.then_inc(up_done, 1)
                    pe.wait_ge(h_done, blk * OT + OT + BANKS)
                    for t in range(TT):
                        if t >= 2:
                            pe.wait_ge(y_done, blk * TT + t - 1)
                        else:
                            pe.wait_ge(y_done, blk * TT)
                        for o in range(OT):
                            m = P if o < OT - 1 else OLAST
                            last = pe.matmul(po[t % 2][:, :], hT[0:m, o, t * P:(t + 1) * P], wd[0:m, o, :],
                                             start=(o == 0), stop=(o == OT - 1))
                        last.then_inc(o_done, 1)

        @block.scalar
        def _(act):
            with act.Fori(0, NBLK // 2) as i:
                for u in range(2):
                    blk = i * 2 + u
                    for k in range(KH):
                        act.wait_ge(tp_done, blk * KH + k + 1)
                        act.activation(xnT[:, k, :], tp[k % 2][:, :], ACT.Copy).then_inc(tp_free, 1)
                    for o in range(OT):
                        m = P if o < OT - 1 else OLAST
                        bank = (u * OT + o) % 2
                        act.wait_ge(gate_done, blk * OT + o + 1)
                        act.wait_ge(h_done, blk * OT + o + 1)
                        act.activation(sil[bank][0:m, :], pg[bank][0:m, :], ACT.Silu).then_inc(sil_done, 1)

        @block.vector
        def _(dve):
            with dve.Fori(0, NBLK // 2) as i:
                for u in range(2):
                    blk = i * 2 + u
                    steps = Steps(stats, 2 * TT + 1, blk)
                    dve.wait_ge(x_in[u], (i + 1) * 16)
                    for t in range(TT):
                        n = steps.mark(dve.bn_stats(st[:, t, :], x[u][:, t, :]))
                    steps.wait(dve, n)
                    dve.memset(hold[:, :], 0.0)
                    for t in range(TT):
                        m = steps.mark(dve.bn_aggr(mv[:, t, :], st[:, t, :]))
                    steps.wait(dve, m)
                    steps.mark(dve.tensor_scalar(ve[:, :], mv[:, :, 1], EPS, None, ALU.add))
                    steps.end()
                    dve.wait_ge(rstd_done, blk + 1)
                    dve.wait_ge(tp_done, blk * KH)
                    for t in range(TT):
                        dve.tensor_scalar(xn[:, t, :], x[u][:, t, :], mv[:, t, 0:1], rstd[:, t:t + 1],
                                          ALU.subtract, ALU.mult).then_inc(xn_done, 1)
                    for o in range(OT):
                        m = P if o < OT - 1 else OLAST
                        bank = (u * OT + o) % 2
                        dve.wait_ge(sil_done, blk * OT + o + 1)
                        dve.wait_ge(up_done, blk * OT + o + 1)
                        dve.wait_ge(o_done, blk * TT)
                        dve.tensor_tensor(hT[0:m, o, :], sil[bank][0:m, :], pu[bank][0:m, :], ALU.mult).then_inc(h_done, 1)
                    for t in range(TT):
                        dve.wait_ge(o_done, blk * TT + t + 1)
                        dve.wait_ge(y_out[u], i * 16)
                        dve.scalar_tensor_tensor(y[u][:, t, :], po[t % 2][:, :], 0.5, x[u][:, t, :],
                                                 ALU.mult, ALU.add).then_inc(y_done, 1)


def decays(nc, x1, xnT_d, a_d, beta_d, Wa, ba, Wb, bb):
    with ExitStack() as ctx:
        s_ = Space(nc, ctx, "dc")
        x = [s_.sb(f"x{j}", [P, TT, HID]) for j in range(2)]
        xn = s_.sb("xn", [P, TT, HID])
        xnT = s_.sb("xnT", [P, KH, TOK])
        st = s_.sb("st", [P, TT, 6])
        mv = s_.sb("mv", [P, TT, 2])
        ve = s_.sb("ve", [P, TT])
        half = s_.sb("half", [P, TT])
        rstd = s_.sb("rstd", [P, TT])
        ident = s_.sb("ident", [P, P])
        wa = [s_.sb(f"wa{j}", [P, KH, BLK]) for j in range(2)]
        wb = s_.sb("wb", [P, KH, 2 * H])
        bab = s_.sb("bab", [P, C])
        bbc = s_.sb("bbc", [2 * H, 1])
        RA = 4
        sa = [s_.sb(f"sa{j}", [P, BLK]) for j in range(RA)]
        be = s_.sb("be", [2 * H, B, 2, T])
        tp = s_.ps("tp", 2)
        pa = s_.ps("pa", 4)
        ident_done = s_.sem("ident_done")
        half_done = s_.sem("half_done")
        x_in = s_.sems("x_in", 2)
        w_in = s_.sem("w_in")
        wa_in = s_.sems("wa_in", 2)
        stats = s_.sem("stats")
        rstd_done = s_.sem("rstd_done")
        xn_done = s_.sem("xn_done")
        tp_done = s_.sem("tp_done")
        tp_free = s_.sem("tp_free")
        xnT_out = s_.sem("xnT_out")
        b_done = s_.sem("b_done")
        beta_done = s_.sem("beta_done")
        nbeta_done = s_.sem("nbeta_done")
        beta_out = s_.sem("beta_out")
        pa_done = s_.sem("pa_done")
        sum_done = s_.sem("sum_done")
        sig_done = s_.sem("sig_done")
        a_out = s_.sems("a_out", RA)
        xv = x1.rearrange("(b t p) h -> b p t h", t=TT, p=P)
        wav = Wa.rearrange("(k p) c -> p k c", p=P)
        NT = TOK // P
        CB = C // BLK
        block = ctx.enter_context(nc.Block())

        @block.sync
        def _(sp):
            sp.dma_start(x[0][:, :, :], xv[0]).then_inc(x_in[0], 16)
            sp.dma_start(x[1][:, :, :], xv[1]).then_inc(x_in[1], 16)
            sp.dma_start(wb[:, :, :], Wb.rearrange("(k p) c -> p k c", p=P)).then_inc(w_in, 16)
            sp.dma_start(bab[:, :], ba.rearrange("(o c) -> o c", o=1).broadcast_to([P, C])).then_inc(w_in, 16)
            sp.dma_start(bbc[:, :], bb.rearrange("(c o) -> c o", o=1)).then_inc(w_in, 16)
            for u in range(2):
                sp.dma_start(wa[u][:, :, :], wav[:, :, u * BLK:(u + 1) * BLK]).then_inc(wa_in[u], 16)
            for blk in range(2, NBLK):
                sp.wait_ge(xn_done, (blk - 1) * TT)
                sp.dma_start(x[blk % 2][:, :, :], xv[blk]).then_inc(x_in[blk % 2], 16)
            sp.wait_ge(tp_free, NBLK * KH + 2)
            sp.dma_start(xnT_d, xnT[:, :, :]).then_inc(xnT_out, 16)
            sp.wait_ge(nbeta_done, B)
            bv = beta_d.rearrange("(b q) c t -> q b c t", b=B)
            for b in range(B):
                sp.dma_start(bv[:, b, :, 0:T], be[:, b]).then_inc(beta_out, 16)
            for cb in range(CB):
                if 1 <= cb < CB - 1:
                    sp.wait_ge(pa_done, cb * NT)
                    sp.dma_start(wa[(cb + 1) % 2][:, :, :], wav[:, :, (cb + 1) * BLK:(cb + 2) * BLK])\
                      .then_inc(wa_in[(cb + 1) % 2], 16)
                with sp.Fori(0, NT // RA) as j:
                    for r in range(RA):
                        sp.wait_ge(sig_done, j * RA + (cb * NT + r + 1))
                        sp.dma_start(a_d[r * P:(r + 1) * P, j, cb * BLK:(cb + 1) * BLK], sa[r][:, :])\
                          .then_inc(a_out[r], 16)
            sp.wait_ge(xnT_out, 16)
            sp.wait_ge(beta_out, 16 * B)
            for r in range(RA):
                sp.wait_ge(a_out[r], 16 * CB * NT // RA)

        @block.gpsimd
        def _(pool):
            identity_step(pool, ident, ident_done)
            pool.memset(half[:, :], -0.5).then_inc(half_done, 1)
            pool.wait_ge(half_done, 1)
            for blk in range(NBLK):
                pool.wait_ge(stats, (blk + 1) * (2 * TT + 1))
                pool.tensor_tensor(rstd[:, :], ve[:, :], half[:, :], ALU.pow).then_inc(rstd_done, 1)

        @block.tensor
        def _(pe):
            pe.sem_inc(tp_free, 2)
            pe.sem_inc(sum_done, 4)
            pe.wait_ge(ident_done, 2)
            for blk in range(NBLK):
                pe.wait_ge(xn_done, (blk + 1) * TT)
                for k in range(KH):
                    pe.wait_ge(tp_free, blk * KH + k + 1)
                    for t in range(TT):
                        last = pe.transpose(tp[k % 2][:, t * P:(t + 1) * P], xn[:, t, k * P:(k + 1) * P], ident[:, :])
                    last.then_inc(tp_done, 1)
            pe.wait_ge(tp_free, NBLK * KH + 2)
            pe.wait_ge(w_in, 48)
            for b in range(B):
                if b >= 2:
                    pe.wait_ge(beta_done, b - 1)
                for k in range(KH):
                    last = pe.matmul(tp[b % 2][0:2 * H, :], wb[:, k, :], xnT[:, k, b * T:(b + 1) * T],
                                     start=(k == 0), stop=(k == KH - 1))
                last.then_inc(b_done, 1)
            with pe.Fori(0, CB // 2) as i:
                for u in range(2):
                    pe.wait_ge(wa_in[u], (i + 1) * 16)
                    for t in range(NT):
                        n = (i * 2 + u) * NT + t
                        pe.wait_ge(sum_done, n + 1)
                        for k in range(KH):
                            last = pe.matmul(pa[t % 4][:, :], xnT[:, k, t * P:(t + 1) * P], wa[u][:, k, :],
                                             start=(k == 0), stop=(k == KH - 1))
                        last.then_inc(pa_done, 1)

        @block.scalar
        def _(act):
            for blk in range(NBLK):
                for k in range(KH):
                    act.wait_ge(tp_done, blk * KH + k + 1)
                    act.activation(xnT[:, k, blk * BLK:(blk + 1) * BLK], tp[k % 2][:, :], ACT.Copy).then_inc(tp_free, 1)
            act.wait_ge(w_in, 48)
            for b in range(B):
                act.wait_ge(b_done, b + 1)
                act.activation(be[:, b, 0, :], tp[b % 2][0:2 * H, :], ACT.Sigmoid, bias=bbc[:, 0:1]).then_inc(beta_done, 1)
            for b in range(B):
                act.wait_ge(beta_done, b + 1)
                act.activation(be[:, b, 1, :], be[:, b, 0, :], ACT.Copy, scale=-S2).then_inc(nbeta_done, 1)
            with act.Fori(0, CB * NT // RA) as i:
                for r in range(RA):
                    act.wait_ge(sum_done, i * RA + r + 1 + 4)
                    act.activation(sa[r][:, :], sa[r][:, :], ACT.Sigmoid).then_inc(sig_done, 1)

        @block.vector
        def _(dve):
            for blk in range(NBLK):
                steps = Steps(stats, 2 * TT + 1, blk)
                dve.wait_ge(x_in[blk % 2], (blk // 2 + 1) * 16)
                for t in range(TT):
                    n = steps.mark(dve.bn_stats(st[:, t, :], x[blk % 2][:, t, :]))
                steps.wait(dve, n)
                for t in range(TT):
                    m = steps.mark(dve.bn_aggr(mv[:, t, :], st[:, t, :]))
                steps.wait(dve, m)
                steps.mark(dve.tensor_scalar(ve[:, :], mv[:, :, 1], EPS, None, ALU.add))
                steps.end()
                dve.wait_ge(rstd_done, blk + 1)
                if blk:
                    dve.wait_ge(tp_done, blk * KH)
                for t in range(TT):
                    dve.tensor_scalar(xn[:, t, :], x[blk % 2][:, t, :], mv[:, t, 0:1], rstd[:, t:t + 1],
                                      ALU.subtract, ALU.mult).then_inc(xn_done, 1)
            dve.wait_ge(w_in, 48)
            for cb in range(CB):
                with dve.Fori(0, NT // RA) as j:
                    for r in range(RA):
                        dve.wait_ge(pa_done, j * RA + (cb * NT + r + 1))
                        dve.wait_ge(a_out[r], (j + cb * (NT // RA)) * 16)
                        dve.tensor_tensor(sa[r][:, :], pa[r][:, :], bab[:, cb * BLK:(cb + 1) * BLK], ALU.add)\
                           .then_inc(sum_done, 1)


def heads(nc, xnT_d, kq_d, kt_d, v_d, Wqkv, conv):
    with ExitStack() as ctx:
        s_ = Space(nc, ctx, "hd")
        xnT = s_.sb("xnT", [P, KH, TOK])
        w = [s_.sb(f"w{j}", [P, 3, KH, P]) for j in range(2)]
        cw = s_.sb("cw", [P, H, 3, K + 1])
        cwh = [s_.sb(f"cwh{j}", [P, 3, K + 1]) for j in range(2)]
        ident = s_.sb("ident", [P, P])
        R = 4
        yr = [s_.sb(f"y{j}", [P, T]) for j in range(R)]
        kq = [[s_.sb(f"kq{u}{b}", [P, T, 2]) for b in range(B)] for u in range(2)]
        vr = [s_.sb(f"v{b}", [P, T]) for b in range(B)]
        tr = [s_.sb(f"t{j}", [P, TT, P]) for j in range(R)]
        pp = s_.ps("pp", R)
        pt = s_.ps("pt", 2)
        ident_done = s_.sem("ident_done")
        x_in = s_.sem("x_in")
        w_in = s_.sems("w_in", 2)
        cw_in = s_.sem("cw_in")
        cwh_done = s_.sem("cwh_done")
        proj_done = s_.sem("proj_done")
        conv_open = s_.sem("conv_open")
        taps = s_.sem("taps")
        conv_done = s_.sem("conv_done")
        silu_done = s_.sem("silu_done")
        tr_done = s_.sem("tr_done")
        tr_free = s_.sem("tr_free")
        kq_out = [s_.sems(f"kq_out{u}", B) for u in range(2)]
        t_out = s_.sems("t_out", R)
        UNITS = [(u, m, b) for u in range(2) for m in range(3) for b in range(B)]
        NU = len(UNITS)
        TRS = [n for n, (u, m, b) in enumerate(UNITS) if m < 2]

        def result(n):
            u, m, b = UNITS[n]
            return vr[b][:, :] if m == 1 else kq[u][b][:, :, m // 2]

        nth = {n: j for j, n in enumerate(TRS)}
        NTR = len(TRS)
        LAG_TR, LAG_EV = 2, 3
        block = ctx.enter_context(nc.Block())

        @block.sync
        def _(sp):
            for b in range(B):
                sp.dma_start(xnT[:, :, b * T:(b + 1) * T], xnT_d[:, :, b * T:(b + 1) * T]).then_inc(x_in, 16)
            with sp.Fori(0, H // 2) as i:
                for n in range(NU + LAG_EV):
                    if n < NU and UNITS[n][1] == 2:
                        u, m, b = UNITS[n]
                        sp.wait_ge(silu_done, i * NU + n + 1)
                        sp.dma_start(kq_d[:, b * H + i * 2 + u, 0:T, :], kq[u][b][:, :, :]).then_inc(kq_out[u][b], 16)
                    if n - LAG_EV in nth:
                        u, m, b = UNITS[n - LAG_EV]
                        j = nth[n - LAG_EV]
                        sp.wait_ge(tr_free, i * NTR + j + 1 + 2)
                        dst = (kt_d, v_d)[m][0:T, b, :].rearrange("(t p) c -> p t c", p=P)
                        sp.dma_start(dst[:, :, bass.ds((i * 2 + u) * D, D)], tr[j % R][:, :, :]).then_inc(t_out[j % R], 16)
            for b in range(B):
                for u in range(2):
                    sp.wait_ge(kq_out[u][b], 16 * (H // 2))
            for r in range(R):
                sp.wait_ge(t_out[r], 16 * (H // 2) * NTR // R)

        @block.gpsimd
        def _(pool):
            identity_step(pool, ident, ident_done)
            pool.dma_start(cw[:, :, :, :], conv.rearrange("h p m k -> p h m k")).then_inc(cw_in, 16)
            with pool.Fori(0, H // 2) as i:
                for u in range(2):
                    pool.wait_ge(proj_done, i * NU)
                    pool.dma_start(w[u][:, :, :, :], Wqkv[i * 2 + u]).then_inc(w_in[u], 16)

        @block.tensor
        def _(pe):
            pe.sem_inc(conv_done, R)
            pe.sem_inc(tr_free, 2)
            pe.wait_ge(ident_done, 2)
            pe.wait_ge(x_in, 16 * B)
            with pe.Fori(0, H // 2) as i:
                for n in range(NU):
                    u, m, b = UNITS[n]
                    if m == 0 and b == 0:
                        pe.wait_ge(w_in[u], (i + 1) * 16)
                    pe.wait_ge(conv_done, i * NU + n + 1)
                    for k in range(KH):
                        last = pe.matmul(pp[n % R][:, :], w[u][:, m, k, :], xnT[:, k, b * T:(b + 1) * T],
                                         start=(k == 0), stop=(k == KH - 1))
                    last.then_inc(proj_done, 1)
                    if n - LAG_TR in nth:
                        j = nth[n - LAG_TR]
                        pe.wait_ge(silu_done, i * NU + n - LAG_TR + 1)
                        pe.wait_ge(tr_free, i * NTR + j + 1)
                        for t in range(TT):
                            last = pe.transpose(pt[j % 2][:, t * P:(t + 1) * P],
                                                result(n - LAG_TR)[:, t * P:(t + 1) * P], ident[:, :])
                        last.then_inc(tr_done, 1)

        @block.scalar
        def _(act):
            act.wait_ge(cw_in, 16)

            def silu(i, n):
                u, m, b = UNITS[n]
                act.wait_ge(conv_done, i * NU + n + 1 + R)
                if m != 1:
                    act.wait_ge(kq_out[u][b], i * 16)
                else:
                    act.wait_ge(tr_done, i * NTR + (nth[n - 3 * B] + 1 if u else 0))
                act.activation(result(n), yr[n % R][:, :], ACT.Silu).then_inc(silu_done, 1)

            with act.Fori(0, H // 2) as i:
                for n in range(NU):
                    u, m, b = UNITS[n]
                    if m == 0 and b == 0:
                        act.wait_ge(conv_done, i * NU + R)
                        act.activation(cwh[u][:, :, :], cw[:, bass.ds(i * 2 + u, 1), :, :].rearrange("p o m k -> p (o m) k"),
                                       ACT.Copy).then_inc(cwh_done, 1)
                        act.wait_ge(cwh_done, i * 2 + u + 1)
                    act.wait_ge(proj_done, i * NU + n + 1)
                    act.activation(yr[n % R][:, :], pp[n % R][:, :], ACT.Identity,
                                   bias=cwh[u][:, m, K:K + 1], scale=cwh[u][:, m, K - 1:K]).then_inc(conv_open, 1)
                    if n >= 1:
                        silu(i, n - 1)
                    if n - LAG_EV in nth:
                        j = nth[n - LAG_EV]
                        act.wait_ge(tr_done, i * NTR + j + 1)
                        act.wait_ge(t_out[j % R], 16 * (i * (NTR // R) + j // R))
                        act.activation(tr[j % R][:, :, :].rearrange("p t c -> p (t c)"), pt[j % 2][:, :], ACT.Copy)\
                           .then_inc(tr_free, 1)
                silu(i, NU - 1)

        @block.vector
        def _(dve):
            with dve.Fori(0, H // 2) as i:
                for n in range(NU):
                    u, m, b = UNITS[n]
                    dve.wait_ge(conv_open, i * NU + n + 1)
                    y, p = yr[n % R], pp[n % R]
                    for j in range(1, K):
                        ins = dve.scalar_tensor_tensor(y[:, j:T], p[:, 0:T - j], cwh[u][:, m, K - 1 - j:K - j],
                                                       y[:, j:T], ALU.mult, ALU.add)
                        if j < K - 1:
                            ins.then_inc(taps, 1)
                            dve.wait_ge(taps, i * (2 * NU) + 2 * n + j)
                        else:
                            ins.then_inc(conv_done, 1)


def scan(nc, kq_d, kt_d, v_d, a_d, beta_d, g_d, z_d, w_d, o_d):
    with ExitStack() as ctx:
        s_ = Space(nc, ctx, "sc")
        S = s_.sb("S", [P, N, D])
        kq = [s_.sb(f"kq{j}", [P, N, SUP, 2]) for j in range(2)]
        HALF = N // 2
        kt = s_.sb("kt", [P, HALF, D])
        wt = s_.sb("wt", [P, HALF, D])
        za = s_.sb("za", [P, HALF, D])
        A3 = za[96:99, :, :].rearrange("p n d -> p (n d)").bitcast(BF16)
        gs = [s_.sb(f"gs{j}", [P, SBLK]) for j in range(2)]
        av = [s_.sb(f"a{j}", [P, CH, DH]) for j in range(2)]
        vv = [s_.sb(f"v{j}", [P, CH, DH]) for j in range(2)]
        bt = [s_.sb(f"bt{j}", [P, 2, CH]) for j in range(2)]
        g2 = [s_.sb(f"g2{j}", [P, CH + 1, 2, CH]) for j in range(2)]
        z = s_.sb("z", [P, CH, 2, DH])
        w = s_.sb("w", [P, CH, DH])
        prod = s_.sb("prod", [P, 2, CH, DH])
        o = s_.sb("o", [P, CH + 1, DH])
        Ac = s_.sb("Ac", [P, CH + 1, DH])
        nbA = s_.sb("nbA", [P, CH, DH])
        r1 = s_.sb("r1", [P, DH])
        a3p = s_.sb("a3p", [P, 3, DH], BF16)
        ones3 = s_.sb("ones3", [3 + 96, P], BF16)
        pA = s_.ps("pA", 2)
        pU = s_.ps("pU", 2)
        pz = s_.ps("pz", 2)
        pG = s_.ps("pG", 2)

        start = s_.sem("start")
        pad_done = s_.sem("pad_done")
        kq_in = s_.sems("kq_in", 2)
        kt_in = s_.sems("kt_in", 2)
        a_in = s_.sems("a_in", 2)
        g2_in = s_.sems("g2_in", 2)
        g_done = s_.sem("g_done")
        gs_done = s_.sem("gs_done")
        gs_out = s_.sems("gs_out", 2)
        z_done = s_.sem("z_done")
        zs_done = s_.sem("zs_done")
        z_out = s_.sems("z_out", 2)
        z_in = s_.sem("z_in")
        w_out = s_.sem("w_out")
        prep = s_.sem("prep")
        zq_done = s_.sem("zq_done")
        o_sum = s_.sem("o_sum")
        o_out = s_.sem("o_out")
        step = s_.sem("step")
        w_in = s_.sems("w_in", 2)
        A_in = s_.sem("A_in")
        A_done = s_.sem("A_done")
        U_done = s_.sem("U_done")
        S_dec = s_.sem("S_dec")
        S_done = s_.sem("S_done")

        LOOP = 8
        TURNS = NCH // LOOP
        GB = N * SUP // SBLK
        GN = SBLK // SUP
        PREP = CH + 7
        STEP = 2 + 2 * (CH - 1) + 2 * CH
        gdv = g_d
        av_d = a_d.rearrange("t b (q d) -> (b q) t d", d=DH)
        vv_d = v_d.rearrange("t b (q d) -> (b q) t d", d=DH)
        ov_d = o_d.rearrange("t b (q d) -> (b q) t d", d=DH)
        ktv = kt_d.rearrange("t b (h d) -> t (b h) d", d=D)
        block = ctx.enter_context(nc.Block())

        def load_chunk(sp, u, t0):
            sp.dma_start(av[u][:, :, :], av_d[:, bass.ds(t0, CH), :]).then_inc(a_in[u], 16)
            sp.dma_start(vv[u][:, :, :], vv_d[:, bass.ds(t0, CH), :]).then_inc(a_in[u], 16)
            sp.dma_start(bt[u][:, :, :], beta_d[:, :, bass.ds(t0, CH)]).then_inc(a_in[u], 16)

        def load_kt(sp, u, t0):
            for hf in range(2):
                r = 32 * (2 * u + hf)
                sp.dma_start(kt[r:r + CH, :, :], ktv[bass.ds(t0, CH), hf * HALF:(hf + 1) * HALF, :]).then_inc(kt_in[u], 16)

        def load_g(sp, u, par, j):
            for half in range(2):
                for q in range(2):
                    src = gdv[par, j * CH:(j + 1) * CH, q, :, j * CH:(j + 1) * CH].rearrange("t n s -> n t s")
                    dst = g2[u][half:P:2, q:q + CH, 1 - q, :]
                    sp.dma_start(dst, src).then_inc(g2_in[u], 16)

        @block.sync
        def _(sp):
            sp.dma_start(kq[0][:, :, :, :], kq_d[:, :, 0:SUP, :]).then_inc(kq_in[0], 16)
            load_chunk(sp, 0, 0)
            load_kt(sp, 0, 0)
            sp.dma_start(kq_d[:, :, T:T + SUP, :], kq_d[:, :, 0:SUP, :]).then_inc(pad_done, 16)
            for d in (a_d, v_d, kt_d):
                sp.dma_start(d[T:T + CH], d[0:CH]).then_inc(pad_done, 16)
            sp.dma_start(beta_d[:, :, T:T + CH], beta_d[:, :, 0:CH]).then_inc(pad_done, 16)
            sp.wait_ge(pad_done, 80)
            for m in range(GB):
                sp.wait_ge(gs_done, m + 1)
                sp.dma_start(gdv[0, :, :, m * GN:(m + 1) * GN, :].rearrange("t q n s -> (t q) n s"),
                             gs[m % 2][:, :].rearrange("p (n s) -> p n s", s=SUP)).then_inc(gs_out[m % 2], 16)
            for m in range(2):
                sp.wait_ge(gs_out[m], 16 * GB // 2)
            load_g(sp, 0, 0, 0)
            with sp.Fori(0, TURNS) as i:
                for cc in range(LOOP):
                    c = i * LOOP + cc
                    u, nu, j = cc % 2, (cc + 1) % 2, cc % CPS
                    banks_before = i * (LOOP * NSB) + cc * NSB
                    t_next = i * (LOOP * CH) + (cc + 1) * CH
                    if j == 0:
                        par = (cc // CPS + 1) % 2
                        nxt = (i * 2 + cc // CPS + 1) * SUP
                        sp.wait_ge(z_done, banks_before)
                        sp.dma_start(kq[par][:, :, :, :], kq_d[:, :, bass.ds(nxt, SUP), :]).then_inc(kq_in[par], 16)
                    sp.wait_ge(step, c * STEP)
                    sp.wait_ge(S_done, banks_before)
                    load_chunk(sp, nu, t_next)
                    load_kt(sp, nu, t_next)
                    if j < CPS - 1:
                        load_g(sp, nu, cc // CPS, j + 1)
                    sp.wait_ge(prep, c * PREP + PREP)
                    for r in range(3):
                        sp.dma_start(A3[r:r + 1, :].rearrange("o (p d) -> o p d", d=DH), a3p[:, r, :]).then_inc(A_in, 16)
                    if j == 2:
                        par = (cc // CPS + 1) % 2
                        sup = i * 2 + cc // CPS + 1
                        for m in range(GB):
                            sp.wait_ge(gs_done, sup * GB + m + 1)
                            sp.dma_start(gdv[par, :, :, m * GN:(m + 1) * GN, :].rearrange("t q n s -> (t q) n s"),
                                         gs[m % 2][:, :].rearrange("p (n s) -> p n s", s=SUP)).then_inc(gs_out[m % 2], 16)
                    if j == 3:
                        for m in range(2):
                            sp.wait_ge(gs_out[m], (i * 2 + cc // CPS + 2) * (16 * GB // 2))
                        load_g(sp, nu, (cc // CPS + 1) % 2, 0)
                    sp.wait_ge(step, c * STEP + STEP)
                    sp.dma_start(w_d[u].rearrange("s (p d) -> p s d", d=DH), w[:, :, :]).then_inc(w_out, 16)
                    sp.wait_ge(w_out, c * 16 + 16)
                    for hf in range(2):
                        r = 32 * (2 * u + hf)
                        sp.dma_start(wt[r:r + CH, :, :].rearrange("s n d -> s (n d)"),
                                     w_d[u, :, hf * (HALF * D):(hf + 1) * (HALF * D)]).then_inc(w_in[u], 16)
                    sp.wait_ge(o_sum, c + 1)
                    for hf in range(2):
                        sp.wait_ge(z_out[hf], c * 16 + 16)
                        sp.dma_start(z[hf * 64:(hf + 1) * 64, :, :, :].rearrange("p t q d -> p (t q) d"),
                                     z_d[hf].rearrange("r (p d) -> p r d", d=DH)).then_inc(z_in, 16)

        @block.scalar
        def _(act):
            def g_banks(sup):
                for m in range(GB):
                    act.wait_ge(g_done, sup * GB + m + 1)
                    act.wait_ge(gs_out[m % 2], sup * (16 * GB // 2) + 16 * (m // 2))
                    act.activation(gs[m % 2][:, :], pG[m % 2][:, :], ACT.Copy).then_inc(gs_done, 1)

            g_banks(0)
            with act.Fori(0, TURNS) as i:
                for cc in range(LOOP):
                    c = i * LOOP + cc
                    if cc % CPS == 2:
                        g_banks(i * 2 + cc // CPS + 1)
                    for m in range(NSB):
                        hf = m // (NSB // 2)
                        act.wait_ge(z_done, (c + 1) * NSB + m + 1)
                        if m % (NSB // 2) == 0:
                            act.wait_ge(z_in, c * 32 + 32)
                        mm = m % (NSB // 2)
                        act.activation(za[32 * hf:32 * hf + 32, mm * NPB:(mm + 1) * NPB, :].rearrange("p n d -> p (n d)"),
                                       pz[m % 2][0:32, :], ACT.Copy).then_inc(zs_done, 1)
                        if m % (NSB // 2) == NSB // 2 - 1:
                            act.wait_ge(zs_done, (c + 1) * NSB + m + 1)
                            act.dma_start(z_d[hf], za[32 * hf:32 * hf + 32, :, :].rearrange("r n d -> r (n d)"))\
                               .then_inc(z_out[hf], 16)

        @block.tensor
        def _(pe):
            def g_banks(sup, par):
                for m in range(GB):
                    if m >= 2:
                        pe.wait_ge(gs_done, sup * GB + m - 1)
                    else:
                        pe.wait_ge(gs_done, sup * GB)
                    for n in range(GN):
                        x = kq[par][:, m * GN + n, :, :]
                        last = pe.matmul(pG[m % 2][:, n * SUP:(n + 1) * SUP], x.rearrange("p t a -> p (t a)"), x[:, :, 0],
                                         start=True, stop=True)
                    last.then_inc(g_done, 1)

            pe.wait_ge(kq_in[0], 16)
            g_banks(0, 0)
            pe.sem_inc(z_done, NSB)
            pe.wait_ge(start, 5)
            with pe.Fori(0, TURNS) as i:
                for cc in range(LOOP):
                    c = i * LOOP + cc
                    u = cc % 2
                    if cc % CPS == 2:
                        par = (cc // CPS + 1) % 2
                        pe.wait_ge(kq_in[par], (i + 1) * 16 + (16 if par == 0 else 0))
                        g_banks(i * 2 + cc // CPS + 1, par)
                    j1 = (cc + 1) % CPS
                    par1 = ((cc + 1) // CPS) % 2
                    pe.wait_ge(A_in, (c + 1) * 48)
                    pe.wait_ge(kt_in[u], (i * 4 + cc // 2 + 1) * 32)
                    pe.wait_ge(w_in[u], (i * 4 + cc // 2 + 1) * 32)

                    def decay_update(m):
                        hf = m // (NSB // 2)
                        if m >= 2:
                            pe.wait_ge(S_done, c * NSB + m - 1)
                        pe.matmul(pA[m % 2][:, :], ones3[96:99, :], A3[:, m * SBLK:(m + 1) * SBLK],
                                  start=True, stop=True).then_inc(A_done, 1)
                        for n in range(NPB):
                            nn = (m % (NSB // 2)) * NPB + n
                            r = 32 * (2 * u + hf)
                            last = pe.matmul(pU[m % 2][:, n * D:(n + 1) * D], kt[r:r + CH, nn, :], wt[r:r + CH, nn, :],
                                             start=True, stop=True)
                        last.then_inc(U_done, 1)

                    def project(m):
                        pe.wait_ge(S_done, c * NSB + m + 1)
                        if m >= 2:
                            pe.wait_ge(zs_done, (c + 1) * NSB + m - 1)
                        else:
                            pe.wait_ge(zs_done, (c + 1) * NSB)
                        for n in range(NPB):
                            nn = m * NPB + n
                            last = pe.matmul(pz[m % 2][0:32, n * D:(n + 1) * D],
                                             kq[par1][:, nn, j1 * CH:(j1 + 1) * CH, :].rearrange("p t a -> p (t a)"), S[:, nn, :],
                                             start=True, stop=True)
                        last.then_inc(z_done, 1)

                    for m in range(NSB + 2):
                        if m < NSB:
                            decay_update(m)
                        if m >= 2:
                            project(m - 2)

        @block.gpsimd
        def _(pool):
            pool.memset(ones3[96:99, :], 1.0).then_inc(start, 1)
            pool.wait_ge(start, 1)
            pool.memset(S[:, :, :], 0.0).then_inc(start, 1)
            pool.memset(z[:, :, :, :], 0.0).then_inc(start, 1)
            pool.memset(Ac[:, 0, :], 1.0).then_inc(start, 1)
            pool.wait_ge(start, 4)
            pool.sem_inc(zs_done, NSB)
            pool.sem_inc(z_in, 32)
            pool.sem_inc(start, 1)

            def prepare(turn, u, uses):
                st = Steps(prep, PREP, turn)
                one = Ac[:, 0, :]
                pool.wait_ge(a_in[u], uses * 48)
                st.mark(pool.tensor_tensor(vv[u][:, :, :], vv[u][:, :, :], mid(bt[u][:, 0, :], 2, DH), ALU.mult))
                for t in range(CH):
                    if t:
                        st.wait(pool, n)
                    n = st.mark(pool.tensor_tensor(Ac[:, t + 1, :], Ac[:, t, :], av[u][:, t, :], ALU.mult))
                st.wait(pool, n)
                st.mark(pool.tensor_tensor(nbA[:, :, :], Ac[:, 0:CH, :], mid(bt[u][:, 1, :], 2, DH), ALU.mult))
                n = st.mark(pool.tensor_tensor(a3p[:, 0, :], Ac[:, CH, :], one, ALU.mult))
                st.wait(pool, n)
                n = st.mark(pool.tensor_tensor(r1[:, :], Ac[:, CH, :], a3p[:, 0, :], ALU.subtract))
                st.wait(pool, n)
                n = st.mark(pool.tensor_tensor(a3p[:, 1, :], r1[:, :], one, ALU.mult))
                st.wait(pool, n)
                n = st.mark(pool.tensor_tensor(r1[:, :], r1[:, :], a3p[:, 1, :], ALU.subtract))
                st.wait(pool, n)
                st.mark(pool.tensor_tensor(a3p[:, 2, :], r1[:, :], one, ALU.mult))
                st.end()

            prepare(0, 0, 1)
            with pool.Fori(0, TURNS) as i:
                for cc in range(LOOP):
                    c = i * LOOP + cc
                    nu = (cc + 1) % 2
                    pool.wait_ge(z_in, c * 32 + 32)
                    pool.tensor_tensor(z[:, :, 1, :], z[:, :, 1, :], Ac[:, 1:CH + 1, :], ALU.mult).then_inc(zq_done, 1)
                    pool.wait_ge(step, c * STEP + 1)
                    pool.wait_ge(A_in, (c + 1) * 48)
                    pool.wait_ge(zq_done, c + 1)
                    prepare(c + 1, nu, i * 4 + (cc + 1) // 2 + 1)
                    pool.wait_ge(step, c * STEP + STEP)
                    pool.tensor_tensor(o[:, 0:CH, :], o[:, 0:CH, :], z[:, :, 1, :], ALU.add).then_inc(o_sum, 1)
                    pool.wait_ge(o_sum, c + 1)
                    pool.dma_start(ov_d[:, bass.ds(c * CH, CH), :], o[:, 0:CH, :]).then_inc(o_out, 16)
            pool.wait_ge(o_out, 16 * NCH)
            for u in range(2):
                pool.wait_ge(kq_in[u], 16 * (TURNS + (u == 0)))
            pool.wait_ge(z_in, 32 * (NCH + 1))
            pool.wait_ge(g2_in[0], 64 * (NCH // 2 + 1))
            pool.wait_ge(kt_in[0], 32 * (NCH // 2 + 1))
            pool.wait_ge(gs_out[0], 16 * (GB // 2) * (T // SUP + 1))
            pool.wait_ge(gs_out[1], 16 * (GB // 2) * (T // SUP + 1))

        @block.vector
        def _(dve):
            dve.wait_ge(start, 5)
            with dve.Fori(0, TURNS) as i:
                for cc in range(LOOP):
                    c = i * LOOP + cc
                    u = cc % 2
                    st = Steps(step, STEP, c)
                    dve.wait_ge(z_in, c * 32 + 32)
                    dve.wait_ge(prep, c * PREP + PREP)
                    n = st.mark(dve.tensor_tensor(prod[:, 0, :, :], z[:, :, 0, :], nbA[:, :, :], ALU.mult))
                    st.wait(dve, n)
                    pu = (cc + 1) % 2
                    dve.wait_ge(w_in[pu], (i * 4 + (cc + 1) // 2) * 32)
                    n = st.mark(dve.tensor_tensor(w[:, :, :], prod[:, 0, :, :], vv[u][:, :, :], ALU.add))
                    dve.wait_ge(g2_in[u], (i * 4 + cc // 2 + 1) * 64)
                    dve.wait_ge(o_out, c * 16)
                    red = None
                    for t in range(CH):
                        if t:
                            st.mark(dve.tensor_tensor(w[:, 0:t, :], w[:, 0:t, :], mid(av[u][:, t, :], 1, t), ALU.mult))
                            st.wait(dve, red)
                            n = st.mark(dve.scalar_tensor_tensor(w[:, t, :], o[:, CH, :], bt[u][:, 1, t:t + 1], w[:, t, :],
                                                                 ALU.mult, ALU.add))
                        st.wait(dve, n)
                        last = t == CH - 1
                        q = 1 if last else 2
                        n = st.mark(dve.tensor_tensor(
                            prod[:, 0:q, 0:t + 1, :], mid(w[:, 0:t + 1, :], 1, q),
                            mid(g2[u][:, t + 1, 0:q, 0:t + 1], 3, DH), ALU.mult))
                        st.wait(dve, n)
                        dst = o[:, t:t + 1, :] if last else o[:, t:CH + 1:CH - t, :]
                        red = st.mark(dve.tensor_reduce(dst, prod[:, 0:q, 0:t + 1, :].rearrange("p q s d -> p q d s"),
                                                        AX.X, ALU.add))
                    st.end()
                    for m in range(NSB):
                        blk = S[:, m * NPB:(m + 1) * NPB, :].rearrange("p n d -> p (n d)")
                        dve.wait_ge(A_done, c * NSB + m + 1)
                        dve.tensor_tensor(blk, blk, pA[m % 2][:, :], ALU.mult).then_inc(S_dec, 1)
                        dve.wait_ge(S_dec, c * NSB + m + 1)
                        dve.wait_ge(U_done, c * NSB + m + 1)
                        dve.tensor_tensor(blk, blk, pU[m % 2][:, :], ALU.add).then_inc(S_done, 1)


def attn_out(nc, x1, xnT_d, o_d, x2, Wg, Wo, ln_w, ln_b):
    with ExitStack() as ctx:
        s_ = Space(nc, ctx, "ao")
        wg = s_.sb("wg", [P, KH, C])
        wo = s_.sb("wo", [P, H, HID])
        lnw = s_.sb("lnw", [P, 1])
        lnb = s_.sb("lnb", [P, 1])
        o = [s_.sb(f"o{j}", [P, TT, C]) for j in range(2)]
        oT = s_.sb("oT", [P, H, T])
        xnT = s_.sb("xnT", [P, KH, T])
        x = s_.sb("x", [P, TT, HID])
        st = s_.sb("st", [P, H, 6])
        mv = s_.sb("mv", [P, H, 2])
        ve = s_.sb("ve", [P, H])
        half = s_.sb("half", [P, H])
        rstd = s_.sb("rstd", [P, H])
        hold = s_.sb("hold", [P, 1])
        ident = s_.sb("ident", [P, P])
        gg = [s_.sb(f"g{j}", [P, T]) for j in range(2)]
        pg = s_.ps("pg", 2)
        pt = s_.ps("pt", 2)
        po = s_.ps("po", 2)
        ident_done = s_.sem("ident_done")
        half_done = s_.sem("half_done")
        w_in = s_.sem("w_in")
        o_in = s_.sems("o_in", 2)
        xT_in = s_.sem("xT_in")
        x_in = s_.sem("x_in")
        stats = s_.sem("stats")
        rstd_done = s_.sem("rstd_done")
        on_done = s_.sem("on_done")
        g_done = s_.sem("g_done")
        t_done = s_.sem("t_done")
        sig_done = s_.sem("sig_done")
        aff_done = s_.sem("aff_done")
        gated = s_.sem("gated")
        p_done = s_.sem("p_done")
        y_done = s_.sem("y_done")
        y_out = s_.sem("y_out")
        ov = o_d.rearrange("(t p) b c -> b p t c", p=P)
        xv = x1.rearrange("(b t p) h -> b p t h", t=TT, p=P)
        yv = x2.rearrange("(b t p) h -> b p t h", t=TT, p=P)
        STATS = 2 * H + 1
        block = ctx.enter_context(nc.Block())

        @block.sync
        def _(sp):
            sp.dma_start(lnw[:, :], ln_w.rearrange("(c o) -> c o", o=1)).then_inc(w_in, 16)
            sp.dma_start(lnb[:, :], ln_b.rearrange("(c o) -> c o", o=1)).then_inc(w_in, 16)
            sp.dma_start(wg[:, :, :], Wg.rearrange("(k p) c -> p k c", p=P)).then_inc(w_in, 16)
            sp.dma_start(wo[:, :, :], Wo.rearrange("(k p) c -> p k c", p=P)).then_inc(w_in, 16)
            with sp.Fori(0, B // 2) as i:
                for u in range(2):
                    b = i * 2 + u
                    sp.wait_ge(t_done, i * (2 * H))
                    sp.dma_start(o[u][:, :, :], ov[b]).then_inc(o_in[u], 16)
                    sp.wait_ge(g_done, b * H)
                    sp.dma_start(xnT[:, :, :], xnT_d[:, :, bass.ds(b * T, T)]).then_inc(xT_in, 16)
                    sp.wait_ge(y_out, b * 16)
                    sp.dma_start(x[:, :, :], xv[b]).then_inc(x_in, 16)

        @block.gpsimd
        def _(pool):
            identity_step(pool, ident, ident_done)
            pool.memset(half[:, :], -0.5).then_inc(half_done, 1)
            pool.wait_ge(half_done, 1)
            with pool.Fori(0, B) as b:
                for t in range(TT):
                    pool.wait_ge(stats, (b * TT + t + 1) * STATS)
                    pool.tensor_tensor(rstd[:, :], ve[:, :], half[:, :], ALU.pow).then_inc(rstd_done, 1)
                pool.wait_ge(y_done, b * TT + TT)
                pool.dma_start(yv[b], x[:, :, :]).then_inc(y_out, 16)
            pool.wait_ge(y_out, 16 * B)

        @block.tensor
        def _(pe):
            pe.sem_inc(gated, 2)
            pe.wait_ge(ident_done, 2)
            pe.wait_ge(w_in, 64)
            with pe.Fori(0, B // 2) as i:
                for u in range(2):
                    b = i * 2 + u
                    pe.wait_ge(xT_in, b * 16 + 16)
                    pe.wait_ge(on_done, (b * TT + TT) * H)
                    for h in range(H):
                        pe.wait_ge(gated, b * H + h + 1)
                        for k in range(KH):
                            last = pe.matmul(pg[h % 2][:, :], wg[:, k, h * D:(h + 1) * D], xnT[:, k, :],
                                             start=(k == 0), stop=(k == KH - 1))
                        last.then_inc(g_done, 1)
                        for t in range(TT):
                            last = pe.transpose(pt[h % 2][:, t * P:(t + 1) * P], o[u][:, t, h * D:(h + 1) * D], ident[:, :])
                        last.then_inc(t_done, 1)
                    pe.wait_ge(gated, b * H + H + 2)
                    for t in range(TT):
                        if t >= 2:
                            pe.wait_ge(y_done, b * TT + t - 1)
                        else:
                            pe.wait_ge(y_done, b * TT)
                        for h in range(H):
                            last = pe.matmul(po[t % 2][:, :], oT[:, h, t * P:(t + 1) * P], wo[:, h, :],
                                             start=(h == 0), stop=(h == H - 1))
                        last.then_inc(p_done, 1)

        @block.scalar
        def _(act):
            act.wait_ge(w_in, 64)
            with act.Fori(0, B) as b:
                for h in range(H):
                    act.wait_ge(g_done, b * H + h + 1)
                    act.wait_ge(gated, b * H + h + 1)
                    act.activation(gg[h % 2][:, :], pg[h % 2][:, :], ACT.Sigmoid).then_inc(sig_done, 1)
                    act.wait_ge(t_done, b * H + h + 1)
                    act.wait_ge(p_done, b * TT)
                    act.activation(oT[:, h, :], pt[h % 2][:, :], ACT.Identity, bias=lnb[:, 0:1], scale=lnw[:, 0:1])\
                       .then_inc(aff_done, 1)

        @block.vector
        def _(dve):
            with dve.Fori(0, B // 2) as i:
                for u in range(2):
                    b = i * 2 + u
                    dve.wait_ge(o_in[u], i * 16 + 16)
                    for t in range(TT):
                        s = Steps(stats, STATS, b * TT + t)
                        for h in range(H):
                            n = s.mark(dve.bn_stats(st[:, h, :], o[u][:, t, h * D:(h + 1) * D]))
                        s.wait(dve, n)
                        dve.memset(hold[:, :], 0.0)
                        for h in range(H):
                            n = s.mark(dve.bn_aggr(mv[:, h, :], st[:, h, :]))
                        s.wait(dve, n)
                        s.mark(dve.tensor_scalar(ve[:, :], mv[:, :, 1], EPS / S2, None, ALU.add))
                        s.end()
                        dve.wait_ge(rstd_done, b * TT + t + 1)
                        for h in range(H):
                            blk = o[u][:, t, h * D:(h + 1) * D]
                            dve.tensor_scalar(blk, blk, mv[:, h, 0:1], rstd[:, h:h + 1], ALU.subtract, ALU.mult)\
                               .then_inc(on_done, 1)
                    for h in range(H):
                        dve.wait_ge(sig_done, b * H + h + 1)
                        dve.wait_ge(aff_done, b * H + h + 1)
                        dve.tensor_tensor(oT[:, h, :], oT[:, h, :], gg[h % 2][:, :], ALU.mult).then_inc(gated, 1)
                    dve.wait_ge(x_in, b * 16 + 16)
                    for t in range(TT):
                        dve.wait_ge(p_done, b * TT + t + 1)
                        dve.tensor_tensor(x[:, t, :], x[:, t, :], po[t % 2][:, :], ALU.add).then_inc(y_done, 1)


def program(nc, t):
    ffn_w = [("wg", [P, KH, INTER]), ("wu", [P, KH, INTER]), ("wd", [P, OT, HID])]

    def scratch(name, shape, dt=F32):
        return nc.dram_tensor(name, tuple(shape), dt, kind="Internal").ap()

    ffn_d = [scratch(n + "_d", s) for n, s in ffn_w]
    x1, x2 = scratch("x1_d", [TOK, HID]), scratch("x2_d", [TOK, HID])
    xnT_d = scratch("xnT_d", [P, KH, TOK])
    a_d, v_d, kt_d = (scratch(n, [T + CH, B, C]) for n in ("a_d", "v_d", "kt_d"))
    o_d = scratch("o_d", [T, B, C])
    beta_d = scratch("beta_d", [NP, 2, T + CH])
    kq_d = scratch("kq_d", [P, N, T + SUP, 2])
    z_d = scratch("z_d", [2, 2 * CH, N * D // 2])
    w_d = scratch("w_d", [2, CH, N * D])
    g_d = scratch("g_d", [2, SUP, 2, N, SUP])

    def with_weights(tag, body):
        with ExitStack() as ctx:
            body(*[ctx.enter_context(nc.sbuf_tensor(f"{tag}_{n}", s, F32)) for n, s in ffn_w])

    def first(wg, wu, wd):
        dequantise(nc, wg, wu, wd, t["lut"], t["gate_idx"], t["up_idx"], t["down_idx"], *ffn_d)
        ffn(nc, "f1", wg, wu, wd, t["x"], x1)

    def second(wg, wu, wd):
        ffn(nc, "f2", wg, wu, wd, x2, t["out"], load=list(zip((wg, wu, wd), ffn_d)))

    with_weights("m1", first)
    decays(nc, x1, xnT_d, a_d, beta_d, t["Wa"], t["ba"], t["Wb"], t["bb"])
    heads(nc, xnT_d, kq_d, kt_d, v_d, t["Wqkv"], t["conv"])
    scan(nc, kq_d, kt_d, v_d, a_d, beta_d, g_d, z_d, w_d, o_d)
    attn_out(nc, x1, xnT_d, o_d, x2, t["Wg"], t["Wo"], t["ln_w"], t["ln_b"])
    with_weights("m2", second)


def kernel(**inputs):
    import numpy as np
    import concourse.bacc as bacc
    from concourse.bass_utils import run_bass_kernel_spmd

    g = {k.split("_", 2)[2]: np.asarray(v) for k, v in inputs.items()}
    per_head = lambda W: W.reshape(H, D, KH, P).transpose(0, 3, 2, 1)
    arrays = {
        "x": g["x"].reshape(TOK, HID),
        "lut": g["lut"],
        "gate_idx": g["gate_idx"].T, "up_idx": g["up_idx"].T, "down_idx": g["down_idx"].T,
        "Wa": g["Wa"].T, "ba": g["ba"],
        "Wb": np.repeat(g["Wb"], 2, axis=0).T, "bb": np.repeat(g["bb"], 2),
        "Wqkv": np.stack([per_head(g[n]) for n in ("Wk", "Wv", "Wq")], axis=2),
        "conv": np.stack([np.concatenate([g[n + "conv_w"], g[n + "conv_b"][:, None]], axis=1).reshape(H, D, K + 1)
                          for n in "kvq"], axis=2),
        "Wg": g["Wg"].T, "Wo": g["Wo"].T, "ln_w": g["ln_w"], "ln_b": g["ln_b"],
    }
    arrays = {f"in_{k}": np.ascontiguousarray(v) for k, v in arrays.items()}
    nc = bacc.Bacc("TRN2", target_bir_lowering=False, num_devices=1)
    t = {k[3:]: nc.dram_tensor(k, v.shape, mybir.dt.from_np(v.dtype), kind="ExternalInput").ap() for k, v in arrays.items()}
    t["out"] = nc.dram_tensor("out", (TOK, HID), F32, kind="ExternalOutput").ap()
    program(nc, t)
    r = run_bass_kernel_spmd(nc, [arrays], core_ids=[0])
    return r.results[0]["out"].reshape(B, T, HID)
```

```python
from contextlib import ExitStack

import concourse.bass as bass
from concourse import mybir

F32 = mybir.dt.float32
BF16 = mybir.dt.bfloat16
F32R = mybir.dt.float32r
I32 = mybir.dt.int32
ALU = mybir.AluOpType
ACT = mybir.ActivationFunctionType
AX = mybir.AxisListType

P = 128
B, T, HID = 4, 512, 512
TOK = B * T
H, D, K = 16, 128, 4
C = H * D
N = B * H
INTER, LUT = 1376, 16
KH = HID // P
OT = (INTER + P - 1) // P
OLAST = INTER - (OT - 1) * P
BLK = 512
NBLK = TOK // BLK
TT = BLK // P
EPS = 1e-5
S2 = 1.0 / D

CH = 16
SUP = 32
CPS = SUP // CH
NCH = T // CH
DH = 64
NP = N * D // DH
KW = 6 * CH
STACK = ((0, 3), (3 * CH, 2), (5 * CH, 1))
SBLK = 512
NSB = N * D // SBLK
NPB = SBLK // D


def mid(ap, axis, n):
    a = ap.unsqueeze(axis)
    shape = list(a.shape)
    shape[axis] = n
    return a.broadcast_to(shape)


class Steps:

    def __init__(self, sem, per, turn):
        self.sem, self.per, self.turn, self.n = sem, per, turn, 0

    def mark(self, ins):
        ins.then_inc(self.sem, 1)
        self.n += 1
        return self.n

    def wait(self, eng, n):
        eng.wait_ge(self.sem, self.turn * self.per + n)

    def end(self):
        assert self.n == self.per, (self.n, self.per)


class Space:

    def __init__(self, nc, ctx, tag):
        self.nc, self.ctx, self.tag = nc, ctx, tag

    def sb(self, name, shape, dt=F32):
        return self.ctx.enter_context(self.nc.sbuf_tensor(f"{self.tag}_{name}", shape, dt))

    def ps(self, name, n=1, shape=(P, 512), dt=F32):
        t = [self.ctx.enter_context(self.nc.psum_tensor(f"{self.tag}_{name}{j}", list(shape), dt)) for j in range(n)]
        return t if n > 1 else t[0]

    def sem(self, name):
        return self.ctx.enter_context(self.nc.semaphore(f"{self.tag}_{name}"))

    def sems(self, name, n):
        return [self.sem(f"{name}{j}") for j in range(n)]


def identity_step(pool, ident, sem):
    pool.memset(ident[:, :], 0.0).then_inc(sem, 1)
    pool.wait_ge(sem, 1)
    pool.affine_select(out=ident[:, :], in_=ident[:, :], compare_op=ALU.not_equal, fill=1.0, base=0,
                       pattern=[[-1, P]], channel_multiplier=1).then_inc(sem, 1)


def after(eng, sem, n):
    if n > 0:
        eng.wait_ge(sem, n)


def quantised_ffn(nc, x, x1, lut, gate_idx, up_idx, down_idx, wg_d, wu_d, wd_d):
    with ExitStack() as ctx:
        s_ = Space(nc, ctx, "f1")
        RING = 3
        PIECE = 2 * KH * P
        idx = [s_.sb(f"idx{j}", [P, PIECE], I32) for j in range(2)]
        idxb = [s_.sb(f"idxb{j}", [P, PIECE], BF16) for j in range(2)]
        hot = [s_.sb(f"hot{j}", [P, PIECE], BF16) for j in range(3)]
        gu = [s_.sb(f"gu{j}", [P, PIECE]) for j in range(RING)]
        wd = s_.sb("wd", [P, OT, HID])
        lut_sb = s_.sb("lut", [P, LUT])
        xt = [s_.sb(f"x{j}", [P, TT, HID]) for j in range(2)]
        xn = s_.sb("xn", [P, TT, HID])
        xnT = s_.sb("xnT", [P, KH, TOK])
        y = xnT[:, :, :].rearrange("p k t -> p (k t)").rearrange("p (t h) -> p t h", h=HID)
        hT = s_.sb("hT", [P, OT, TOK])
        sil = [s_.sb(f"sil{j}", [P, BLK]) for j in range(2)]
        st = s_.sb("st", [P, TT, 6])
        mv = s_.sb("mv", [P, TT, 2])
        ve = s_.sb("ve", [P, TT])
        half = s_.sb("half", [P, TT])
        rstd = s_.sb("rstd", [P, TT])
        hold = s_.sb("hold", [P, 1])
        ident = s_.sb("ident", [P, P])
        tp = s_.ps("tp", 2)
        pg = s_.ps("pg", 2)
        pu = s_.ps("pu", 2)
        po = s_.ps("po", 2)
        lut_in = s_.sem("lut_in")
        idx_in = s_.sems("idx_in", 2)
        cast_done = s_.sem("cast_done")
        hot_done = s_.sem("hot_done")
        acc_done = s_.sem("acc_done")
        stored = s_.sems("stored", RING)
        consts_done = s_.sem("consts_done")
        x_in = s_.sems("x_in", 2)
        stats = s_.sem("stats")
        rstd_done = s_.sem("rstd_done")
        xn_done = s_.sem("xn_done")
        tp_done = s_.sem("tp_done")
        tp_free = s_.sem("tp_free")
        gate_done = s_.sem("gate_done")
        up_done = s_.sem("up_done")
        sil_done = s_.sem("sil_done")
        h_done = s_.sem("h_done")
        o_done = s_.sem("o_done")
        y_done = s_.sem("y_done")
        y_out = s_.sem("y_out")
        xv = x.rearrange("(b t p) h -> b p t h", t=TT, p=P)
        yv = x1.rearrange("(b t p) h -> b p t h", t=TT, p=P)

        SLOTS = OT * NBLK
        WD = (OT + 1) // 2
        PIECES = OT + WD
        NT = TOK // P
        GROUPS = ((0, 4), (4, 8), (8, OT))
        ALL = PIECES * LUT
        STEPS = [min(LUT + (9 * (n + 1) + 1) // 2, ALL) for n in range(SLOTS)]

        def rows(o):
            return P if o < OT - 1 else OLAST

        def width(p):
            if p < OT:
                return 2 * KH * rows(p)
            return min(2, OT - 2 * (p - OT)) * HID

        def weight(p, mat, k):
            m = rows(p)
            return gu[p % RING][:, (mat * KH + k) * m:(mat * KH + k + 1) * m]

        def dest(p):
            if p < OT:
                return gu[p % RING][:, 0:width(p)]
            return wd[:, :, :].rearrange("p a h -> p (a h)")[:, 2 * (p - OT) * HID:2 * (p - OT) * HID + width(p)]

        def loads(p):
            return 2 if width(p) > HID or p < OT else 1

        def idx_count(p):
            return 16 * sum(loads(q) for q in range(p % 2, p + 1, 2))

        block = ctx.enter_context(nc.Block())

        @block.sync
        def _(sp):
            def load_idx(p):
                t = idx[p % 2]
                after(sp, cast_done, p - 1)
                if p < OT:
                    m = rows(p)
                    for j, src in enumerate((gate_idx, up_idx)):
                        sp.dma_start(t[:, j * KH * m:(j + 1) * KH * m].rearrange("p (k o) -> p k o", o=m),
                                     src[:, p * P:p * P + m].rearrange("(k p) o -> p k o", p=P)).then_inc(idx_in[p % 2], 16)
                else:
                    for j in range(loads(p)):
                        a = 2 * (p - OT) + j
                        m = rows(a)
                        if m < P:
                            sp.wait_ge(consts_done, 4)
                        sp.dma_start(t[0:m, j * HID:(j + 1) * HID], down_idx[a * P:a * P + m, :]).then_inc(idx_in[p % 2], 16)

            def load_x(b):
                sp.dma_start(xt[b % 2][:, :, :], xv[b]).then_inc(x_in[b % 2], 16)

            load_x(0)
            sp.dma_start(lut_sb[:, :], lut.rearrange("(o k) -> o k", o=1).broadcast_to([P, LUT])).then_inc(lut_in, 16)
            load_idx(0)
            load_x(1)
            load_idx(1)
            for b in (2, 3):
                sp.wait_ge(xn_done, (b - 1) * TT)
                load_x(b)
            for p in range(2, PIECES + 1):
                if p < PIECES:
                    load_idx(p)
                q = p - 2
                if q < OT:
                    m = rows(q)
                    sp.wait_ge(acc_done, LUT * (q + 1))
                    for j, d in enumerate((wg_d, wu_d)):
                        sp.dma_start(d[:, :, q * P:q * P + m],
                                     gu[q % RING][:, j * KH * m:(j + 1) * KH * m].rearrange("p (k o) -> p k o", o=m))\
                          .then_inc(stored[q % RING], 16)
            for b in range(NBLK):
                if b < 2:
                    sp.wait_ge(xn_done, (b + 3) * TT)
                else:
                    sp.wait_ge(y_done, (b - 1) * TT)
                load_x(b)
            sp.wait_ge(acc_done, ALL)
            sp.dma_start(wd_d, wd[:, :, :]).then_inc(y_out, 16)
            for b in range(NBLK):
                sp.wait_ge(y_done, (len(GROUPS) - 1) * NT + (b + 1) * TT)
                sp.dma_start(yv[b], y[:, b * TT:(b + 1) * TT, :]).then_inc(y_out, 16)
            sp.wait_ge(y_out, 16 * (NBLK + 1))
            for j in range(RING):
                sp.wait_ge(stored[j], 32 * len(range(j, OT, RING)))

        @block.gpsimd
        def _(pool):
            identity_step(pool, ident, consts_done)
            pool.memset(half[:, :], -0.5).then_inc(consts_done, 1)
            pool.wait_ge(consts_done, 3)
            for b in range(NBLK):
                pool.wait_ge(stats, (b + 1) * (2 * TT + 1))
                pool.tensor_tensor(rstd[:, :], ve[:, :], half[:, :], ALU.pow).then_inc(rstd_done, 1)
            last = PIECES - 1
            pool.wait_ge(cast_done, last - 1)
            pool.memset(idx[last % 2][OLAST:P, 0:HID], 0).then_inc(consts_done, 1)

        @block.tensor
        def _(pe):
            def transposes(b):
                pe.wait_ge(xn_done, (b + 1) * TT)
                for k in range(KH):
                    after(pe, tp_free, b * KH + k - 1)
                    for t in range(TT):
                        last = pe.transpose(tp[k % 2][:, t * P:(t + 1) * P], xn[:, t, k * P:(k + 1) * P], ident[:, :])
                    last.then_inc(tp_done, 1)

            def gate_up(o, b):
                n = o * NBLK + b
                m = rows(o)
                after(pe, h_done, n - 1)
                for mat, (bank, sem) in enumerate(((pg, gate_done), (pu, up_done))):
                    for k in range(KH):
                        last = pe.matmul(bank[n % 2][0:m, :], weight(o, mat, k), xnT[:, k, b * BLK:(b + 1) * BLK],
                                         start=(k == 0), stop=(k == KH - 1))
                    last.then_inc(sem, 1)

            pe.wait_ge(consts_done, 2)
            transposes(0)
            transposes(1)
            for o in range(OT):
                pe.wait_ge(acc_done, LUT * (o + 1))
                for b in range(NBLK):
                    if o == 0:
                        pe.wait_ge(tp_free, (b + 1) * KH)
                    gate_up(o, b)
                    if o == 0 and b + 2 < NBLK:
                        transposes(b + 2)
            pe.wait_ge(h_done, SLOTS)
            for g, (a0, a1) in enumerate(GROUPS):
                pe.wait_ge(acc_done, LUT * (OT + (a1 + 1) // 2))
                for t in range(NT):
                    after(pe, y_done, g * NT + t - 1)
                    for a in range(a0, a1):
                        m = rows(a)
                        last = pe.matmul(po[t % 2][:, :], hT[0:m, a, t * P:(t + 1) * P], wd[0:m, a, :],
                                         start=(a == a0), stop=(a == a1 - 1))
                    last.then_inc(o_done, 1)

        @block.scalar
        def _(act):
            casts = 0

            def cast(p):
                act.wait_ge(idx_in[p % 2], idx_count(p))
                if p == PIECES - 1:
                    act.wait_ge(consts_done, 4)
                after(act, hot_done, LUT * (p - 1))
                act.activation(idxb[p % 2][:, 0:width(p)], idx[p % 2][:, 0:width(p)], ACT.Copy).then_inc(cast_done, 1)

            def copies(b):
                for k in range(KH):
                    act.wait_ge(tp_done, b * KH + k + 1)
                    act.activation(xnT[:, k, b * BLK:(b + 1) * BLK], tp[k % 2][:, :], ACT.Copy).then_inc(tp_free, 1)

            cast(0)
            cast(1)
            copies(0)
            copies(1)
            casts = 2
            for n in range(SLOTS):
                while casts < PIECES and LUT * (casts - 1) <= STEPS[n]:
                    cast(casts)
                    casts += 1
                m = rows(n // NBLK)
                act.wait_ge(gate_done, n + 1)
                after(act, h_done, n - 1)
                act.activation(sil[n % 2][0:m, :], pg[n % 2][0:m, :], ACT.Silu).then_inc(sil_done, 1)
                if n + 2 < NBLK:
                    copies(n + 2)
            while casts < PIECES:
                cast(casts)
                casts += 1

        @block.vector
        def _(dve):
            def normalise(b):
                steps = Steps(stats, 2 * TT + 1, b)
                xb = xt[b % 2]
                dve.wait_ge(x_in[b % 2], 16 * (b // 2 + 1))
                for t in range(TT):
                    n = steps.mark(dve.bn_stats(st[:, t, :], xb[:, t, :]))
                steps.wait(dve, n)
                dve.memset(hold[:, :], 0.0)
                for t in range(TT):
                    n = steps.mark(dve.bn_aggr(mv[:, t, :], st[:, t, :]))
                steps.wait(dve, n)
                steps.mark(dve.tensor_scalar(ve[:, :], mv[:, :, 1], EPS, None, ALU.add))
                steps.end()
                dve.wait_ge(rstd_done, b + 1)
                after(dve, tp_done, b * KH)
                for t in range(TT):
                    dve.tensor_scalar(xn[:, t, :], xb[:, t, :], mv[:, t, 0:1], rstd[:, t:t + 1],
                                      ALU.subtract, ALU.mult).then_inc(xn_done, 1)

            def dequantise(first, last):
                for n in range(first, last):
                    p, k = divmod(n, LUT)
                    w, d = width(p), dest(p)
                    if k == 0:
                        dve.wait_ge(cast_done, p + 1)
                        if RING <= p < OT:
                            dve.wait_ge(up_done, NBLK * (p - RING + 1))
                            dve.wait_ge(stored[p % RING], 32 * (p // RING))
                    for kk in [0, 1] if k == 0 else [k + 1] if k + 1 < LUT else []:
                        dve.tensor_scalar(hot[(LUT * p + kk) % 3][:, 0:w], idxb[p % 2][:, 0:w], float(kk), None,
                                          ALU.is_equal).then_inc(hot_done, 1)
                    dve.wait_ge(hot_done, n + 1)
                    if k == 0:
                        dve.tensor_scalar(d, hot[n % 3][:, 0:w], lut_sb[:, 0:1], None, ALU.mult).then_inc(acc_done, 1)
                    else:
                        dve.wait_ge(acc_done, n)
                        dve.scalar_tensor_tensor(d, hot[n % 3][:, 0:w], lut_sb[:, k:k + 1], d,
                                                 ALU.mult, ALU.add).then_inc(acc_done, 1)

            normalise(0)
            normalise(1)
            dve.wait_ge(lut_in, 16)
            dequantise(0, LUT)
            done = LUT
            for n in range(SLOTS):
                if n + 2 < NBLK:
                    normalise(n + 2)
                dequantise(done, STEPS[n])
                done = STEPS[n]
                o, b = divmod(n, NBLK)
                m = rows(o)
                dve.wait_ge(sil_done, n + 1)
                dve.wait_ge(up_done, n + 1)
                dve.tensor_tensor(hT[0:m, o, b * BLK:(b + 1) * BLK], sil[n % 2][0:m, :], pu[n % 2][0:m, :],
                                  ALU.mult).then_inc(h_done, 1)
            for g in range(len(GROUPS)):
                for t in range(NT):
                    more = min(done + 2, ALL)
                    dequantise(done, more)
                    done = more
                    b = t // TT
                    dve.wait_ge(o_done, g * NT + t + 1)
                    if g == 0:
                        if t % TT == 0:
                            dve.wait_ge(x_in[b % 2], 32 + 16 * (b // 2 + 1))
                        rest = xt[b % 2][:, t % TT, :]
                    else:
                        dve.wait_ge(y_done, (g - 1) * NT + t + 1)
                        rest = y[:, t, :]
                    dve.scalar_tensor_tensor(y[:, t, :], po[t % 2][:, :], 0.5, rest, ALU.mult, ALU.add).then_inc(y_done, 1)
            assert done == ALL


def ffn(nc, tag, wg, wu, wd, src, dst, load):
    with ExitStack() as ctx:
        s_ = Space(nc, ctx, tag)
        x = [s_.sb(f"x{j}", [P, TT, HID]) for j in range(2)]
        y = [s_.sb(f"y{j}", [P, TT, HID]) for j in range(2)]
        xn = s_.sb("xn", [P, TT, HID])
        xnT = s_.sb("xnT", [P, KH, BLK])
        hT = s_.sb("hT", [P, OT, BLK])
        sil = [s_.sb(f"sil{j}", [P, BLK]) for j in range(2)]
        st = s_.sb("st", [P, TT, 6])
        mv = s_.sb("mv", [P, TT, 2])
        ve = s_.sb("ve", [P, TT])
        half = s_.sb("half", [P, TT])
        rstd = s_.sb("rstd", [P, TT])
        hold = s_.sb("hold", [P, 1])
        ident = s_.sb("ident", [P, P])
        tp = s_.ps("tp", 2)
        pg = s_.ps("pg", 2)
        pu = s_.ps("pu", 2)
        po = s_.ps("po", 2)
        w_in = s_.sem("w_in")
        consts_done = s_.sem("consts_done")
        x_in = s_.sems("x_in", 2)
        y_out = s_.sems("y_out", 2)
        stats = s_.sem("stats")
        rstd_done = s_.sem("rstd_done")
        xn_done = s_.sem("xn_done")
        tp_done = s_.sem("tp_done")
        tp_free = s_.sem("tp_free")
        gate_done = s_.sem("gate_done")
        up_done = s_.sem("up_done")
        sil_done = s_.sem("sil_done")
        h_done = s_.sem("h_done")
        o_done = s_.sem("o_done")
        y_done = s_.sem("y_done")
        xv = src.rearrange("(b t p) h -> b p t h", t=TT, p=P)
        yv = dst.rearrange("(b t p) h -> b p t h", t=TT, p=P)
        BANKS = 2
        block = ctx.enter_context(nc.Block())

        @block.sync
        def _(sp):
            for w, d in load:
                sp.dma_start(w[:, :, :], d).then_inc(w_in, 16)
            with sp.Fori(0, NBLK // 2) as i:
                for u in range(2):
                    sp.wait_ge(y_out[u], i * 16)
                    sp.dma_start(x[u][:, :, :], xv[i * 2 + u]).then_inc(x_in[u], 16)

        @block.gpsimd
        def _(pool):
            identity_step(pool, ident, consts_done)
            pool.memset(half[:, :], -0.5).then_inc(consts_done, 1)
            pool.wait_ge(consts_done, 3)
            with pool.Fori(0, NBLK // 2) as i:
                for u in range(2):
                    pool.wait_ge(stats, (i * 2 + u + 1) * (2 * TT + 1))
                    pool.tensor_tensor(rstd[:, :], ve[:, :], half[:, :], ALU.pow).then_inc(rstd_done, 1)
                    pool.wait_ge(y_done, (i * 2 + u + 1) * TT)
                    pool.dma_start(yv[i * 2 + u], y[u][:, :, :]).then_inc(y_out[u], 16)
            for u in range(2):
                pool.wait_ge(y_out[u], 16 * NBLK // 2)

        @block.tensor
        def _(pe):
            pe.sem_inc(tp_free, BANKS)
            pe.sem_inc(h_done, BANKS)
            pe.wait_ge(consts_done, 2)
            pe.wait_ge(w_in, 16 * len(load))
            with pe.Fori(0, NBLK // 2) as i:
                for u in range(2):
                    blk = i * 2 + u
                    pe.wait_ge(xn_done, (blk + 1) * TT)
                    for k in range(KH):
                        pe.wait_ge(tp_free, blk * KH + k + 1)
                        for t in range(TT):
                            last = pe.transpose(tp[k % 2][:, t * P:(t + 1) * P], xn[:, t, k * P:(k + 1) * P], ident[:, :])
                        last.then_inc(tp_done, 1)
                    pe.wait_ge(tp_free, blk * KH + KH + BANKS)
                    for o in range(OT):
                        m = P if o < OT - 1 else OLAST
                        bank = (u * OT + o) % 2
                        pe.wait_ge(h_done, blk * OT + o + 1)
                        for k in range(KH):
                            last = pe.matmul(pg[bank][0:m, :], wg[:, k, o * P:o * P + m], xnT[:, k, :],
                                             start=(k == 0), stop=(k == KH - 1))
                        last.then_inc(gate_done, 1)
                        for k in range(KH):
                            last = pe.matmul(pu[bank][0:m, :], wu[:, k, o * P:o * P + m], xnT[:, k, :],
                                             start=(k == 0), stop=(k == KH - 1))
                        last.then_inc(up_done, 1)
                    pe.wait_ge(h_done, blk * OT + OT + BANKS)
                    for t in range(TT):
                        if t >= 2:
                            pe.wait_ge(y_done, blk * TT + t - 1)
                        else:
                            pe.wait_ge(y_done, blk * TT)
                        for o in range(OT):
                            m = P if o < OT - 1 else OLAST
                            last = pe.matmul(po[t % 2][:, :], hT[0:m, o, t * P:(t + 1) * P], wd[0:m, o, :],
                                             start=(o == 0), stop=(o == OT - 1))
                        last.then_inc(o_done, 1)

        @block.scalar
        def _(act):
            with act.Fori(0, NBLK // 2) as i:
                for u in range(2):
                    blk = i * 2 + u
                    for k in range(KH):
                        act.wait_ge(tp_done, blk * KH + k + 1)
                        act.activation(xnT[:, k, :], tp[k % 2][:, :], ACT.Copy).then_inc(tp_free, 1)
                    for o in range(OT):
                        m = P if o < OT - 1 else OLAST
                        bank = (u * OT + o) % 2
                        act.wait_ge(gate_done, blk * OT + o + 1)
                        act.wait_ge(h_done, blk * OT + o + 1)
                        act.activation(sil[bank][0:m, :], pg[bank][0:m, :], ACT.Silu).then_inc(sil_done, 1)

        @block.vector
        def _(dve):
            with dve.Fori(0, NBLK // 2) as i:
                for u in range(2):
                    blk = i * 2 + u
                    steps = Steps(stats, 2 * TT + 1, blk)
                    dve.wait_ge(x_in[u], (i + 1) * 16)
                    for t in range(TT):
                        n = steps.mark(dve.bn_stats(st[:, t, :], x[u][:, t, :]))
                    steps.wait(dve, n)
                    dve.memset(hold[:, :], 0.0)
                    for t in range(TT):
                        m = steps.mark(dve.bn_aggr(mv[:, t, :], st[:, t, :]))
                    steps.wait(dve, m)
                    steps.mark(dve.tensor_scalar(ve[:, :], mv[:, :, 1], EPS, None, ALU.add))
                    steps.end()
                    dve.wait_ge(rstd_done, blk + 1)
                    dve.wait_ge(tp_done, blk * KH)
                    for t in range(TT):
                        dve.tensor_scalar(xn[:, t, :], x[u][:, t, :], mv[:, t, 0:1], rstd[:, t:t + 1],
                                          ALU.subtract, ALU.mult).then_inc(xn_done, 1)
                    for o in range(OT):
                        m = P if o < OT - 1 else OLAST
                        bank = (u * OT + o) % 2
                        dve.wait_ge(sil_done, blk * OT + o + 1)
                        dve.wait_ge(up_done, blk * OT + o + 1)
                        dve.wait_ge(o_done, blk * TT)
                        dve.tensor_tensor(hT[0:m, o, :], sil[bank][0:m, :], pu[bank][0:m, :], ALU.mult).then_inc(h_done, 1)
                    for t in range(TT):
                        dve.wait_ge(o_done, blk * TT + t + 1)
                        dve.wait_ge(y_out[u], i * 16)
                        dve.scalar_tensor_tensor(y[u][:, t, :], po[t % 2][:, :], 0.5, x[u][:, t, :],
                                                 ALU.mult, ALU.add).then_inc(y_done, 1)


def decays(nc, x1, xnT_d, a_d, beta_d, Wa, ba, Wb, bb):
    with ExitStack() as ctx:
        s_ = Space(nc, ctx, "dc")
        x = [s_.sb(f"x{j}", [P, TT, HID]) for j in range(2)]
        xn = s_.sb("xn", [P, TT, HID])
        xnT = s_.sb("xnT", [P, KH, TOK])
        st = s_.sb("st", [P, TT, 6])
        mv = s_.sb("mv", [P, TT, 2])
        ve = s_.sb("ve", [P, TT])
        half = s_.sb("half", [P, TT])
        rstd = s_.sb("rstd", [P, TT])
        ident = s_.sb("ident", [P, P])
        wa = [s_.sb(f"wa{j}", [P, KH, BLK]) for j in range(2)]
        wb = s_.sb("wb", [P, KH, 2 * H])
        bab = s_.sb("bab", [P, C])
        bbc = s_.sb("bbc", [2 * H, 1])
        RA = 4
        sa = [s_.sb(f"sa{j}", [P, BLK]) for j in range(RA)]
        be = s_.sb("be", [2 * H, B, 2, T])
        tp = s_.ps("tp", 2)
        pa = s_.ps("pa", 4)
        consts_done = s_.sem("consts_done")
        x_in = s_.sems("x_in", 2)
        w_in = s_.sem("w_in")
        wa_in = s_.sems("wa_in", 2)
        stats = s_.sem("stats")
        rstd_done = s_.sem("rstd_done")
        xn_done = s_.sem("xn_done")
        tp_done = s_.sem("tp_done")
        tp_free = s_.sem("tp_free")
        xnT_out = s_.sem("xnT_out")
        b_done = s_.sem("b_done")
        beta_done = s_.sem("beta_done")
        nbeta_done = s_.sem("nbeta_done")
        beta_out = s_.sem("beta_out")
        pa_done = s_.sem("pa_done")
        sum_done = s_.sem("sum_done")
        sig_done = s_.sem("sig_done")
        a_out = s_.sems("a_out", RA)
        xv = x1.rearrange("(b t p) h -> b p t h", t=TT, p=P)
        wav = Wa.rearrange("(k p) c -> p k c", p=P)
        NT = TOK // P
        CB = C // BLK
        block = ctx.enter_context(nc.Block())

        @block.sync
        def _(sp):
            sp.dma_start(x[0][:, :, :], xv[0]).then_inc(x_in[0], 16)
            sp.dma_start(x[1][:, :, :], xv[1]).then_inc(x_in[1], 16)
            sp.dma_start(wb[:, :, :], Wb.rearrange("(k p) c -> p k c", p=P)).then_inc(w_in, 16)
            sp.dma_start(bab[:, :], ba.rearrange("(o c) -> o c", o=1).broadcast_to([P, C])).then_inc(w_in, 16)
            sp.dma_start(bbc[:, :], bb.rearrange("(c o) -> c o", o=1)).then_inc(w_in, 16)
            for u in range(2):
                sp.dma_start(wa[u][:, :, :], wav[:, :, u * BLK:(u + 1) * BLK]).then_inc(wa_in[u], 16)
            for blk in range(2, NBLK):
                sp.wait_ge(xn_done, (blk - 1) * TT)
                sp.dma_start(x[blk % 2][:, :, :], xv[blk]).then_inc(x_in[blk % 2], 16)
            sp.wait_ge(tp_free, NBLK * KH + 2)
            sp.dma_start(xnT_d, xnT[:, :, :]).then_inc(xnT_out, 16)
            sp.wait_ge(nbeta_done, B)
            bv = beta_d.rearrange("(b q) c t -> q b c t", b=B)
            for b in range(B):
                sp.dma_start(bv[:, b, :, 0:T], be[:, b]).then_inc(beta_out, 16)
            for cb in range(CB):
                if 1 <= cb < CB - 1:
                    sp.wait_ge(pa_done, cb * NT)
                    sp.dma_start(wa[(cb + 1) % 2][:, :, :], wav[:, :, (cb + 1) * BLK:(cb + 2) * BLK])\
                      .then_inc(wa_in[(cb + 1) % 2], 16)
                with sp.Fori(0, NT // RA) as j:
                    for r in range(RA):
                        sp.wait_ge(sig_done, j * RA + (cb * NT + r + 1))
                        sp.dma_start(a_d[r * P:(r + 1) * P, j, cb * BLK:(cb + 1) * BLK], sa[r][:, :])\
                          .then_inc(a_out[r], 16)
            sp.wait_ge(xnT_out, 16)
            sp.wait_ge(beta_out, 16 * B)
            for r in range(RA):
                sp.wait_ge(a_out[r], 16 * CB * NT // RA)

        @block.gpsimd
        def _(pool):
            identity_step(pool, ident, consts_done)
            pool.memset(half[:, :], -0.5).then_inc(consts_done, 1)
            pool.wait_ge(consts_done, 3)
            for blk in range(NBLK):
                pool.wait_ge(stats, (blk + 1) * (2 * TT + 1))
                pool.tensor_tensor(rstd[:, :], ve[:, :], half[:, :], ALU.pow).then_inc(rstd_done, 1)

        @block.tensor
        def _(pe):
            pe.sem_inc(tp_free, 2)
            pe.sem_inc(sum_done, 4)
            pe.wait_ge(consts_done, 2)
            for blk in range(NBLK):
                pe.wait_ge(xn_done, (blk + 1) * TT)
                for k in range(KH):
                    pe.wait_ge(tp_free, blk * KH + k + 1)
                    for t in range(TT):
                        last = pe.transpose(tp[k % 2][:, t * P:(t + 1) * P], xn[:, t, k * P:(k + 1) * P], ident[:, :])
                    last.then_inc(tp_done, 1)
            pe.wait_ge(tp_free, NBLK * KH + 2)
            pe.wait_ge(w_in, 48)
            for b in range(B):
                if b >= 2:
                    pe.wait_ge(beta_done, b - 1)
                for k in range(KH):
                    last = pe.matmul(tp[b % 2][0:2 * H, :], wb[:, k, :], xnT[:, k, b * T:(b + 1) * T],
                                     start=(k == 0), stop=(k == KH - 1))
                last.then_inc(b_done, 1)
            with pe.Fori(0, CB // 2) as i:
                for u in range(2):
                    pe.wait_ge(wa_in[u], (i + 1) * 16)
                    for t in range(NT):
                        n = (i * 2 + u) * NT + t
                        pe.wait_ge(sum_done, n + 1)
                        for k in range(KH):
                            last = pe.matmul(pa[t % 4][:, :], xnT[:, k, t * P:(t + 1) * P], wa[u][:, k, :],
                                             start=(k == 0), stop=(k == KH - 1))
                        last.then_inc(pa_done, 1)

        @block.scalar
        def _(act):
            for blk in range(NBLK):
                for k in range(KH):
                    act.wait_ge(tp_done, blk * KH + k + 1)
                    act.activation(xnT[:, k, blk * BLK:(blk + 1) * BLK], tp[k % 2][:, :], ACT.Copy).then_inc(tp_free, 1)
            act.wait_ge(w_in, 48)
            for b in range(B):
                act.wait_ge(b_done, b + 1)
                act.activation(be[:, b, 0, :], tp[b % 2][0:2 * H, :], ACT.Sigmoid, bias=bbc[:, 0:1]).then_inc(beta_done, 1)
            for b in range(B):
                act.wait_ge(beta_done, b + 1)
                act.activation(be[:, b, 1, :], be[:, b, 0, :], ACT.Copy, scale=-S2).then_inc(nbeta_done, 1)
            with act.Fori(0, CB * NT // RA) as i:
                for r in range(RA):
                    act.wait_ge(sum_done, i * RA + r + 1 + 4)
                    act.activation(sa[r][:, :], sa[r][:, :], ACT.Sigmoid).then_inc(sig_done, 1)

        @block.vector
        def _(dve):
            for blk in range(NBLK):
                steps = Steps(stats, 2 * TT + 1, blk)
                dve.wait_ge(x_in[blk % 2], (blk // 2 + 1) * 16)
                for t in range(TT):
                    n = steps.mark(dve.bn_stats(st[:, t, :], x[blk % 2][:, t, :]))
                steps.wait(dve, n)
                for t in range(TT):
                    m = steps.mark(dve.bn_aggr(mv[:, t, :], st[:, t, :]))
                steps.wait(dve, m)
                steps.mark(dve.tensor_scalar(ve[:, :], mv[:, :, 1], EPS, None, ALU.add))
                steps.end()
                dve.wait_ge(rstd_done, blk + 1)
                if blk:
                    dve.wait_ge(tp_done, blk * KH)
                for t in range(TT):
                    dve.tensor_scalar(xn[:, t, :], x[blk % 2][:, t, :], mv[:, t, 0:1], rstd[:, t:t + 1],
                                      ALU.subtract, ALU.mult).then_inc(xn_done, 1)
            dve.wait_ge(w_in, 48)
            for cb in range(CB):
                with dve.Fori(0, NT // RA) as j:
                    for r in range(RA):
                        dve.wait_ge(pa_done, j * RA + (cb * NT + r + 1))
                        dve.wait_ge(a_out[r], (j + cb * (NT // RA)) * 16)
                        dve.tensor_tensor(sa[r][:, :], pa[r][:, :], bab[:, cb * BLK:(cb + 1) * BLK], ALU.add)\
                           .then_inc(sum_done, 1)


def heads(nc, xnT_d, kq_d, kt_d, v_d, Wqkv, conv):
    with ExitStack() as ctx:
        s_ = Space(nc, ctx, "hd")
        x = [s_.sb(f"x{j}", [P, KH, T]) for j in range(2)]
        w = [s_.sb(f"w{j}", [P, 3, KH, P]) for j in range(2)]
        xh, xl = (s_.sb(name, [P, B, KH, T], F32R) for name in ("xh", "xl"))
        wh, wl = ([s_.sb(f"{name}{j}", [P, 3, KH, P], F32R) for j in range(2)] for name in ("wh", "wl"))
        cw = s_.sb("cw", [P, H, 3, K + 1])
        cwh = [s_.sb(f"cwh{j}", [P, 3, K + 1]) for j in range(2)]
        ident = s_.sb("ident", [P, P])
        R = 4
        yr = [s_.sb(f"y{j}", [P, T]) for j in range(R)]
        kq = [[s_.sb(f"kq{u}{b}", [P, T, 2]) for b in range(B)] for u in range(2)]
        vr = [s_.sb(f"v{b}", [P, T]) for b in range(B)]
        tr = [s_.sb(f"t{j}", [P, TT, P]) for j in range(B)]
        kp = [s_.sb(f"kp{j}", [P, 3, TT, P], BF16) for j in range(B)]
        kr = [s_.sb(f"kr{j}", [P, TT, P]) for j in range(2)]
        pp = s_.ps("pp", R)
        pt = s_.ps("pt", 2)
        consts_done = s_.sem("consts_done")
        x_in = s_.sems("x_in", 2)
        hi_done = s_.sem("hi_done")
        lo_done = s_.sem("lo_done")
        w_in = s_.sems("w_in", 2)
        cw_in = s_.sem("cw_in")
        cwh_done = s_.sem("cwh_done")
        proj_done = s_.sem("proj_done")
        conv_open = s_.sem("conv_open")
        taps = s_.sem("taps")
        conv_done = s_.sem("conv_done")
        silu_done = s_.sem("silu_done")
        tr_done = s_.sem("tr_done")
        v_free = s_.sem("v_free")
        k1_done = s_.sem("k1_done")
        k_free = s_.sem("k_free")
        k2_done = s_.sem("k2_done")
        k3_done = s_.sem("k3_done")
        kq_out = [s_.sems(f"kq_out{u}", B) for u in range(2)]
        v_out = s_.sems("v_out", B)
        k_out = s_.sems("k_out", B)
        UNITS = [(u, m, b) for u in range(2) for m in range(3) for b in range(B)]
        NU = len(UNITS)
        TRS = [n for n, (u, m, b) in enumerate(UNITS) if m < 2]

        def result(n):
            u, m, b = UNITS[n]
            return vr[b][:, :] if m == 1 else kq[u][b][:, :, m // 2]

        nth = {n: j for j, n in enumerate(TRS)}
        NTR = len(TRS)
        NKV = NTR // 2
        LAG_TR, LAG_EV, LAG_K3 = 2, 3, 4
        SPLITS = {2: (0, 1), NU // 2 + 2: (1, 0)}
        FIRST = B + 1

        def bank_free(pe, i, j):
            if j < 2:
                pe.wait_ge(v_free, i * NKV)
            else:
                u, m, b = UNITS[TRS[j - 2]]
                pe.wait_ge((k_free, v_free)[m], i * NKV + u * B + b + 1)
        block = ctx.enter_context(nc.Block())

        @block.sync
        def _(sp):
            for b in range(B):
                after(sp, lo_done, b - 1)
                sp.dma_start(x[b % 2][:, :, :], xnT_d[:, :, b * T:(b + 1) * T]).then_inc(x_in[b % 2], 16)
            with sp.Fori(0, H // 2) as i:
                for n in range(NU + LAG_EV):
                    if n < NU and UNITS[n][1] == 2:
                        u, m, b = UNITS[n]
                        sp.wait_ge(silu_done, i * NU + n + 1)
                        sp.dma_start(kq_d[:, b * H + i * 2 + u, 0:T, :], kq[u][b][:, :, :]).then_inc(kq_out[u][b], 16)
                    if n - LAG_K3 in nth and UNITS[n - LAG_K3][1] == 0:
                        u, m, b = UNITS[n - LAG_K3]
                        sp.wait_ge(k3_done, i * NKV + u * B + b + 1)
                        for part in range(3):
                            dst = kt_d[part, 0:T, b, :].rearrange("(t p) (i c) -> i p t c", p=P, c=2 * D)[i]
                            sp.dma_start(dst[:, :, u * D:(u + 1) * D], kp[b][:, part, :, :]).then_inc(k_out[b], 16)
            for b in range(B):
                for u in range(2):
                    sp.wait_ge(kq_out[u][b], 16 * (H // 2))
                sp.wait_ge(k_out[b], 48 * H)

        @block.gpsimd
        def _(pool):
            identity_step(pool, ident, consts_done)
            pool.dma_start(cw[:, :, :, :], conv.rearrange("h p m k -> p h m k")).then_inc(cw_in, 16)
            pool.dma_start(w[0][:, :, :, :], Wqkv[0]).then_inc(w_in[0], 16)
            with pool.Fori(0, H // 2) as i:
                for u in range(2):
                    pool.wait_ge(lo_done, i * 2 + (FIRST - 1 + u))
                    pool.dma_start(w[1 - u][:, :, :, :], Wqkv[i * 2 + (u + 1)]).then_inc(w_in[1 - u], 16)
                for u in range(2):
                    for b in range(B):
                        pool.wait_ge(v_free, i * NKV + u * B + b + 1)
                        dst = v_d[0:T, b, :].rearrange("(t p) (h c) -> h p t c", p=P, c=D)
                        pool.dma_start(dst[i * 2 + u], tr[b][:, :, :]).then_inc(v_out[b], 16)

            for b in range(B):
                pool.wait_ge(v_out[b], 16 * H)

        @block.tensor
        def _(pe):
            pe.sem_inc(conv_done, R)
            pe.wait_ge(consts_done, 2)
            pe.wait_ge(lo_done, FIRST)
            with pe.Fori(0, H // 2) as i:
                for n in range(NU):
                    u, m, b = UNITS[n]
                    if m == 0 and b == 0:
                        pe.wait_ge(lo_done, i * 2 + (FIRST + u))
                    pe.wait_ge(conv_done, i * NU + n + 1)
                    passes = [(k, p, q) for k in range(KH) for p, q in ((wl, xh), (wh, xl), (wh, xh))]
                    for j, (k, p, q) in enumerate(passes):
                        last = pe.matmul(pp[n % R][:, :], p[u][:, m, k, :], q[:, b, k, :],
                                         start=(j == 0), stop=(j == len(passes) - 1))
                    last.then_inc(proj_done, 1)
                    if n - LAG_TR in nth:
                        j = nth[n - LAG_TR]
                        pe.wait_ge(silu_done, i * NU + n - LAG_TR + 1)
                        bank_free(pe, i, j)
                        for t in range(TT):
                            last = pe.transpose(pt[j % 2][:, t * P:(t + 1) * P],
                                                result(n - LAG_TR)[:, t * P:(t + 1) * P], ident[:, :])
                        last.then_inc(tr_done, 1)

        @block.scalar
        def _(act):
            for b in range(B):
                act.wait_ge(x_in[b % 2], 16 * (b // 2 + 1))
                act.activation(xh[:, b, :, :], x[b % 2][:, :, :], ACT.Copy).then_inc(hi_done, 1)

            def high(u):
                act.activation(wh[u][:, :, :, :], w[u][:, :, :, :], ACT.Copy).then_inc(hi_done, 1)

            act.wait_ge(w_in[0], 16)
            high(0)
            act.wait_ge(cw_in, 16)

            def silu(i, n):
                u, m, b = UNITS[n]
                act.wait_ge(conv_done, i * NU + n + 1 + R)
                if m != 1:
                    act.wait_ge(kq_out[u][b], i * 16)
                else:
                    act.wait_ge(tr_done, i * NTR + (nth[n - 3 * B] + 1 if u else 0))
                act.activation(result(n), yr[n % R][:, :], ACT.Silu).then_inc(silu_done, 1)

            with act.Fori(0, H // 2) as i:
                for n in range(NU):
                    u, m, b = UNITS[n]
                    if m == 0 and b == 0:
                        act.wait_ge(conv_done, i * NU + R)
                        act.activation(cwh[u][:, :, :], cw[:, bass.ds(i * 2 + u, 1), :, :].rearrange("p o m k -> p (o m) k"),
                                       ACT.Copy).then_inc(cwh_done, 1)
                        act.wait_ge(cwh_done, i * 2 + u + 1)
                    act.wait_ge(proj_done, i * NU + n + 1)
                    if n in SPLITS:
                        more, v = SPLITS[n]
                        act.wait_ge(w_in[v], i * 16 + (16 + 16 * more))
                        high(v)
                    act.activation(yr[n % R][:, :], pp[n % R][:, :], ACT.Identity,
                                   bias=cwh[u][:, m, K:K + 1], scale=cwh[u][:, m, K - 1:K]).then_inc(conv_open, 1)
                    if n >= 1:
                        silu(i, n - 1)
                    if n - LAG_EV in nth:
                        j = nth[n - LAG_EV]
                        u, m, b = UNITS[n - LAG_EV]
                        act.wait_ge(tr_done, i * NTR + j + 1)
                        if m:
                            act.wait_ge(v_out[b], i * 32 + u * 16)
                            act.activation(tr[b][:, :, :].rearrange("p t c -> p (t c)"), pt[j % 2][:, :], ACT.Copy)\
                               .then_inc(v_free, 1)
                        else:
                            act.wait_ge(k_out[b], i * 96 + u * 48)
                            act.activation(kp[b][:, 0, :, :].rearrange("p t c -> p (t c)"), pt[j % 2][:, :], ACT.Copy)\
                               .then_inc(k1_done, 1)
                    if n - LAG_K3 in nth and UNITS[n - LAG_K3][1] == 0:
                        u, m, b = UNITS[n - LAG_K3]
                        act.wait_ge(k_free, i * NKV + u * B + b + 1)
                        act.activation(kp[b][:, 1, :, :], kr[b % 2][:, :, :], ACT.Copy).then_inc(k2_done, 1)
                silu(i, NU - 1)

        @block.vector
        def _(dve):
            for b in range(B):
                dve.wait_ge(hi_done, b + 1)
                dve.tensor_tensor(xl[:, b, :, :], x[b % 2][:, :, :], xh[:, b, :, :].bitcast(F32), ALU.subtract)\
                   .then_inc(lo_done, 1)

            def low(u):
                dve.tensor_tensor(wl[u][:, :, :, :], w[u][:, :, :, :], wh[u][:, :, :, :].bitcast(F32), ALU.subtract)\
                   .then_inc(lo_done, 1)

            dve.wait_ge(hi_done, FIRST)
            low(0)
            with dve.Fori(0, H // 2) as i:
                for n in range(NU):
                    u, m, b = UNITS[n]
                    dve.wait_ge(conv_open, i * NU + n + 1)
                    y, p = yr[n % R], pp[n % R]
                    for j in range(1, K):
                        ins = dve.scalar_tensor_tensor(y[:, j:T], p[:, 0:T - j], cwh[u][:, m, K - 1 - j:K - j],
                                                       y[:, j:T], ALU.mult, ALU.add)
                        if j < K - 1:
                            ins.then_inc(taps, 1)
                            dve.wait_ge(taps, i * (2 * NU) + 2 * n + j)
                        else:
                            ins.then_inc(conv_done, 1)
                    if n in SPLITS:
                        more, v = SPLITS[n]
                        dve.wait_ge(hi_done, i * 2 + (FIRST + 1 + more))
                        low(v)
                    if n - LAG_EV in nth and UNITS[n - LAG_EV][1] == 0:
                        u, m, b = UNITS[n - LAG_EV]
                        dve.wait_ge(k1_done, i * NKV + u * B + b + 1)
                        dve.tensor_tensor(kr[b % 2][:, :, :].rearrange("p t c -> p (t c)"), pt[nth[n - LAG_EV] % 2][:, :],
                                          kp[b][:, 0, :, :].rearrange("p t c -> p (t c)"), ALU.subtract).then_inc(k_free, 1)
                    if n - LAG_K3 in nth and UNITS[n - LAG_K3][1] == 0:
                        u, m, b = UNITS[n - LAG_K3]
                        dve.wait_ge(k2_done, i * NKV + u * B + b + 1)
                        dve.tensor_tensor(kp[b][:, 2, :, :], kr[b % 2][:, :, :], kp[b][:, 1, :, :], ALU.subtract)\
                           .then_inc(k3_done, 1)


def scan(nc, kq_d, kt_d, v_d, a_d, beta_d, g_d, z_d, w_d, o_d):
    with ExitStack() as ctx:
        s_ = Space(nc, ctx, "sc")
        S = s_.sb("S", [P, N, D])
        kq = [s_.sb(f"kq{j}", [P, N, SUP, 2]) for j in range(2)]
        kt = s_.sb("kt", [P, N, D], BF16)
        wt = s_.sb("wt", [P, N, D], BF16)
        A3 = wt[KW:KW + 3, :, :].rearrange("p n d -> p (n d)")
        za = s_.sb("za", [P, N // 4, D])
        gs = [s_.sb(f"gs{j}", [2 * SUP, SBLK]) for j in range(2)]
        av = [s_.sb(f"a{j}", [P, CH, DH]) for j in range(2)]
        vv = [s_.sb(f"v{j}", [P, CH, DH]) for j in range(2)]
        bt = [s_.sb(f"bt{j}", [P, 2, CH]) for j in range(2)]
        g2 = [s_.sb(f"g2{j}", [P, CH + 1, 2, CH]) for j in range(2)]
        z = s_.sb("z", [P, CH, 2, DH])
        zq = s_.sb("zq", [P, CH, DH])
        pk = s_.sb("pk", [P, CH, DH])
        hist = s_.sb("hist", [P, CH * (CH + 1) // 2, DH])
        wp = s_.sb("wp", [P, 3, CH, DH], BF16)
        o = s_.sb("o", [P, CH, DH])
        Ac = s_.sb("Ac", [P, CH + 1, DH])
        nbA = s_.sb("nbA", [P, CH, DH])
        r1 = s_.sb("r1", [P, DH])
        a3p = s_.sb("a3p", [P, 3, DH], BF16)
        ones3 = s_.sb("ones3", [KW + 3, P], BF16)
        pA = s_.ps("pA", 2)
        pU = s_.ps("pU", 2)
        pz = s_.ps("pz", 2)
        pG = s_.ps("pG", 2)

        start = s_.sem("start")
        pad_done = s_.sem("pad_done")
        kq_in = s_.sems("kq_in", 2)
        kt_in = s_.sem("kt_in")
        a_in = s_.sems("a_in", 2)
        g2_in = s_.sems("g2_in", 2)
        g_done = s_.sem("g_done")
        gs_done = s_.sem("gs_done")
        gs_out = s_.sems("gs_out", 2)
        z_done = s_.sem("z_done")
        zs_done = s_.sem("zs_done")
        z_out = s_.sems("z_out", 4)
        z_in = s_.sem("z_in")
        w_out = s_.sems("w_out", 3)
        pq_done = s_.sem("pq_done")
        prep = s_.sem("prep")
        zq_done = s_.sem("zq_done")
        o_sum = s_.sem("o_sum")
        o_out = s_.sem("o_out")
        step = s_.sem("step")
        w_in = s_.sem("w_in")
        wp_done = s_.sem("wp_done")
        A_in = s_.sem("A_in")
        A_done = s_.sem("A_done")
        U_done = s_.sem("U_done")
        S_dec = s_.sem("S_dec")
        S_done = s_.sem("S_done")

        LOOP = 8
        TURNS = NCH // LOOP
        GB = N * SUP // SBLK
        GN = SBLK // SUP
        PREP = CH + 7
        W_END = 4 + 3 * (CH - 2) + 2
        STEP = W_END + 2 + CH + 1
        SPT = LOOP // CPS

        def w_at(t):
            return hist[:, t * (t + 1) // 2:(t + 1) * (t + 2) // 2, :]

        gdv = g_d
        av_d = a_d.rearrange("t b (q d) -> (b q) t d", d=DH)
        vv_d = v_d.rearrange("t b (q d) -> (b q) t d", d=DH)
        ov_d = o_d.rearrange("t b (q d) -> (b q) t d", d=DH)
        block = ctx.enter_context(nc.Block())

        def load_chunk(sp, u, t0):
            sp.dma_start(av[u][:, :, :], av_d[:, bass.ds(t0, CH), :]).then_inc(a_in[u], 16)
            sp.dma_start(vv[u][:, :, :], vv_d[:, bass.ds(t0, CH), :]).then_inc(a_in[u], 16)
            sp.dma_start(bt[u][:, :, :], beta_d[:, :, bass.ds(t0, CH)]).then_inc(a_in[u], 16)

        def load_kt(sp, t0):
            for r, parts in STACK:
                for part in range(parts):
                    lo = r + part * CH
                    sp.dma_start(kt[lo:lo + CH, :, :].rearrange("s n d -> s (n d)"),
                                 kt_d[part, bass.ds(t0, CH)].rearrange("t b c -> t (b c)")).then_inc(kt_in, 16)

        def load_g(sp, u, par, j):
            for half in range(2):
                for q in range(2):
                    src = gdv[par, j * CH:(j + 1) * CH, q, :, j * CH:(j + 1) * CH].rearrange("t n s -> n t s")
                    dst = g2[u][half:P:2, q:q + CH, 1 - q, :]
                    sp.dma_start(dst, src).then_inc(g2_in[u], 16)

        @block.sync
        def _(sp):
            sp.dma_start(kq[0][:, :, :, :], kq_d[:, :, 0:SUP, :]).then_inc(kq_in[0], 16)
            load_chunk(sp, 0, 0)
            sp.dma_start(kq_d[:, :, T:T + SUP, :], kq_d[:, :, 0:SUP, :]).then_inc(pad_done, 16)
            for d in (a_d, v_d):
                sp.dma_start(d[T:T + CH], d[0:CH]).then_inc(pad_done, 16)
            sp.dma_start(beta_d[:, :, T:T + CH], beta_d[:, :, 0:CH]).then_inc(pad_done, 16)
            sp.wait_ge(pad_done, 64)
            for m in range(GB):
                sp.wait_ge(gs_done, m + 1)
                sp.dma_start(gdv[0, :, :, m * GN:(m + 1) * GN, :].rearrange("t q n s -> (t q) n s"),
                             gs[m % 2][:, :].rearrange("p (n s) -> p n s", s=SUP)).then_inc(gs_out[m % 2], 16)
            for m in range(2):
                sp.wait_ge(gs_out[m], 16 * GB // 2)
            load_g(sp, 0, 0, 0)
            with sp.Fori(0, TURNS) as i:
                for cc in range(LOOP):
                    c = i * LOOP + cc
                    u, nu, j = cc % 2, (cc + 1) % 2, cc % CPS
                    banks_before = i * (LOOP * NSB) + cc * NSB
                    t_next = i * (LOOP * CH) + (cc + 1) * CH
                    if j == 0:
                        par = (cc // CPS + 1) % 2
                        nxt = (i * SPT + cc // CPS + 1) * SUP
                        sp.wait_ge(z_done, banks_before)
                        sp.dma_start(kq[par][:, :, :, :], kq_d[:, :, bass.ds(nxt, SUP), :]).then_inc(kq_in[par], 16)
                    if j == CPS - 1:
                        par = (cc // CPS + 1) % 2
                        sup = i * SPT + cc // CPS + 1
                        for m in range(GB):
                            sp.wait_ge(gs_done, sup * GB + m + 1)
                            sp.dma_start(gdv[par, :, :, m * GN:(m + 1) * GN, :].rearrange("t q n s -> (t q) n s"),
                                         gs[m % 2][:, :].rearrange("p (n s) -> p n s", s=SUP)).then_inc(gs_out[m % 2], 16)
                    sp.wait_ge(step, c * STEP)
                    sp.wait_ge(S_done, banks_before)
                    load_chunk(sp, nu, t_next)
                    load_kt(sp, i * (LOOP * CH) + cc * CH)
                    if j < CPS - 1:
                        load_g(sp, nu, (cc // CPS) % 2, j + 1)
                    sp.wait_ge(prep, c * PREP + PREP)
                    for r in range(3):
                        sp.dma_start(A3[r:r + 1, :].rearrange("o (p d) -> o p d", d=DH), a3p[:, r, :]).then_inc(A_in, 16)
                    if j == CPS - 1:
                        for m in range(2):
                            sp.wait_ge(gs_out[m], (i * SPT + cc // CPS + 2) * (16 * GB // 2))
                        load_g(sp, nu, (cc // CPS + 1) % 2, 0)
                    for part in range(3):
                        if part < 2:
                            sp.wait_ge(wp_done, c * 2 + (part + 1))
                        else:
                            sp.wait_ge(step, c * STEP + (W_END + 2))
                        sp.dma_start(w_d[part * CH:(part + 1) * CH, :].rearrange("s (p d) -> p s d", d=DH),
                                     wp[:, part, :, :]).then_inc(w_out[part], 16)
                    for part, (r, copies) in enumerate(STACK):
                        sp.wait_ge(w_out[part], c * 16 + 16)
                        for lo in range(r, r + copies * CH, CH):
                            sp.dma_start(wt[lo:lo + CH, :, :].rearrange("s n d -> s (n d)"),
                                         w_d[part * CH:(part + 1) * CH, :]).then_inc(w_in, 16)
                    sp.wait_ge(zq_done, c + 1)
                    for q in range(4):
                        sp.wait_ge(z_out[q], c * 16 + 16)
                        sp.dma_start(z[q * 32:(q + 1) * 32, :, :, :].rearrange("p t q d -> p (t q) d"),
                                     z_d[q].rearrange("r (p d) -> p r d", d=DH)).then_inc(z_in, 16)

        @block.scalar
        def _(act):
            def g_banks(sup):
                for m in range(GB):
                    act.wait_ge(g_done, sup * GB + m + 1)
                    act.wait_ge(gs_out[m % 2], sup * (16 * GB // 2) + 16 * (m // 2))
                    act.activation(gs[m % 2][:, :], pG[m % 2][0:2 * SUP, :], ACT.Copy).then_inc(gs_done, 1)

            g_banks(0)
            with act.Fori(0, TURNS) as i:
                for cc in range(LOOP):
                    c = i * LOOP + cc
                    if cc % CPS == CPS - 1:
                        g_banks(i * SPT + cc // CPS + 1)

                    def q_terms(t):
                        for x in range(t + 1):
                            ins = act.activation(w_at(t)[:, x, :], w_at(t)[:, x, :], ACT.Copy, scale=g2[cc % 2][:, t + 1, 0, x:x + 1])
                        ins.then_inc(pq_done, 1)

                    act.wait_ge(g2_in[cc % 2], (i * 4 + cc // 2 + 1) * 64)
                    for t in range(CH - 2):
                        act.wait_ge(step, c * STEP + (3 * t + 5))
                        q_terms(t)
                    act.wait_ge(step, c * STEP + W_END)
                    act.wait_ge(w_out[0], c * 16)
                    act.activation(wp[:, 0, :, :], w_at(CH - 1), ACT.Copy).then_inc(wp_done, 1)
                    act.wait_ge(step, c * STEP + (W_END + 1))
                    act.wait_ge(w_out[1], c * 16)
                    act.activation(wp[:, 1, :, :], pk[:, :, :], ACT.Copy).then_inc(wp_done, 1)
                    q_terms(CH - 2)
                    q_terms(CH - 1)
                    for m in range(NSB):
                        q, mm = m // (NSB // 4), m % (NSB // 4)
                        act.wait_ge(z_done, (c + 1) * NSB + m + 1)
                        if m == 0:
                            act.wait_ge(z_in, c * 64 + 64)
                        act.activation(za[32 * q:32 * q + 32, mm * NPB:(mm + 1) * NPB, :].rearrange("p n d -> p (n d)"),
                                       pz[m % 2][0:32, :], ACT.Copy).then_inc(zs_done, 1)
                        if mm == NSB // 4 - 1:
                            act.wait_ge(zs_done, (c + 1) * NSB + m + 1)
                            act.dma_start(z_d[q], za[32 * q:32 * q + 32, :, :].rearrange("r n d -> r (n d)"))\
                               .then_inc(z_out[q], 16)

        @block.tensor
        def _(pe):
            def g_banks(sup, par):
                for m in range(GB):
                    if m >= 2:
                        pe.wait_ge(gs_done, sup * GB + m - 1)
                    else:
                        pe.wait_ge(gs_done, sup * GB)
                    for n in range(GN):
                        x = kq[par][:, m * GN + n, :, :]
                        last = pe.matmul(pG[m % 2][0:2 * SUP, n * SUP:(n + 1) * SUP], x.rearrange("p t a -> p (t a)"), x[:, :, 0],
                                         start=True, stop=True)
                    last.then_inc(g_done, 1)

            pe.wait_ge(kq_in[0], 16)
            g_banks(0, 0)
            pe.sem_inc(z_done, NSB)
            pe.wait_ge(start, 5)
            with pe.Fori(0, TURNS) as i:
                for cc in range(LOOP):
                    c = i * LOOP + cc
                    u = cc % 2
                    if cc % CPS == CPS - 1:
                        sup = cc // CPS + 1
                        pe.wait_ge(kq_in[sup % 2], i * (16 * SPT // 2) + 16 * (sup // 2 + 1))
                        g_banks(i * SPT + sup, sup % 2)
                    j1 = (cc + 1) % CPS
                    par1 = ((cc + 1) // CPS) % 2
                    pe.wait_ge(A_in, (c + 1) * 48)
                    for m in range(NSB):
                        if m >= 2:
                            pe.wait_ge(S_dec, c * NSB + m - 1)
                        pe.matmul(pA[m % 2][:, :], ones3[KW:KW + 3, :], A3[:, m * SBLK:(m + 1) * SBLK],
                                  start=True, stop=True).then_inc(A_done, 1)
                    pe.wait_ge(kt_in, c * 96 + 96)
                    pe.wait_ge(w_in, c * 96 + 96)

                    def update(m):
                        if m >= 2:
                            pe.wait_ge(S_done, c * NSB + m - 1)
                        for n in range(NPB):
                            nn = m * NPB + n
                            last = pe.matmul(pU[m % 2][:, n * D:(n + 1) * D], kt[0:KW, nn, :], wt[0:KW, nn, :],
                                             start=True, stop=True)
                        last.then_inc(U_done, 1)

                    def project(m):
                        pe.wait_ge(S_done, c * NSB + m + 1)
                        if m >= 2:
                            pe.wait_ge(zs_done, (c + 1) * NSB + m - 1)
                        else:
                            pe.wait_ge(zs_done, (c + 1) * NSB)
                        for n in range(NPB):
                            nn = m * NPB + n
                            last = pe.matmul(pz[m % 2][0:32, n * D:(n + 1) * D],
                                             kq[par1][:, nn, j1 * CH:(j1 + 1) * CH, :].rearrange("p t a -> p (t a)"), S[:, nn, :],
                                             start=True, stop=True)
                        last.then_inc(z_done, 1)

                    for m in range(NSB + 2):
                        if m < NSB:
                            update(m)
                        if m >= 2:
                            project(m - 2)

        @block.gpsimd
        def _(pool):
            pool.memset(ones3[KW:KW + 3, :], 1.0).then_inc(start, 1)
            pool.wait_ge(start, 1)
            pool.memset(S[:, :, :], 0.0).then_inc(start, 1)
            pool.memset(z[:, :, :, :], 0.0).then_inc(start, 1)
            pool.memset(Ac[:, 0, :], 1.0).then_inc(start, 1)
            pool.wait_ge(start, 4)
            pool.sem_inc(zs_done, NSB)
            pool.sem_inc(z_in, 64)
            pool.sem_inc(start, 1)

            def prepare(turn, u, uses):
                st = Steps(prep, PREP, turn)
                one = Ac[:, 0, :]
                pool.wait_ge(a_in[u], uses * 48)
                st.mark(pool.tensor_tensor(vv[u][:, :, :], vv[u][:, :, :], mid(bt[u][:, 0, :], 2, DH), ALU.mult))
                for t in range(CH):
                    if t:
                        st.wait(pool, n)
                    n = st.mark(pool.tensor_tensor(Ac[:, t + 1, :], Ac[:, t, :], av[u][:, t, :], ALU.mult))
                st.wait(pool, n)
                st.mark(pool.tensor_tensor(nbA[:, :, :], Ac[:, 0:CH, :], mid(bt[u][:, 1, :], 2, DH), ALU.mult))
                n = st.mark(pool.tensor_tensor(a3p[:, 0, :], Ac[:, CH, :], one, ALU.mult))
                st.wait(pool, n)
                n = st.mark(pool.tensor_tensor(r1[:, :], Ac[:, CH, :], a3p[:, 0, :], ALU.subtract))
                st.wait(pool, n)
                n = st.mark(pool.tensor_tensor(a3p[:, 1, :], r1[:, :], one, ALU.mult))
                st.wait(pool, n)
                n = st.mark(pool.tensor_tensor(r1[:, :], r1[:, :], a3p[:, 1, :], ALU.subtract))
                st.wait(pool, n)
                st.mark(pool.tensor_tensor(a3p[:, 2, :], r1[:, :], one, ALU.mult))
                st.end()

            prepare(0, 0, 1)
            with pool.Fori(0, TURNS) as i:
                for cc in range(LOOP):
                    c = i * LOOP + cc
                    nu = (cc + 1) % 2
                    pool.wait_ge(z_in, c * 64 + 64)
                    pool.tensor_tensor(zq[:, :, :], z[:, :, 1, :], Ac[:, 1:CH + 1, :], ALU.mult).then_inc(zq_done, 1)
                    pool.wait_ge(step, c * STEP + 1)
                    pool.wait_ge(A_in, (c + 1) * 48)
                    pool.wait_ge(zq_done, c + 1)
                    prepare(c + 1, nu, i * 4 + (cc + 1) // 2 + 1)
                    pool.wait_ge(step, c * STEP + STEP)
                    pool.tensor_tensor(o[:, :, :], o[:, :, :], zq[:, :, :], ALU.add).then_inc(o_sum, 1)
                    pool.wait_ge(o_sum, c + 1)
                    pool.dma_start(ov_d[:, bass.ds(c * CH, CH), :], o[:, :, :]).then_inc(o_out, 16)
            pool.wait_ge(o_out, 16 * NCH)
            for u in range(2):
                pool.wait_ge(kq_in[u], 16 * (T // SUP // 2 + (u == 0)))
            pool.wait_ge(z_in, 64 * (NCH + 1))
            pool.wait_ge(g2_in[0], 64 * (NCH // 2 + 1))
            pool.wait_ge(gs_out[0], 16 * (GB // 2) * (T // SUP + 1))
            pool.wait_ge(gs_out[1], 16 * (GB // 2) * (T // SUP + 1))

        @block.vector
        def _(dve):
            def beta_g(u):
                g = g2[u][:, 0:CH, 1, :]
                return dve.tensor_tensor(g, g, mid(bt[u][:, 1, :], 2, CH), ALU.mult)

            dve.wait_ge(a_in[0], 48)
            dve.wait_ge(g2_in[0], 64)
            dve.wait_ge(start, 5)
            beta_g(0).then_inc(start, 1)
            dve.wait_ge(start, 6)
            with dve.Fori(0, TURNS) as i:
                for cc in range(LOOP):
                    c = i * LOOP + cc
                    u = cc % 2
                    st = Steps(step, STEP, c)
                    dve.wait_ge(step, c * STEP)
                    dve.wait_ge(z_in, c * 64 + 64)
                    dve.wait_ge(prep, c * PREP + PREP)
                    n = st.mark(dve.tensor_tensor(pk[:, :, :], z[:, :, 0, :], nbA[:, :, :], ALU.mult))
                    st.wait(dve, n)
                    n = st.mark(dve.tensor_tensor(pk[:, :, :], pk[:, :, :], vv[u][:, :, :], ALU.add))
                    for t in range(CH):
                        w = w_at(t)
                        if t:
                            st.mark(dve.tensor_tensor(w[:, 0:t, :], w_at(t - 1), mid(av[u][:, t, :], 1, t), ALU.mult))
                        st.wait(dve, n)
                        n = st.mark(dve.tensor_reduce(w[:, t, :], pk[:, 0:t + 1, :].rearrange("p s d -> p d s"),
                                                      AX.X, ALU.add))
                        st.wait(dve, n)
                        if t < CH - 1:
                            n = st.mark(dve.tensor_tensor(pk[:, 0:t + 1, :], w, mid(g2[u][:, t + 1, 1, 0:t + 1], 2, DH),
                                                          ALU.mult))
                    assert st.n == W_END

                    def bank(m):
                        return S[:, m * NPB:(m + 1) * NPB, :].rearrange("p n d -> p (n d)")

                    def decay(banks):
                        for m in banks:
                            dve.wait_ge(A_done, c * NSB + m + 1)
                            dve.tensor_tensor(bank(m), bank(m), pA[m % 2][:, :], ALU.mult).then_inc(S_dec, 1)

                    decay(range(0, 2))
                    dve.wait_ge(wp_done, c * 2 + 1)
                    st.mark(dve.tensor_tensor(pk[:, :, :], w_at(CH - 1), wp[:, 0, :, :], ALU.subtract))
                    decay(range(2, 4))
                    dve.wait_ge(wp_done, c * 2 + 2)
                    dve.wait_ge(w_out[2], c * 16)
                    st.mark(dve.tensor_tensor(wp[:, 2, :, :], pk[:, :, :], wp[:, 1, :, :], ALU.subtract))
                    decay(range(4, NSB))

                    def q_sum(t):
                        dve.wait_ge(pq_done, c * CH + t + 1)
                        st.mark(dve.tensor_reduce(o[:, t, :], w_at(t).rearrange("p s d -> p d s"), AX.X, ALU.add))

                    BETWEEN = 13
                    dve.wait_ge(o_out, c * 16)
                    for m in range(NSB):
                        dve.wait_ge(U_done, c * NSB + m + 1)
                        dve.wait_ge(S_dec, c * NSB + m + 1)
                        dve.tensor_tensor(bank(m), bank(m), pU[m % 2][:, :], ALU.add).then_inc(S_done, 1)
                        if m < BETWEEN:
                            q_sum(m)
                    for t in range(BETWEEN, CH):
                        q_sum(t)
                    nu = (cc + 1) % 2
                    dve.wait_ge(a_in[nu], (i * 4 + (cc + 1) // 2 + 1) * 48)
                    dve.wait_ge(g2_in[nu], (i * 4 + (cc + 1) // 2 + 1) * 64)
                    st.mark(beta_g(nu))
                    st.end()


def attn_out(nc, x1, xnT_d, o_d, x2, Wg, Wo, ln_w, ln_b):
    with ExitStack() as ctx:
        s_ = Space(nc, ctx, "ao")
        wg = s_.sb("wg", [P, KH, C])
        wo = s_.sb("wo", [P, H, HID])
        lnw = s_.sb("lnw", [P, 1])
        lnb = s_.sb("lnb", [P, 1])
        o = s_.sb("o", [P, TT, C])
        oT = s_.sb("oT", [P, H, T])
        xnT = s_.sb("xnT", [P, KH, T])
        x = s_.sb("x", [P, TT, HID])
        st = s_.sb("st", [P, H, 6])
        mv = s_.sb("mv", [P, H, 2])
        ve = s_.sb("ve", [P, H])
        half = s_.sb("half", [P, H])
        rstd = s_.sb("rstd", [P, H])
        hold = s_.sb("hold", [P, 1])
        ident = s_.sb("ident", [P, P])
        gg = s_.sb("g", [P, H, T])
        pg = s_.ps("pg", 2)
        pt = s_.ps("pt", 2)
        po = s_.ps("po", 2)
        consts_done = s_.sem("consts_done")
        ln_in = s_.sem("ln_in")
        wg_in = s_.sems("wg_in", 2)
        wo_in = s_.sem("wo_in")
        o_in = s_.sem("o_in")
        o0_in = s_.sems("o0_in", 2)
        xT_in = s_.sem("xT_in")
        x_in = s_.sem("x_in")
        stats = s_.sem("stats")
        rstd_done = s_.sem("rstd_done")
        on_done = s_.sem("on_done")
        g_done = s_.sem("g_done")
        t_done = s_.sem("t_done")
        sig_done = s_.sem("sig_done")
        aff_done = s_.sem("aff_done")
        gated = s_.sem("gated")
        p_done = s_.sem("p_done")
        y_done = s_.sem("y_done")
        y_out = s_.sem("y_out")
        ov = o_d.rearrange("(t p) b c -> b p t c", p=P)
        xv = x1.rearrange("(b t p) h -> b p t h", t=TT, p=P)
        yv = x2.rearrange("(b t p) h -> b p t h", t=TT, p=P)
        STATS = 2 * H + 1
        block = ctx.enter_context(nc.Block())

        @block.sync
        def _(sp):
            sp.dma_start(o[:, 0, :], o_d[0:P, 0, :]).then_inc(o0_in[0], 16)
            sp.dma_start(xnT[:, :, :], xnT_d[:, :, 0:T]).then_inc(xT_in, 16)
            wgv = Wg.rearrange("(k p) c -> p k c", p=P)
            sp.dma_start(wg[:, :, 0:C // 2], wgv[:, :, 0:C // 2]).then_inc(wg_in[0], 16)
            sp.dma_start(o[:, 1:TT, :], ov[0][:, 1:TT, :]).then_inc(o0_in[1], 16)
            sp.dma_start(wg[:, :, C // 2:C], wgv[:, :, C // 2:C]).then_inc(wg_in[1], 16)
            sp.dma_start(lnw[:, :], ln_w.rearrange("(c o) -> c o", o=1)).then_inc(ln_in, 16)
            sp.dma_start(lnb[:, :], ln_b.rearrange("(c o) -> c o", o=1)).then_inc(ln_in, 16)
            sp.dma_start(x[:, :, :], xv[0]).then_inc(x_in, 16)
            sp.dma_start(wo[:, :, :], Wo.rearrange("(k p) c -> p k c", p=P)).then_inc(wo_in, 16)
            with sp.Fori(1, B) as b:
                sp.wait_ge(g_done, b * H)
                sp.dma_start(xnT[:, :, :], xnT_d[:, :, bass.ds(b * T, T)]).then_inc(xT_in, 16)
                sp.wait_ge(t_done, b * H)
                sp.dma_start(o[:, :, :], ov[b]).then_inc(o_in, 16)
                sp.wait_ge(y_out, b * 16)
                sp.dma_start(x[:, :, :], xv[b]).then_inc(x_in, 16)

        @block.gpsimd
        def _(pool):
            identity_step(pool, ident, consts_done)
            pool.memset(half[:, :], -0.5).then_inc(consts_done, 1)
            pool.wait_ge(consts_done, 3)

            def rstds(b):
                for t in range(TT):
                    pool.wait_ge(stats, b * (TT * STATS) + (t + 1) * STATS)
                    pool.tensor_tensor(rstd[:, :], ve[:, :], half[:, :], ALU.pow).then_inc(rstd_done, 1)

            def store(b):
                pool.wait_ge(y_done, b * TT + TT)
                pool.dma_start(yv[b], x[:, :, :]).then_inc(y_out, 16)

            rstds(0)
            with pool.Fori(0, B - 1) as b:
                rstds(b + 1)
                store(b)
            store(B - 1)
            pool.wait_ge(y_out, 16 * B)

        @block.tensor
        def _(pe):
            def gates(b, waits):
                for h in range(H):
                    if waits and h % (H // 2) == 0:
                        pe.wait_ge(wg_in[h // (H // 2)], 16)
                    pe.wait_ge(sig_done, b * H + h + 1)
                    for k in range(KH):
                        last = pe.matmul(pg[h % 2][:, :], wg[:, k, h * D:(h + 1) * D], xnT[:, k, :],
                                         start=(k == 0), stop=(k == KH - 1))
                    last.then_inc(g_done, 1)

            def project(b):
                pe.wait_ge(on_done, (b * TT + TT) * H)
                for h in range(H):
                    pe.wait_ge(aff_done, b * H + h + 1)
                    for t in range(TT):
                        last = pe.transpose(pt[h % 2][:, t * P:(t + 1) * P], o[:, t, h * D:(h + 1) * D], ident[:, :])
                    last.then_inc(t_done, 1)
                pe.wait_ge(gated, b * H + H)
                for t in range(TT):
                    if t >= 2:
                        pe.wait_ge(y_done, b * TT + t - 1)
                    else:
                        pe.wait_ge(y_done, b * TT)
                    for h in range(H):
                        last = pe.matmul(po[t % 2][:, :], oT[:, h, t * P:(t + 1) * P], wo[:, h, :],
                                         start=(h == 0), stop=(h == H - 1))
                    last.then_inc(p_done, 1)

            pe.sem_inc(sig_done, 2)
            pe.sem_inc(aff_done, 2)
            pe.wait_ge(consts_done, 2)
            pe.wait_ge(xT_in, 16)
            gates(0, True)
            pe.wait_ge(wo_in, 16)
            with pe.Fori(0, B - 1) as b:
                project(b)
                pe.wait_ge(xT_in, b * 16 + 32)
                gates(b + 1, False)
            project(B - 1)

        @block.scalar
        def _(act):
            act.wait_ge(ln_in, 32)
            with act.Fori(0, B) as b:
                for h in range(H):
                    act.wait_ge(g_done, b * H + h + 1)
                    act.wait_ge(gated, b * H)
                    act.activation(gg[:, h, :], pg[h % 2][:, :], ACT.Sigmoid).then_inc(sig_done, 1)
                for h in range(H):
                    act.wait_ge(t_done, b * H + h + 1)
                    act.wait_ge(p_done, b * TT)
                    act.activation(oT[:, h, :], pt[h % 2][:, :], ACT.Identity, bias=lnb[:, 0:1], scale=lnw[:, 0:1])\
                       .then_inc(aff_done, 1)

        @block.vector
        def _(dve):
            def normalise(b, t):
                s = Steps(stats, STATS, b * TT + t)
                for h in range(H):
                    n = s.mark(dve.bn_stats(st[:, h, :], o[:, t, h * D:(h + 1) * D]))
                s.wait(dve, n)
                dve.memset(hold[:, :], 0.0)
                for h in range(H):
                    n = s.mark(dve.bn_aggr(mv[:, h, :], st[:, h, :]))
                s.wait(dve, n)
                s.mark(dve.tensor_scalar(ve[:, :], mv[:, :, 1], EPS / S2, None, ALU.add))
                s.end()
                dve.wait_ge(rstd_done, b * TT + t + 1)
                for h in range(H):
                    blk = o[:, t, h * D:(h + 1) * D]
                    dve.tensor_scalar(blk, blk, mv[:, h, 0:1], rstd[:, h:h + 1], ALU.subtract, ALU.mult)\
                       .then_inc(on_done, 1)

            def gate(b):
                for h in range(H):
                    dve.wait_ge(aff_done, b * H + h + 3)
                    dve.tensor_tensor(oT[:, h, :], oT[:, h, :], gg[:, h, :], ALU.mult).then_inc(gated, 1)
                dve.wait_ge(x_in, b * 16 + 16)

            def residual(b, t):
                dve.wait_ge(p_done, b * TT + t + 1)
                dve.tensor_tensor(x[:, t, :], x[:, t, :], po[t % 2][:, :], ALU.add).then_inc(y_done, 1)

            for t in range(TT):
                if t < 2:
                    dve.wait_ge(o0_in[t], 16)
                normalise(0, t)
            with dve.Fori(0, B - 1) as b:
                gate(b)
                dve.wait_ge(o_in, b * 16 + 16)
                for t in range(TT):
                    normalise(b + 1, t)
                    residual(b, t)
            gate(B - 1)
            for t in range(TT):
                residual(B - 1, t)


def program(nc, t):
    ffn_w = [("wg", [P, KH, INTER]), ("wu", [P, KH, INTER]), ("wd", [P, OT, HID])]

    def scratch(name, shape, dt=F32):
        return nc.dram_tensor(name, tuple(shape), dt, kind="Internal").ap()

    ffn_d = [scratch(n + "_d", s) for n, s in ffn_w]
    x1, x2 = scratch("x1_d", [TOK, HID]), scratch("x2_d", [TOK, HID])
    xnT_d = scratch("xnT_d", [P, KH, TOK])
    a_d, v_d = (scratch(n, [T + CH, B, C]) for n in ("a_d", "v_d"))
    kt_d = scratch("kt_d", [3, T, B, C], BF16)
    o_d = scratch("o_d", [T, B, C])
    beta_d = scratch("beta_d", [NP, 2, T + CH])
    kq_d = scratch("kq_d", [P, N, T + SUP, 2])
    z_d = scratch("z_d", [4, 2 * CH, N * D // 4])
    w_d = scratch("w_d", [3 * CH, N * D], BF16)
    g_d = scratch("g_d", [2, SUP, 2, N, SUP])

    def with_weights(tag, body):
        with ExitStack() as ctx:
            body(*[ctx.enter_context(nc.sbuf_tensor(f"{tag}_{n}", s, F32)) for n, s in ffn_w])

    def second(wg, wu, wd):
        ffn(nc, "f2", wg, wu, wd, x2, t["out"], load=list(zip((wg, wu, wd), ffn_d)))

    quantised_ffn(nc, t["x"], x1, t["lut"], t["gate_idx"], t["up_idx"], t["down_idx"], *ffn_d)
    decays(nc, x1, xnT_d, a_d, beta_d, t["Wa"], t["ba"], t["Wb"], t["bb"])
    heads(nc, xnT_d, kq_d, kt_d, v_d, t["Wqkv"], t["conv"])
    scan(nc, kq_d, kt_d, v_d, a_d, beta_d, g_d, z_d, w_d, o_d)
    attn_out(nc, x1, xnT_d, o_d, x2, t["Wg"], t["Wo"], t["ln_w"], t["ln_b"])
    with_weights("m2", second)


def kernel(**inputs):
    import numpy as np
    import concourse.bacc as bacc
    from concourse.bass_utils import run_bass_kernel_spmd

    g = {k.split("_", 2)[2]: np.asarray(v) for k, v in inputs.items()}
    per_head = lambda W: W.reshape(H, D, KH, P).transpose(0, 3, 2, 1)
    qkv = np.stack([per_head(g[n]) for n in ("Wk", "Wv", "Wq")], axis=2)
    arrays = {
        "x": g["x"].reshape(TOK, HID),
        "lut": g["lut"],
        "gate_idx": g["gate_idx"].T, "up_idx": g["up_idx"].T, "down_idx": g["down_idx"].T,
        "Wa": g["Wa"].T, "ba": g["ba"],
        "Wb": np.repeat(g["Wb"], 2, axis=0).T, "bb": np.repeat(g["bb"], 2),
        "Wqkv": np.concatenate([qkv, qkv[0:1]]),
        "conv": np.stack([np.concatenate([g[n + "conv_w"], g[n + "conv_b"][:, None]], axis=1).reshape(H, D, K + 1)
                          for n in "kvq"], axis=2),
        "Wg": g["Wg"].T, "Wo": g["Wo"].T, "ln_w": g["ln_w"], "ln_b": g["ln_b"],
    }
    arrays = {f"in_{k}": np.ascontiguousarray(v) for k, v in arrays.items()}
    nc = bacc.Bacc("TRN2", target_bir_lowering=False, num_devices=1)
    t = {k[3:]: nc.dram_tensor(k, v.shape, mybir.dt.from_np(v.dtype), kind="ExternalInput").ap() for k, v in arrays.items()}
    t["out"] = nc.dram_tensor("out", (TOK, HID), F32, kind="ExternalOutput").ap()
    program(nc, t)
    r = run_bass_kernel_spmd(nc, [arrays], core_ids=[0])
    return r.results[0]["out"].reshape(B, T, HID)
```

```python
from contextlib import ExitStack

import concourse.bass as bass
from concourse import mybir

F32 = mybir.dt.float32
BF16 = mybir.dt.bfloat16
F32R = mybir.dt.float32r
I32 = mybir.dt.int32
ALU = mybir.AluOpType
ACT = mybir.ActivationFunctionType
AX = mybir.AxisListType

P = 128
B, T, HID = 4, 512, 512
TOK = B * T
H, D, K = 16, 128, 4
C = H * D
N = B * H
INTER, LUT = 1376, 16
KH = HID // P
OT = (INTER + P - 1) // P
OLAST = INTER - (OT - 1) * P
BLK = 512
NBLK = TOK // BLK
TT = BLK // P
EPS = 1e-5
S2 = 1.0 / D

CH = 16
SUP = 32
CPS = SUP // CH
NCH = T // CH
DH = 64
NP = N * D // DH
KW = 6 * CH
STACK = ((0, 3), (3 * CH, 2), (5 * CH, 1))
SBLK = 512
NSB = N * D // SBLK
NPB = SBLK // D


def mid(ap, axis, n):
    a = ap.unsqueeze(axis)
    shape = list(a.shape)
    shape[axis] = n
    return a.broadcast_to(shape)


class Steps:

    def __init__(self, sem, per, turn):
        self.sem, self.per, self.turn, self.n = sem, per, turn, 0

    def mark(self, ins):
        ins.then_inc(self.sem, 1)
        self.n += 1
        return self.n

    def wait(self, eng, n):
        eng.wait_ge(self.sem, self.turn * self.per + n)

    def end(self):
        assert self.n == self.per, (self.n, self.per)


class Space:

    def __init__(self, nc, ctx, tag):
        self.nc, self.ctx, self.tag = nc, ctx, tag

    def sb(self, name, shape, dt=F32):
        return self.ctx.enter_context(self.nc.sbuf_tensor(f"{self.tag}_{name}", shape, dt))

    def ps(self, name, n=1, shape=(P, 512), dt=F32):
        t = [self.ctx.enter_context(self.nc.psum_tensor(f"{self.tag}_{name}{j}", list(shape), dt)) for j in range(n)]
        return t if n > 1 else t[0]

    def sem(self, name):
        return self.ctx.enter_context(self.nc.semaphore(f"{self.tag}_{name}"))

    def sems(self, name, n):
        return [self.sem(f"{name}{j}") for j in range(n)]


def identity_step(pool, ident, sem):
    pool.memset(ident[:, :], 0.0).then_inc(sem, 1)
    pool.wait_ge(sem, 1)
    pool.affine_select(out=ident[:, :], in_=ident[:, :], compare_op=ALU.not_equal, fill=1.0, base=0,
                       pattern=[[-1, P]], channel_multiplier=1).then_inc(sem, 1)


def after(eng, sem, n):
    if n > 0:
        eng.wait_ge(sem, n)


def quantised_ffn(nc, x, x1, lut, gate_idx, up_idx, down_idx, wg_d, wu_d, wd_d):
    with ExitStack() as ctx:
        s_ = Space(nc, ctx, "f1")
        RING = 3
        PIECE = 2 * KH * P
        idx = [s_.sb(f"idx{j}", [P, PIECE], I32) for j in range(2)]
        idxb = [s_.sb(f"idxb{j}", [P, PIECE], BF16) for j in range(2)]
        hot = [s_.sb(f"hot{j}", [P, PIECE], BF16) for j in range(3)]
        gu = [s_.sb(f"gu{j}", [P, PIECE]) for j in range(RING)]
        wd = s_.sb("wd", [P, OT, HID])
        lut_sb = s_.sb("lut", [P, LUT])
        xt = [s_.sb(f"x{j}", [P, TT, HID]) for j in range(2)]
        xn = s_.sb("xn", [P, TT, HID])
        xnT = s_.sb("xnT", [P, KH, TOK])
        y = xnT[:, :, :].rearrange("p k t -> p (k t)").rearrange("p (t h) -> p t h", h=HID)
        hT = s_.sb("hT", [P, OT, TOK])
        sil = [s_.sb(f"sil{j}", [P, BLK]) for j in range(2)]
        st = s_.sb("st", [P, TT, 6])
        mv = s_.sb("mv", [P, TT, 2])
        ve = s_.sb("ve", [P, TT])
        half = s_.sb("half", [P, TT])
        rstd = s_.sb("rstd", [P, TT])
        hold = s_.sb("hold", [P, 1])
        ident = s_.sb("ident", [P, P])
        tp = s_.ps("tp", 2)
        pg = s_.ps("pg", 2)
        pu = s_.ps("pu", 2)
        po = s_.ps("po", 2)
        lut_in = s_.sem("lut_in")
        idx_in = s_.sems("idx_in", 2)
        cast_done = s_.sem("cast_done")
        hot_done = s_.sem("hot_done")
        acc_done = s_.sem("acc_done")
        stored = s_.sems("stored", RING)
        consts_done = s_.sem("consts_done")
        x_in = s_.sems("x_in", 2)
        stats = s_.sem("stats")
        rstd_done = s_.sem("rstd_done")
        xn_done = s_.sem("xn_done")
        tp_done = s_.sem("tp_done")
        tp_free = s_.sem("tp_free")
        gate_done = s_.sem("gate_done")
        up_done = s_.sem("up_done")
        sil_done = s_.sem("sil_done")
        h_done = s_.sem("h_done")
        o_done = s_.sem("o_done")
        y_done = s_.sem("y_done")
        y_out = s_.sem("y_out")
        xv = x.rearrange("(b t p) h -> b p t h", t=TT, p=P)
        yv = x1.rearrange("(b t p) h -> b p t h", t=TT, p=P)

        SLOTS = OT * NBLK
        WD = (OT + 1) // 2
        PIECES = OT + WD
        NT = TOK // P
        GROUPS = ((0, 4), (4, 8), (8, OT))
        ALL = PIECES * LUT
        STEPS = [min(LUT + (9 * (n + 1) + 1) // 2, ALL) for n in range(SLOTS)]

        def rows(o):
            return P if o < OT - 1 else OLAST

        def width(p):
            if p < OT:
                return 2 * KH * rows(p)
            return min(2, OT - 2 * (p - OT)) * HID

        def weight(p, mat, k):
            m = rows(p)
            return gu[p % RING][:, (mat * KH + k) * m:(mat * KH + k + 1) * m]

        def dest(p):
            if p < OT:
                return gu[p % RING][:, 0:width(p)]
            return wd[:, :, :].rearrange("p a h -> p (a h)")[:, 2 * (p - OT) * HID:2 * (p - OT) * HID + width(p)]

        def loads(p):
            return 2 if width(p) > HID or p < OT else 1

        def idx_count(p):
            return 16 * sum(loads(q) for q in range(p % 2, p + 1, 2))

        block = ctx.enter_context(nc.Block())

        @block.sync
        def _(sp):
            def load_idx(p):
                t = idx[p % 2]
                after(sp, cast_done, p - 1)
                if p < OT:
                    m = rows(p)
                    for j, src in enumerate((gate_idx, up_idx)):
                        sp.dma_start(t[:, j * KH * m:(j + 1) * KH * m].rearrange("p (k o) -> p k o", o=m),
                                     src[:, p * P:p * P + m].rearrange("(k p) o -> p k o", p=P)).then_inc(idx_in[p % 2], 16)
                else:
                    for j in range(loads(p)):
                        a = 2 * (p - OT) + j
                        m = rows(a)
                        if m < P:
                            sp.wait_ge(consts_done, 4)
                        sp.dma_start(t[0:m, j * HID:(j + 1) * HID], down_idx[a * P:a * P + m, :]).then_inc(idx_in[p % 2], 16)

            def load_x(b):
                sp.dma_start(xt[b % 2][:, :, :], xv[b]).then_inc(x_in[b % 2], 16)

            load_x(0)
            sp.dma_start(lut_sb[:, :], lut.rearrange("(o k) -> o k", o=1).broadcast_to([P, LUT])).then_inc(lut_in, 16)
            load_idx(0)
            load_x(1)
            load_idx(1)
            for b in (2, 3):
                sp.wait_ge(xn_done, (b - 1) * TT)
                load_x(b)
            for p in range(2, PIECES + 1):
                if p < PIECES:
                    load_idx(p)
                q = p - 2
                if q < OT:
                    m = rows(q)
                    sp.wait_ge(acc_done, LUT * (q + 1))
                    for j, d in enumerate((wg_d, wu_d)):
                        sp.dma_start(d[:, :, q * P:q * P + m],
                                     gu[q % RING][:, j * KH * m:(j + 1) * KH * m].rearrange("p (k o) -> p k o", o=m))\
                          .then_inc(stored[q % RING], 16)
            for b in range(NBLK):
                if b < 2:
                    sp.wait_ge(xn_done, (b + 3) * TT)
                else:
                    sp.wait_ge(y_done, (b - 1) * TT)
                load_x(b)
            sp.wait_ge(acc_done, ALL)
            sp.dma_start(wd_d, wd[:, :, :]).then_inc(y_out, 16)
            for b in range(NBLK):
                sp.wait_ge(y_done, (len(GROUPS) - 1) * NT + (b + 1) * TT)
                sp.dma_start(yv[b], y[:, b * TT:(b + 1) * TT, :]).then_inc(y_out, 16)
            sp.wait_ge(y_out, 16 * (NBLK + 1))
            for j in range(RING):
                sp.wait_ge(stored[j], 32 * len(range(j, OT, RING)))

        @block.gpsimd
        def _(pool):
            identity_step(pool, ident, consts_done)
            pool.memset(half[:, :], -0.5).then_inc(consts_done, 1)
            pool.wait_ge(consts_done, 3)
            for b in range(NBLK):
                pool.wait_ge(stats, (b + 1) * (2 * TT + 1))
                pool.tensor_tensor(rstd[:, :], ve[:, :], half[:, :], ALU.pow).then_inc(rstd_done, 1)
            last = PIECES - 1
            pool.wait_ge(cast_done, last - 1)
            pool.memset(idx[last % 2][OLAST:P, 0:HID], 0).then_inc(consts_done, 1)

        @block.tensor
        def _(pe):
            def transposes(b):
                pe.wait_ge(xn_done, (b + 1) * TT)
                for k in range(KH):
                    after(pe, tp_free, b * KH + k - 1)
                    for t in range(TT):
                        last = pe.transpose(tp[k % 2][:, t * P:(t + 1) * P], xn[:, t, k * P:(k + 1) * P], ident[:, :])
                    last.then_inc(tp_done, 1)

            def gate_up(o, b):
                n = o * NBLK + b
                m = rows(o)
                after(pe, h_done, n - 1)
                for mat, (bank, sem) in enumerate(((pg, gate_done), (pu, up_done))):
                    for k in range(KH):
                        last = pe.matmul(bank[n % 2][0:m, :], weight(o, mat, k), xnT[:, k, b * BLK:(b + 1) * BLK],
                                         start=(k == 0), stop=(k == KH - 1))
                    last.then_inc(sem, 1)

            pe.wait_ge(consts_done, 2)
            transposes(0)
            transposes(1)
            for o in range(OT):
                pe.wait_ge(acc_done, LUT * (o + 1))
                for b in range(NBLK):
                    if o == 0:
                        pe.wait_ge(tp_free, (b + 1) * KH)
                    gate_up(o, b)
                    if o == 0 and b + 2 < NBLK:
                        transposes(b + 2)
            pe.wait_ge(h_done, SLOTS)
            for g, (a0, a1) in enumerate(GROUPS):
                pe.wait_ge(acc_done, LUT * (OT + (a1 + 1) // 2))
                for t in range(NT):
                    after(pe, y_done, g * NT + t - 1)
                    for a in range(a0, a1):
                        m = rows(a)
                        last = pe.matmul(po[t % 2][:, :], hT[0:m, a, t * P:(t + 1) * P], wd[0:m, a, :],
                                         start=(a == a0), stop=(a == a1 - 1))
                    last.then_inc(o_done, 1)

        @block.scalar
        def _(act):
            def cast(p):
                act.wait_ge(idx_in[p % 2], idx_count(p))
                if p == PIECES - 1:
                    act.wait_ge(consts_done, 4)
                after(act, hot_done, LUT * (p - 1))
                act.activation(idxb[p % 2][:, 0:width(p)], idx[p % 2][:, 0:width(p)], ACT.Copy).then_inc(cast_done, 1)

            def copies(b):
                for k in range(KH):
                    act.wait_ge(tp_done, b * KH + k + 1)
                    act.activation(xnT[:, k, b * BLK:(b + 1) * BLK], tp[k % 2][:, :], ACT.Copy).then_inc(tp_free, 1)

            cast(0)
            cast(1)
            copies(0)
            copies(1)
            casts = 2
            for n in range(SLOTS):
                while casts < PIECES and LUT * (casts - 1) <= STEPS[n]:
                    cast(casts)
                    casts += 1
                m = rows(n // NBLK)
                act.wait_ge(gate_done, n + 1)
                after(act, h_done, n - 1)
                act.activation(sil[n % 2][0:m, :], pg[n % 2][0:m, :], ACT.Silu).then_inc(sil_done, 1)
                if n + 2 < NBLK:
                    copies(n + 2)
            while casts < PIECES:
                cast(casts)
                casts += 1

        @block.vector
        def _(dve):
            def normalise(b):
                steps = Steps(stats, 2 * TT + 1, b)
                xb = xt[b % 2]
                dve.wait_ge(x_in[b % 2], 16 * (b // 2 + 1))
                for t in range(TT):
                    n = steps.mark(dve.bn_stats(st[:, t, :], xb[:, t, :]))
                steps.wait(dve, n)
                dve.memset(hold[:, :], 0.0)
                for t in range(TT):
                    n = steps.mark(dve.bn_aggr(mv[:, t, :], st[:, t, :]))
                steps.wait(dve, n)
                steps.mark(dve.tensor_scalar(ve[:, :], mv[:, :, 1], EPS, None, ALU.add))
                steps.end()
                dve.wait_ge(rstd_done, b + 1)
                after(dve, tp_done, b * KH)
                for t in range(TT):
                    dve.tensor_scalar(xn[:, t, :], xb[:, t, :], mv[:, t, 0:1], rstd[:, t:t + 1],
                                      ALU.subtract, ALU.mult).then_inc(xn_done, 1)

            def dequantise(first, last):
                for n in range(first, last):
                    p, k = divmod(n, LUT)
                    w, d = width(p), dest(p)
                    if k == 0:
                        dve.wait_ge(cast_done, p + 1)
                        if RING <= p < OT:
                            dve.wait_ge(up_done, NBLK * (p - RING + 1))
                            dve.wait_ge(stored[p % RING], 32 * (p // RING))
                    for kk in [0, 1] if k == 0 else [k + 1] if k + 1 < LUT else []:
                        dve.tensor_scalar(hot[(LUT * p + kk) % 3][:, 0:w], idxb[p % 2][:, 0:w], float(kk), None,
                                          ALU.is_equal).then_inc(hot_done, 1)
                    dve.wait_ge(hot_done, n + 1)
                    if k == 0:
                        dve.tensor_scalar(d, hot[n % 3][:, 0:w], lut_sb[:, 0:1], None, ALU.mult).then_inc(acc_done, 1)
                    else:
                        dve.wait_ge(acc_done, n)
                        dve.scalar_tensor_tensor(d, hot[n % 3][:, 0:w], lut_sb[:, k:k + 1], d,
                                                 ALU.mult, ALU.add).then_inc(acc_done, 1)

            normalise(0)
            normalise(1)
            dve.wait_ge(lut_in, 16)
            dequantise(0, LUT)
            done = LUT
            for n in range(SLOTS):
                if n + 2 < NBLK:
                    normalise(n + 2)
                dequantise(done, STEPS[n])
                done = STEPS[n]
                o, b = divmod(n, NBLK)
                m = rows(o)
                dve.wait_ge(sil_done, n + 1)
                dve.wait_ge(up_done, n + 1)
                dve.tensor_tensor(hT[0:m, o, b * BLK:(b + 1) * BLK], sil[n % 2][0:m, :], pu[n % 2][0:m, :],
                                  ALU.mult).then_inc(h_done, 1)
            for g in range(len(GROUPS)):
                for t in range(NT):
                    more = min(done + 2, ALL)
                    dequantise(done, more)
                    done = more
                    b = t // TT
                    dve.wait_ge(o_done, g * NT + t + 1)
                    if g == 0:
                        if t % TT == 0:
                            dve.wait_ge(x_in[b % 2], 32 + 16 * (b // 2 + 1))
                        rest = xt[b % 2][:, t % TT, :]
                    else:
                        dve.wait_ge(y_done, (g - 1) * NT + t + 1)
                        rest = y[:, t, :]
                    dve.scalar_tensor_tensor(y[:, t, :], po[t % 2][:, :], 0.5, rest, ALU.mult, ALU.add).then_inc(y_done, 1)
            assert done == ALL


def ffn(nc, src, dst, wg_d, wu_d, wd_d):
    with ExitStack() as ctx:
        s_ = Space(nc, ctx, "f2")
        x = [s_.sb(f"x{j}", [P, TT, HID]) for j in range(2)]
        xn = s_.sb("xn", [P, TT, HID])
        xh, xl = (s_.sb(name, [P, KH, BLK], F32R) for name in ("xh", "xl"))
        wh, wl = (s_.sb(name, [P, 2, KH, INTER], F32R) for name in ("wh", "wl"))
        wd = s_.sb("wd", [P, OT, HID])
        hT = s_.sb("hT", [P, OT, BLK])
        whole = [w[:, :, :].rearrange("p a h -> p (a h)")[:, 0:KH * INTER].rearrange("p (k o) -> p k o", o=INTER)
                 for w in (wd, hT)]
        sil = [s_.sb(f"sil{j}", [P, BLK]) for j in range(2)]
        st = s_.sb("st", [P, TT, 6])
        mv = s_.sb("mv", [P, TT, 2])
        ve = s_.sb("ve", [P, TT])
        half = s_.sb("half", [P, TT])
        rstd = s_.sb("rstd", [P, TT])
        hold = s_.sb("hold", [P, 1])
        ident = s_.sb("ident", [P, P])
        tp = s_.ps("tp", 2)
        pg = s_.ps("pg", 2)
        pu = s_.ps("pu", 2)
        po = s_.ps("po", 2)
        w_in = s_.sem("w_in")
        consts_done = s_.sem("consts_done")
        x_in = s_.sems("x_in", 2)
        y_out = s_.sems("y_out", 2)
        stats = s_.sem("stats")
        rstd_done = s_.sem("rstd_done")
        xn_done = s_.sem("xn_done")
        tp_done = s_.sem("tp_done")
        hi_done = s_.sem("hi_done")
        lo_done = s_.sem("lo_done")
        gate_done = s_.sem("gate_done")
        up_done = s_.sem("up_done")
        sil_done = s_.sem("sil_done")
        h_done = s_.sem("h_done")
        o_done = s_.sem("o_done")
        y_done = s_.sem("y_done")
        xv = src.rearrange("(b t p) h -> b p t h", t=TT, p=P)
        yv = dst.rearrange("(b t p) h -> b p t h", t=TT, p=P)
        SLICES = 2 * KH

        def slice_count(n):
            return KH + n

        def token_count(n):
            return n + (SLICES if n > KH else 0)

        def rows(o):
            return P if o < OT - 1 else OLAST

        block = ctx.enter_context(nc.Block())

        @block.sync
        def _(sp):
            for b in range(2):
                sp.dma_start(x[b][:, :, :], xv[b]).then_inc(x_in[b], 16)
            sp.wait_ge(lo_done, slice_count(KH))
            sp.dma_start(wd[:, :, :], wd_d).then_inc(w_in, 16)
            for b in range(NBLK):
                u = b % 2
                sp.wait_ge(y_done, (b + 1) * TT)
                sp.dma_start(yv[b], x[u][:, :, :]).then_inc(y_out[u], 16)
                if b + 2 < NBLK:
                    sp.wait_ge(y_out[u], 16)
                    sp.dma_start(x[u][:, :, :], xv[b + 2]).then_inc(x_in[u], 16)
            for u in range(2):
                sp.wait_ge(y_out[u], 16 * NBLK // 2)

        @block.gpsimd
        def _(pool):
            identity_step(pool, ident, consts_done)
            pool.memset(half[:, :], -0.5).then_inc(consts_done, 1)
            pool.wait_ge(consts_done, 3)
            for b in range(NBLK):
                pool.wait_ge(stats, (b + 1) * (2 * TT + 1))
                pool.tensor_tensor(rstd[:, :], ve[:, :], half[:, :], ALU.pow).then_inc(rstd_done, 1)

        @block.tensor
        def _(pe):
            def transposes(b):
                pe.wait_ge(xn_done, (b + 1) * TT)
                for k in range(KH):
                    n = b * KH + k
                    if n >= 2:
                        pe.wait_ge(lo_done, token_count(n - 1))
                    for t in range(TT):
                        last = pe.transpose(tp[k % 2][:, t * P:(t + 1) * P], xn[:, t, k * P:(k + 1) * P], ident[:, :])
                    last.then_inc(tp_done, 1)

            pe.wait_ge(consts_done, 2)
            transposes(0)
            for b in range(NBLK):
                if b:
                    pe.wait_ge(lo_done, token_count((b + 1) * KH))
                for o in range(OT):
                    n = b * OT + o
                    m = rows(o)
                    after(pe, h_done, n - 1)
                    for mat, (bank, sem) in enumerate(((pg, gate_done), (pu, up_done))):
                        if n == 0:
                            pe.wait_ge(lo_done, slice_count((mat + 1) * KH))
                        passes = [(k, p, q) for k in range(KH) for p, q in ((wl, xh), (wh, xl), (wh, xh))]
                        for j, (k, p, q) in enumerate(passes):
                            last = pe.matmul(bank[n % 2][0:m, :], p[:, mat, k, o * P:o * P + m], q[:, k, :],
                                             start=(j == 0), stop=(j == len(passes) - 1))
                        last.then_inc(sem, 1)
                if b + 1 < NBLK:
                    transposes(b + 1)
                pe.wait_ge(h_done, (b + 1) * OT)
                pe.wait_ge(w_in, 48)
                for t in range(TT):
                    after(pe, y_done, b * TT + t - 1)
                    for o in range(OT):
                        m = rows(o)
                        last = pe.matmul(po[t % 2][:, :], hT[0:m, o, t * P:(t + 1) * P], wd[0:m, o, :],
                                         start=(o == 0), stop=(o == OT - 1))
                    last.then_inc(o_done, 1)

        @block.scalar
        def _(act):
            def high(b):
                after(act, up_done, b * OT)
                for k in range(KH):
                    act.wait_ge(tp_done, b * KH + k + 1)
                    act.activation(xh[:, k, :], tp[k % 2][:, :], ACT.Copy).then_inc(hi_done, 1)

            for w, d in zip(whole, (wg_d, wu_d)):
                act.dma_start(w, d).then_inc(w_in, 16)
            high(0)
            act.wait_ge(w_in, 32)
            for mat in range(2):
                for k in range(KH):
                    act.activation(wh[:, mat, k, :], whole[mat][:, k, :], ACT.Copy).then_inc(hi_done, 1)
            for b in range(NBLK):
                for o in range(OT):
                    n = b * OT + o
                    m = rows(o)
                    act.wait_ge(gate_done, n + 1)
                    after(act, h_done, n - 1)
                    act.activation(sil[n % 2][0:m, :], pg[n % 2][0:m, :], ACT.Silu).then_inc(sil_done, 1)
                if b + 1 < NBLK:
                    high(b + 1)

        @block.vector
        def _(dve):
            def normalise(b):
                steps = Steps(stats, 2 * TT + 1, b)
                xb = x[b % 2]
                dve.wait_ge(x_in[b % 2], 16 * (b // 2 + 1))
                for t in range(TT):
                    n = steps.mark(dve.bn_stats(st[:, t, :], xb[:, t, :]))
                steps.wait(dve, n)
                dve.memset(hold[:, :], 0.0)
                for t in range(TT):
                    n = steps.mark(dve.bn_aggr(mv[:, t, :], st[:, t, :]))
                steps.wait(dve, n)
                steps.mark(dve.tensor_scalar(ve[:, :], mv[:, :, 1], EPS, None, ALU.add))
                steps.end()
                dve.wait_ge(rstd_done, b + 1)
                after(dve, tp_done, b * KH)
                for t in range(TT):
                    dve.tensor_scalar(xn[:, t, :], xb[:, t, :], mv[:, t, 0:1], rstd[:, t:t + 1],
                                      ALU.subtract, ALU.mult).then_inc(xn_done, 1)

            def low(b):
                for k in range(KH):
                    dve.wait_ge(hi_done, token_count(b * KH + k + 1))
                    dve.tensor_tensor(xl[:, k, :], tp[k % 2][:, :], xh[:, k, :].bitcast(F32), ALU.subtract)\
                       .then_inc(lo_done, 1)

            normalise(0)
            low(0)
            for mat in range(2):
                for k in range(KH):
                    dve.wait_ge(hi_done, slice_count(mat * KH + k + 1))
                    dve.tensor_tensor(wl[:, mat, k, :], whole[mat][:, k, :], wh[:, mat, k, :].bitcast(F32), ALU.subtract)\
                       .then_inc(lo_done, 1)
            for b in range(NBLK):
                for o in range(OT):
                    n = b * OT + o
                    m = rows(o)
                    if o == OT // 2 and b + 1 < NBLK:
                        normalise(b + 1)
                    dve.wait_ge(sil_done, n + 1)
                    dve.wait_ge(up_done, n + 1)
                    if b:
                        dve.wait_ge(o_done, b * TT)
                    else:
                        dve.wait_ge(lo_done, slice_count(SLICES))
                    dve.tensor_tensor(hT[0:m, o, :], sil[n % 2][0:m, :], pu[n % 2][0:m, :], ALU.mult).then_inc(h_done, 1)
                if b + 1 < NBLK:
                    low(b + 1)
                for t in range(TT):
                    dve.wait_ge(o_done, b * TT + t + 1)
                    xt = x[b % 2][:, t, :]
                    dve.scalar_tensor_tensor(xt, po[t % 2][:, :], 0.5, xt, ALU.mult, ALU.add).then_inc(y_done, 1)


def decays(nc, x1, xnT_d, a_d, beta_d, Wa, ba, Wb, bb):
    with ExitStack() as ctx:
        s_ = Space(nc, ctx, "dc")
        x = [s_.sb(f"x{j}", [P, TT, HID]) for j in range(2)]
        xn = s_.sb("xn", [P, TT, HID])
        xnT = s_.sb("xnT", [P, KH, TOK])
        st = s_.sb("st", [P, TT, 6])
        mv = s_.sb("mv", [P, TT, 2])
        ve = s_.sb("ve", [P, TT])
        half = s_.sb("half", [P, TT])
        rstd = s_.sb("rstd", [P, TT])
        ident = s_.sb("ident", [P, P])
        wa = [s_.sb(f"wa{j}", [P, KH, BLK]) for j in range(2)]
        xh, xl = (s_.sb(name, [P, KH, TOK], F32R) for name in ("xh", "xl"))
        wah, wal = ([s_.sb(f"{name}{j}", [P, KH, BLK], F32R) for j in range(2)] for name in ("wah", "wal"))
        wb = s_.sb("wb", [P, KH, 2 * H])
        bab = s_.sb("bab", [P, C])
        bbc = s_.sb("bbc", [2 * H, 1])
        RA = 4
        sa = [s_.sb(f"sa{j}", [P, BLK]) for j in range(RA)]
        be = s_.sb("be", [2 * H, B, 2, T])
        tp = s_.ps("tp", 2)
        pa = s_.ps("pa", 4)
        consts_done = s_.sem("consts_done")
        x_in = s_.sems("x_in", 2)
        w_in = s_.sem("w_in")
        wa_in = s_.sems("wa_in", 2)
        stats = s_.sem("stats")
        rstd_done = s_.sem("rstd_done")
        xn_done = s_.sem("xn_done")
        tp_done = s_.sem("tp_done")
        tp_free = s_.sem("tp_free")
        hi_done = s_.sem("hi_done")
        lo_done = s_.sem("lo_done")
        b_done = s_.sem("b_done")
        beta_done = s_.sem("beta_done")
        kept_out = s_.sem("kept_out")
        pa_done = s_.sem("pa_done")
        sum_done = s_.sem("sum_done")
        sig_done = s_.sem("sig_done")
        a_out = s_.sems("a_out", RA)
        xv = x1.rearrange("(b t p) h -> b p t h", t=TT, p=P)
        wav = Wa.rearrange("(k p) c -> p k c", p=P)
        NT = TOK // P
        CB = C // BLK
        block = ctx.enter_context(nc.Block())

        @block.sync
        def _(sp):
            sp.dma_start(x[0][:, :, :], xv[0]).then_inc(x_in[0], 16)
            sp.dma_start(x[1][:, :, :], xv[1]).then_inc(x_in[1], 16)
            sp.dma_start(wb[:, :, :], Wb.rearrange("(k p) c -> p k c", p=P)).then_inc(w_in, 16)
            sp.dma_start(bab[:, :], ba.rearrange("(o c) -> o c", o=1).broadcast_to([P, C])).then_inc(w_in, 16)
            sp.dma_start(bbc[:, :], bb.rearrange("(c o) -> c o", o=1)).then_inc(w_in, 16)
            for u in range(2):
                sp.dma_start(wa[u][:, :, :], wav[:, :, u * BLK:(u + 1) * BLK]).then_inc(wa_in[u], 16)
            for blk in range(2, NBLK):
                sp.wait_ge(xn_done, (blk - 1) * TT)
                sp.dma_start(x[blk % 2][:, :, :], xv[blk]).then_inc(x_in[blk % 2], 16)
            sp.wait_ge(tp_free, NBLK * KH + 2)
            sp.dma_start(xnT_d, xnT[:, :, :]).then_inc(kept_out, 16)
            sp.wait_ge(beta_done, 2 * B)
            bv = beta_d.rearrange("(b q) c t -> q b c t", b=B)
            for b in range(B):
                sp.dma_start(bv[:, b, :, 0:T], be[:, b]).then_inc(kept_out, 16)
            for cb in range(2, CB):
                sp.wait_ge(lo_done, NBLK + cb - 1)
                sp.dma_start(wa[cb % 2][:, :, :], wav[:, :, cb * BLK:(cb + 1) * BLK]).then_inc(wa_in[cb % 2], 16)
            for cb in range(CB):
                with sp.Fori(0, NT // RA) as j:
                    for r in range(RA):
                        sp.wait_ge(sig_done, j * RA + (cb * NT + r + 1))
                        sp.dma_start(a_d[r * P:(r + 1) * P, j, cb * BLK:(cb + 1) * BLK], sa[r][:, :])\
                          .then_inc(a_out[r], 16)
            sp.wait_ge(kept_out, 16 * (B + 1))
            for r in range(RA):
                sp.wait_ge(a_out[r], 16 * CB * NT // RA)

        @block.gpsimd
        def _(pool):
            identity_step(pool, ident, consts_done)
            pool.memset(half[:, :], -0.5).then_inc(consts_done, 1)
            pool.wait_ge(consts_done, 3)
            for blk in range(NBLK):
                pool.wait_ge(stats, (blk + 1) * (2 * TT + 1))
                pool.tensor_tensor(rstd[:, :], ve[:, :], half[:, :], ALU.pow).then_inc(rstd_done, 1)

        @block.tensor
        def _(pe):
            pe.sem_inc(tp_free, 2)
            pe.sem_inc(sum_done, 4)
            pe.wait_ge(consts_done, 2)
            for blk in range(NBLK):
                pe.wait_ge(xn_done, (blk + 1) * TT)
                for k in range(KH):
                    pe.wait_ge(tp_free, blk * KH + k + 1)
                    for t in range(TT):
                        last = pe.transpose(tp[k % 2][:, t * P:(t + 1) * P], xn[:, t, k * P:(k + 1) * P], ident[:, :])
                    last.then_inc(tp_done, 1)
            pe.wait_ge(tp_free, NBLK * KH + 2)
            pe.wait_ge(w_in, 48)
            for b in range(B):
                if b >= 2:
                    pe.wait_ge(beta_done, b - 1)
                for k in range(KH):
                    last = pe.matmul(tp[b % 2][0:2 * H, :], wb[:, k, :], xnT[:, k, b * T:(b + 1) * T],
                                     start=(k == 0), stop=(k == KH - 1))
                last.then_inc(b_done, 1)
            with pe.Fori(0, CB // 2) as i:
                for u in range(2):
                    pe.wait_ge(lo_done, i * 2 + (NBLK + u + 1))
                    for t in range(NT):
                        n = (i * 2 + u) * NT + t
                        pe.wait_ge(sum_done, n + 1)
                        passes = [(k, p, q) for k in range(KH) for p, q in ((xl, wah), (xh, wal), (xh, wah))]
                        for j, (k, p, q) in enumerate(passes):
                            last = pe.matmul(pa[t % 4][:, :], p[:, k, t * P:(t + 1) * P], q[u][:, k, :],
                                             start=(j == 0), stop=(j == len(passes) - 1))
                        last.then_inc(pa_done, 1)

        @block.scalar
        def _(act):
            for blk in range(NBLK):
                for k in range(KH):
                    act.wait_ge(tp_done, blk * KH + k + 1)
                    act.activation(xnT[:, k, blk * BLK:(blk + 1) * BLK], tp[k % 2][:, :], ACT.Copy).then_inc(tp_free, 1)
                act.wait_ge(tp_free, (blk + 1) * KH + 2)
                act.activation(xh[:, :, blk * BLK:(blk + 1) * BLK], xnT[:, :, blk * BLK:(blk + 1) * BLK], ACT.Copy)\
                   .then_inc(hi_done, 1)

            def high(cb):
                act.wait_ge(wa_in[cb % 2], 16 * (cb // 2 + 1))
                after(act, pa_done, (cb - 1) * NT if cb >= 2 else 0)
                act.activation(wah[cb % 2][:, :, :], wa[cb % 2][:, :, :], ACT.Copy).then_inc(hi_done, 1)

            high(0)
            high(1)
            act.wait_ge(w_in, 48)
            for b in range(B):
                act.wait_ge(b_done, b + 1)
                act.activation(be[:, b, 0, :], tp[b % 2][0:2 * H, :], ACT.Sigmoid, bias=bbc[:, 0:1]).then_inc(beta_done, 1)
            for b in range(B):
                act.wait_ge(beta_done, b + 1)
                act.activation(be[:, b, 1, :], be[:, b, 0, :], ACT.Copy, scale=-S2).then_inc(beta_done, 1)
            for cb in range(CB):
                with act.Fori(0, NT // RA) as i:
                    for r in range(RA):
                        act.wait_ge(sum_done, i * RA + (cb * NT + r + 1 + 4))
                        act.activation(sa[r][:, :], sa[r][:, :], ACT.Sigmoid).then_inc(sig_done, 1)
                if cb + 2 < CB:
                    high(cb + 2)

        @block.vector
        def _(dve):
            for blk in range(NBLK):
                steps = Steps(stats, 2 * TT + 1, blk)
                dve.wait_ge(x_in[blk % 2], (blk // 2 + 1) * 16)
                for t in range(TT):
                    n = steps.mark(dve.bn_stats(st[:, t, :], x[blk % 2][:, t, :]))
                steps.wait(dve, n)
                for t in range(TT):
                    m = steps.mark(dve.bn_aggr(mv[:, t, :], st[:, t, :]))
                steps.wait(dve, m)
                steps.mark(dve.tensor_scalar(ve[:, :], mv[:, :, 1], EPS, None, ALU.add))
                steps.end()
                dve.wait_ge(rstd_done, blk + 1)
                if blk:
                    dve.wait_ge(tp_done, blk * KH)
                for t in range(TT):
                    dve.tensor_scalar(xn[:, t, :], x[blk % 2][:, t, :], mv[:, t, 0:1], rstd[:, t:t + 1],
                                      ALU.subtract, ALU.mult).then_inc(xn_done, 1)
            for blk in range(NBLK):
                cols = slice(blk * BLK, (blk + 1) * BLK)
                dve.wait_ge(hi_done, blk + 1)
                dve.tensor_tensor(xl[:, :, cols], xnT[:, :, cols], xh[:, :, cols].bitcast(F32), ALU.subtract)\
                   .then_inc(lo_done, 1)

            def low(cb):
                dve.wait_ge(hi_done, NBLK + cb + 1)
                dve.tensor_tensor(wal[cb % 2][:, :, :], wa[cb % 2][:, :, :], wah[cb % 2][:, :, :].bitcast(F32),
                                  ALU.subtract).then_inc(lo_done, 1)

            low(0)
            low(1)
            dve.wait_ge(w_in, 48)
            for cb in range(CB):
                with dve.Fori(0, NT // RA) as j:
                    for r in range(RA):
                        dve.wait_ge(pa_done, j * RA + (cb * NT + r + 1))
                        dve.wait_ge(a_out[r], (j + cb * (NT // RA)) * 16)
                        dve.tensor_tensor(sa[r][:, :], pa[r][:, :], bab[:, cb * BLK:(cb + 1) * BLK], ALU.add)\
                           .then_inc(sum_done, 1)
                if cb + 2 < CB:
                    low(cb + 2)


def heads(nc, xnT_d, kq_d, kt_d, v_d, Wqkv, conv):
    with ExitStack() as ctx:
        s_ = Space(nc, ctx, "hd")
        x = [s_.sb(f"x{j}", [P, KH, T]) for j in range(2)]
        w = [s_.sb(f"w{j}", [P, 3, KH, P]) for j in range(2)]
        xh, xl = (s_.sb(name, [P, B, KH, T], F32R) for name in ("xh", "xl"))
        wh, wl = ([s_.sb(f"{name}{j}", [P, 3, KH, P], F32R) for j in range(2)] for name in ("wh", "wl"))
        cw = s_.sb("cw", [P, H, 3, K + 1])
        cwh = [s_.sb(f"cwh{j}", [P, 3, K + 1]) for j in range(2)]
        ident = s_.sb("ident", [P, P])
        R = 4
        yr = [s_.sb(f"y{j}", [P, T]) for j in range(R)]
        kq = [[s_.sb(f"kq{u}{b}", [P, T, 2]) for b in range(B)] for u in range(2)]
        vr = [s_.sb(f"v{b}", [P, T]) for b in range(B)]
        tr = [s_.sb(f"t{j}", [P, TT, P]) for j in range(B)]
        kp = [s_.sb(f"kp{j}", [P, 3, TT, P], BF16) for j in range(B)]
        kr = [s_.sb(f"kr{j}", [P, TT, P]) for j in range(B)]
        pp = s_.ps("pp", R)
        pt = s_.ps("pt", 2)
        consts_done = s_.sem("consts_done")
        x_in = s_.sems("x_in", 2)
        hi_done = s_.sem("hi_done")
        lo_done = s_.sem("lo_done")
        w_in = s_.sems("w_in", 2)
        cw_in = s_.sem("cw_in")
        cwh_done = s_.sem("cwh_done")
        proj_done = s_.sem("proj_done")
        conv_open = s_.sem("conv_open")
        taps = s_.sem("taps")
        conv_done = s_.sem("conv_done")
        silu_done = s_.sem("silu_done")
        tr_done = s_.sem("tr_done")
        v_free = s_.sem("v_free")
        k1_done = s_.sem("k1_done")
        k_free = s_.sem("k_free")
        k2_done = s_.sem("k2_done")
        k3_done = s_.sem("k3_done")
        kq_out = [s_.sems(f"kq_out{u}", B) for u in range(2)]
        v_out = s_.sems("v_out", B)
        k_out = s_.sems("k_out", B)
        UNITS = [(u, m, b) for u in range(2) for m in range(3) for b in range(B)]
        NU = len(UNITS)
        TRS = [n for n, (u, m, b) in enumerate(UNITS) if m < 2]

        def result(n):
            u, m, b = UNITS[n]
            return vr[b][:, :] if m == 1 else kq[u][b][:, :, m // 2]

        nth = {n: j for j, n in enumerate(TRS)}
        NTR = len(TRS)
        NKV = NTR // 2
        LAG_TR, LAG_EV, LAG_K3 = 2, 3, 4
        SPLITS = {2: (0, 1), NU // 2 + 2: (1, 0)}
        LOADS = {0: 0, 3: 1}
        FIRST = B + 1

        def bank_free(pe, i, j):
            if j < 2:
                pe.wait_ge(v_free, i * NKV)
            else:
                u, m, b = UNITS[TRS[j - 2]]
                pe.wait_ge((k_free, v_free)[m], i * NKV + u * B + b + 1)
        block = ctx.enter_context(nc.Block())

        @block.sync
        def _(sp):
            for b in range(B):
                after(sp, lo_done, b - 1)
                sp.dma_start(x[b % 2][:, :, :], xnT_d[:, :, b * T:(b + 1) * T]).then_inc(x_in[b % 2], 16)
            with sp.Fori(0, H // 2) as i:
                for n in range(NU + LAG_EV):
                    if n < NU and UNITS[n][1] == 2:
                        u, m, b = UNITS[n]
                        sp.wait_ge(silu_done, i * NU + n + 1)
                        sp.dma_start(kq_d[:, b * H + i * 2 + u, 0:T, :], kq[u][b][:, :, :]).then_inc(kq_out[u][b], 16)
                    if n - LAG_K3 in nth and UNITS[n - LAG_K3][1] == 0:
                        u, m, b = UNITS[n - LAG_K3]
                        sp.wait_ge(k3_done, i * NKV + u * B + b + 1)
                        for part in range(3):
                            dst = kt_d[part, 0:T, b, :].rearrange("(t p) (i c) -> i p t c", p=P, c=2 * D)[i]
                            sp.dma_start(dst[:, :, u * D:(u + 1) * D], kp[b][:, part, :, :]).then_inc(k_out[b], 16)
            for b in range(B):
                for u in range(2):
                    sp.wait_ge(kq_out[u][b], 16 * (H // 2))
                sp.wait_ge(k_out[b], 48 * H)

        @block.gpsimd
        def _(pool):
            identity_step(pool, ident, consts_done)
            pool.dma_start(cw[:, :, :, :], conv.rearrange("h p m k -> p h m k")).then_inc(cw_in, 16)
            pool.dma_start(w[0][:, :, :, :], Wqkv[0]).then_inc(w_in[0], 16)
            pool.wait_ge(lo_done, FIRST)
            with pool.Fori(0, H // 2) as i:
                for n in range(NU):
                    if n in LOADS:
                        u = LOADS[n]
                        pool.wait_ge(lo_done, i * 2 + (FIRST - 1 + u))
                        pool.dma_start(w[1 - u][:, :, :, :], Wqkv[i * 2 + (u + 1)]).then_inc(w_in[1 - u], 16)
                    if n in SPLITS:
                        more, v = SPLITS[n]
                        pool.wait_ge(hi_done, i * 2 + (FIRST + 1 + more))
                        pool.tensor_tensor(wl[v][:, :, :, :], w[v][:, :, :, :], wh[v][:, :, :, :].bitcast(F32), ALU.subtract)\
                            .then_inc(lo_done, 1)
                    if n - LAG_EV in nth and UNITS[n - LAG_EV][1] == 1:
                        u, m, b = UNITS[n - LAG_EV]
                        pool.wait_ge(v_free, i * NKV + u * B + b + 1)
                        dst = v_d[0:T, b, :].rearrange("(t p) (h c) -> h p t c", p=P, c=D)
                        pool.dma_start(dst[i * 2 + u], tr[b][:, :, :]).then_inc(v_out[b], 16)
                    if n - LAG_K3 in nth and UNITS[n - LAG_K3][1] == 0:
                        u, m, b = UNITS[n - LAG_K3]
                        pool.wait_ge(k2_done, i * NKV + u * B + b + 1)
                        pool.tensor_tensor(kp[b][:, 2, :, :], kr[b][:, :, :], kp[b][:, 1, :, :], ALU.subtract)\
                            .then_inc(k3_done, 1)
            for b in range(B):
                pool.wait_ge(v_out[b], 16 * H)

        @block.tensor
        def _(pe):
            pe.sem_inc(conv_done, R)
            pe.wait_ge(consts_done, 2)
            pe.wait_ge(lo_done, FIRST)
            with pe.Fori(0, H // 2) as i:
                for n in range(NU):
                    u, m, b = UNITS[n]
                    if m == 0 and b == 0:
                        pe.wait_ge(lo_done, i * 2 + (FIRST + u))
                    pe.wait_ge(conv_done, i * NU + n + 1)
                    passes = [(k, p, q) for k in range(KH) for p, q in ((wl, xh), (wh, xl), (wh, xh))]
                    for j, (k, p, q) in enumerate(passes):
                        last = pe.matmul(pp[n % R][:, :], p[u][:, m, k, :], q[:, b, k, :],
                                         start=(j == 0), stop=(j == len(passes) - 1))
                    last.then_inc(proj_done, 1)
                    if n - LAG_TR in nth:
                        j = nth[n - LAG_TR]
                        pe.wait_ge(silu_done, i * NU + n - LAG_TR + 1)
                        bank_free(pe, i, j)
                        for t in range(TT):
                            last = pe.transpose(pt[j % 2][:, t * P:(t + 1) * P],
                                                result(n - LAG_TR)[:, t * P:(t + 1) * P], ident[:, :])
                        last.then_inc(tr_done, 1)

        @block.scalar
        def _(act):
            for b in range(B):
                act.wait_ge(x_in[b % 2], 16 * (b // 2 + 1))
                act.activation(xh[:, b, :, :], x[b % 2][:, :, :], ACT.Copy).then_inc(hi_done, 1)

            def high(u):
                act.activation(wh[u][:, :, :, :], w[u][:, :, :, :], ACT.Copy).then_inc(hi_done, 1)

            act.wait_ge(w_in[0], 16)
            high(0)
            act.wait_ge(cw_in, 16)

            def silu(i, n):
                u, m, b = UNITS[n]
                act.wait_ge(conv_done, i * NU + n + 1 + R)
                if m != 1:
                    act.wait_ge(kq_out[u][b], i * 16)
                else:
                    act.wait_ge(tr_done, i * NTR + (nth[n - 3 * B] + 1 if u else 0))
                act.activation(result(n), yr[n % R][:, :], ACT.Silu).then_inc(silu_done, 1)

            with act.Fori(0, H // 2) as i:
                for n in range(NU):
                    u, m, b = UNITS[n]
                    if m == 0 and b == 0:
                        act.wait_ge(conv_done, i * NU + R)
                        act.activation(cwh[u][:, :, :], cw[:, bass.ds(i * 2 + u, 1), :, :].rearrange("p o m k -> p (o m) k"),
                                       ACT.Copy).then_inc(cwh_done, 1)
                        act.wait_ge(cwh_done, i * 2 + u + 1)
                    act.wait_ge(proj_done, i * NU + n + 1)
                    if n in SPLITS:
                        more, v = SPLITS[n]
                        act.wait_ge(w_in[v], i * 16 + (16 + 16 * more))
                        high(v)
                    act.activation(yr[n % R][:, :], pp[n % R][:, :], ACT.Identity,
                                   bias=cwh[u][:, m, K:K + 1], scale=cwh[u][:, m, K - 1:K]).then_inc(conv_open, 1)
                    if n >= 1:
                        silu(i, n - 1)
                    if n - LAG_EV in nth:
                        j = nth[n - LAG_EV]
                        u, m, b = UNITS[n - LAG_EV]
                        act.wait_ge(tr_done, i * NTR + j + 1)
                        if m:
                            act.wait_ge(v_out[b], i * 32 + u * 16)
                            act.activation(tr[b][:, :, :].rearrange("p t c -> p (t c)"), pt[j % 2][:, :], ACT.Copy)\
                               .then_inc(v_free, 1)
                        else:
                            act.wait_ge(k_out[b], i * 96 + u * 48)
                            act.activation(kp[b][:, 0, :, :].rearrange("p t c -> p (t c)"), pt[j % 2][:, :], ACT.Copy)\
                               .then_inc(k1_done, 1)
                    if n - LAG_K3 in nth and UNITS[n - LAG_K3][1] == 0:
                        u, m, b = UNITS[n - LAG_K3]
                        act.wait_ge(k_free, i * NKV + u * B + b + 1)
                        act.activation(kp[b][:, 1, :, :], kr[b][:, :, :], ACT.Copy).then_inc(k2_done, 1)
                silu(i, NU - 1)

        @block.vector
        def _(dve):
            for b in range(B):
                dve.wait_ge(hi_done, b + 1)
                dve.tensor_tensor(xl[:, b, :, :], x[b % 2][:, :, :], xh[:, b, :, :].bitcast(F32), ALU.subtract)\
                   .then_inc(lo_done, 1)

            dve.wait_ge(hi_done, FIRST)
            dve.tensor_tensor(wl[0][:, :, :, :], w[0][:, :, :, :], wh[0][:, :, :, :].bitcast(F32), ALU.subtract)\
               .then_inc(lo_done, 1)
            with dve.Fori(0, H // 2) as i:
                for n in range(NU):
                    u, m, b = UNITS[n]
                    dve.wait_ge(conv_open, i * NU + n + 1)
                    y, p = yr[n % R], pp[n % R]
                    for j in range(1, K):
                        ins = dve.scalar_tensor_tensor(y[:, j:T], p[:, 0:T - j], cwh[u][:, m, K - 1 - j:K - j],
                                                       y[:, j:T], ALU.mult, ALU.add)
                        if j < K - 1:
                            ins.then_inc(taps, 1)
                            dve.wait_ge(taps, i * (2 * NU) + 2 * n + j)
                        else:
                            ins.then_inc(conv_done, 1)
                    if n - LAG_EV in nth and UNITS[n - LAG_EV][1] == 0:
                        u, m, b = UNITS[n - LAG_EV]
                        dve.wait_ge(k1_done, i * NKV + u * B + b + 1)
                        dve.tensor_tensor(kr[b][:, :, :].rearrange("p t c -> p (t c)"), pt[nth[n - LAG_EV] % 2][:, :],
                                          kp[b][:, 0, :, :].rearrange("p t c -> p (t c)"), ALU.subtract).then_inc(k_free, 1)


def scan(nc, kq_d, kt_d, v_d, a_d, beta_d, g_d, z_d, w_d, o_d):
    with ExitStack() as ctx:
        s_ = Space(nc, ctx, "sc")
        S = s_.sb("S", [P, N, D])
        kq = [s_.sb(f"kq{j}", [P, N, SUP, 2]) for j in range(2)]
        kt = s_.sb("kt", [P, N, D], BF16)
        wt = s_.sb("wt", [P, N, D], BF16)
        A3 = wt[KW:KW + 3, :, :].rearrange("p n d -> p (n d)")
        za = s_.sb("za", [P, N // 4, D])
        gs = [s_.sb(f"gs{j}", [2 * SUP, SBLK]) for j in range(2)]
        av = [s_.sb(f"a{j}", [P, CH, DH]) for j in range(2)]
        vv = [s_.sb(f"v{j}", [P, CH, DH]) for j in range(2)]
        bt = [s_.sb(f"bt{j}", [P, 2, CH]) for j in range(2)]
        g2 = [s_.sb(f"g2{j}", [P, CH + 1, 2, CH]) for j in range(2)]
        z = s_.sb("z", [P, CH, 2, DH])
        zq = s_.sb("zq", [P, CH, DH])
        pk = s_.sb("pk", [P, CH, DH])
        hist = s_.sb("hist", [P, CH * (CH + 1) // 2, DH])
        wp = s_.sb("wp", [P, 3, CH, DH], BF16)
        o = s_.sb("o", [P, CH, DH])
        Ac = s_.sb("Ac", [P, CH + 1, DH])
        nbA = s_.sb("nbA", [P, CH, DH])
        r1 = s_.sb("r1", [P, DH])
        a3p = s_.sb("a3p", [P, 3, DH], BF16)
        ones3 = s_.sb("ones3", [KW + 3, P], BF16)
        pA = s_.ps("pA", 2)
        pU = s_.ps("pU", 2)
        pz = s_.ps("pz", 2)
        pG = s_.ps("pG", 2)

        start = s_.sem("start")
        pad_done = s_.sem("pad_done")
        kq_in = s_.sems("kq_in", 2)
        kt_in = s_.sem("kt_in")
        a_in = s_.sems("a_in", 2)
        g2_in = s_.sems("g2_in", 2)
        g_done = s_.sem("g_done")
        gs_done = s_.sem("gs_done")
        gs_out = s_.sems("gs_out", 2)
        z_done = s_.sem("z_done")
        zs_done = s_.sem("zs_done")
        z_out = s_.sems("z_out", 4)
        z_in = s_.sem("z_in")
        w_out = s_.sems("w_out", 3)
        pq_done = s_.sem("pq_done")
        prep = s_.sem("prep")
        zq_done = s_.sem("zq_done")
        o_sum = s_.sem("o_sum")
        o_out = s_.sem("o_out")
        step = s_.sem("step")
        w_in = s_.sem("w_in")
        wp_done = s_.sem("wp_done")
        A_in = s_.sem("A_in")
        A_done = s_.sem("A_done")
        U_done = s_.sem("U_done")
        S_dec = s_.sem("S_dec")
        S_done = s_.sem("S_done")

        LOOP = 8
        TURNS = NCH // LOOP
        GB = N * SUP // SBLK
        GN = SBLK // SUP
        PREP = CH + 7
        W_END = 4 + 3 * (CH - 2) + 2
        STEP = W_END + 2 + CH + 1
        SPT = LOOP // CPS

        def w_at(t):
            return hist[:, t * (t + 1) // 2:(t + 1) * (t + 2) // 2, :]

        gdv = g_d
        av_d = a_d.rearrange("t b (q d) -> (b q) t d", d=DH)
        vv_d = v_d.rearrange("t b (q d) -> (b q) t d", d=DH)
        ov_d = o_d.rearrange("t b (q d) -> (b q) t d", d=DH)
        block = ctx.enter_context(nc.Block())

        def load_chunk(sp, u, t0):
            sp.dma_start(av[u][:, :, :], av_d[:, bass.ds(t0, CH), :]).then_inc(a_in[u], 16)
            sp.dma_start(vv[u][:, :, :], vv_d[:, bass.ds(t0, CH), :]).then_inc(a_in[u], 16)
            sp.dma_start(bt[u][:, :, :], beta_d[:, :, bass.ds(t0, CH)]).then_inc(a_in[u], 16)

        def load_kt(sp, t0):
            for r, parts in STACK:
                for part in range(parts):
                    lo = r + part * CH
                    sp.dma_start(kt[lo:lo + CH, :, :].rearrange("s n d -> s (n d)"),
                                 kt_d[part, bass.ds(t0, CH)].rearrange("t b c -> t (b c)")).then_inc(kt_in, 16)

        def load_g(sp, u, par, j):
            for half in range(2):
                for q in range(2):
                    src = gdv[par, j * CH:(j + 1) * CH, q, :, j * CH:(j + 1) * CH].rearrange("t n s -> n t s")
                    dst = g2[u][half:P:2, q:q + CH, 1 - q, :]
                    sp.dma_start(dst, src).then_inc(g2_in[u], 16)

        @block.sync
        def _(sp):
            sp.dma_start(kq[0][:, :, :, :], kq_d[:, :, 0:SUP, :]).then_inc(kq_in[0], 16)
            load_chunk(sp, 0, 0)
            for m in range(GB):
                sp.wait_ge(gs_done, m + 1)
                sp.dma_start(gdv[0, :, :, m * GN:(m + 1) * GN, :].rearrange("t q n s -> (t q) n s"),
                             gs[m % 2][:, :].rearrange("p (n s) -> p n s", s=SUP)).then_inc(gs_out[m % 2], 16)
            for m in range(2):
                sp.wait_ge(gs_out[m], 16 * GB // 2)
            load_g(sp, 0, 0, 0)
            sp.dma_start(kq_d[:, :, T:T + SUP, :], kq_d[:, :, 0:SUP, :]).then_inc(pad_done, 16)
            for d in (a_d, v_d):
                sp.dma_start(d[T:T + CH], d[0:CH]).then_inc(pad_done, 16)
            sp.dma_start(beta_d[:, :, T:T + CH], beta_d[:, :, 0:CH]).then_inc(pad_done, 16)
            sp.wait_ge(pad_done, 64)
            with sp.Fori(0, TURNS) as i:
                for cc in range(LOOP):
                    c = i * LOOP + cc
                    u, nu, j = cc % 2, (cc + 1) % 2, cc % CPS
                    banks_before = i * (LOOP * NSB) + cc * NSB
                    t_next = i * (LOOP * CH) + (cc + 1) * CH
                    if j == 0:
                        par = (cc // CPS + 1) % 2
                        nxt = (i * SPT + cc // CPS + 1) * SUP
                        sp.wait_ge(z_done, banks_before)
                        sp.dma_start(kq[par][:, :, :, :], kq_d[:, :, bass.ds(nxt, SUP), :]).then_inc(kq_in[par], 16)
                    if j == CPS - 1:
                        par = (cc // CPS + 1) % 2
                        sup = i * SPT + cc // CPS + 1
                        for m in range(GB):
                            sp.wait_ge(gs_done, sup * GB + m + 1)
                            sp.dma_start(gdv[par, :, :, m * GN:(m + 1) * GN, :].rearrange("t q n s -> (t q) n s"),
                                         gs[m % 2][:, :].rearrange("p (n s) -> p n s", s=SUP)).then_inc(gs_out[m % 2], 16)
                    sp.wait_ge(step, c * STEP)
                    sp.wait_ge(S_done, banks_before)
                    load_chunk(sp, nu, t_next)
                    load_kt(sp, i * (LOOP * CH) + cc * CH)
                    if j < CPS - 1:
                        load_g(sp, nu, (cc // CPS) % 2, j + 1)
                    sp.wait_ge(prep, c * PREP + PREP)
                    for r in range(3):
                        sp.dma_start(A3[r:r + 1, :].rearrange("o (p d) -> o p d", d=DH), a3p[:, r, :]).then_inc(A_in, 16)
                    if j == CPS - 1:
                        for m in range(2):
                            sp.wait_ge(gs_out[m], (i * SPT + cc // CPS + 2) * (16 * GB // 2))
                        load_g(sp, nu, (cc // CPS + 1) % 2, 0)
                    for part in range(3):
                        if part < 2:
                            sp.wait_ge(wp_done, c * 2 + (part + 1))
                        else:
                            sp.wait_ge(step, c * STEP + (W_END + 2))
                        sp.dma_start(w_d[part * CH:(part + 1) * CH, :].rearrange("s (p d) -> p s d", d=DH),
                                     wp[:, part, :, :]).then_inc(w_out[part], 16)
                    for part, (r, copies) in enumerate(STACK):
                        sp.wait_ge(w_out[part], c * 16 + 16)
                        for lo in range(r, r + copies * CH, CH):
                            sp.dma_start(wt[lo:lo + CH, :, :].rearrange("s n d -> s (n d)"),
                                         w_d[part * CH:(part + 1) * CH, :]).then_inc(w_in, 16)
                    sp.wait_ge(zq_done, c + 1)
                    for q in range(4):
                        sp.wait_ge(z_out[q], c * 16 + 16)
                        sp.dma_start(z[q * 32:(q + 1) * 32, :, :, :].rearrange("p t q d -> p (t q) d"),
                                     z_d[q].rearrange("r (p d) -> p r d", d=DH)).then_inc(z_in, 16)

        @block.scalar
        def _(act):
            def g_banks(sup):
                for m in range(GB):
                    act.wait_ge(g_done, sup * GB + m + 1)
                    act.wait_ge(gs_out[m % 2], sup * (16 * GB // 2) + 16 * (m // 2))
                    act.activation(gs[m % 2][:, :], pG[m % 2][0:2 * SUP, :], ACT.Copy).then_inc(gs_done, 1)

            g_banks(0)
            with act.Fori(0, TURNS) as i:
                for cc in range(LOOP):
                    c = i * LOOP + cc
                    if cc % CPS == CPS - 1:
                        g_banks(i * SPT + cc // CPS + 1)

                    def q_terms(t):
                        for x in range(t + 1):
                            ins = act.activation(w_at(t)[:, x, :], w_at(t)[:, x, :], ACT.Copy, scale=g2[cc % 2][:, t + 1, 0, x:x + 1])
                        ins.then_inc(pq_done, 1)

                    act.wait_ge(g2_in[cc % 2], (i * 4 + cc // 2 + 1) * 64)
                    for t in range(CH - 2):
                        act.wait_ge(step, c * STEP + (3 * t + 5))
                        q_terms(t)
                    act.wait_ge(step, c * STEP + W_END)
                    act.wait_ge(w_out[0], c * 16)
                    act.activation(wp[:, 0, :, :], w_at(CH - 1), ACT.Copy).then_inc(wp_done, 1)
                    act.wait_ge(step, c * STEP + (W_END + 1))
                    act.wait_ge(w_out[1], c * 16)
                    act.activation(wp[:, 1, :, :], pk[:, :, :], ACT.Copy).then_inc(wp_done, 1)
                    q_terms(CH - 2)
                    q_terms(CH - 1)
                    for m in range(NSB):
                        q, mm = m // (NSB // 4), m % (NSB // 4)
                        act.wait_ge(z_done, (c + 1) * NSB + m + 1)
                        if m == 0:
                            act.wait_ge(z_in, c * 64 + 64)
                        act.activation(za[32 * q:32 * q + 32, mm * NPB:(mm + 1) * NPB, :].rearrange("p n d -> p (n d)"),
                                       pz[m % 2][0:32, :], ACT.Copy).then_inc(zs_done, 1)
                        if mm == NSB // 4 - 1:
                            act.wait_ge(zs_done, (c + 1) * NSB + m + 1)
                            act.dma_start(z_d[q], za[32 * q:32 * q + 32, :, :].rearrange("r n d -> r (n d)"))\
                               .then_inc(z_out[q], 16)

        @block.tensor
        def _(pe):
            def g_banks(sup, par):
                for m in range(GB):
                    if m >= 2:
                        pe.wait_ge(gs_done, sup * GB + m - 1)
                    else:
                        pe.wait_ge(gs_done, sup * GB)
                    for n in range(GN):
                        x = kq[par][:, m * GN + n, :, :]
                        last = pe.matmul(pG[m % 2][0:2 * SUP, n * SUP:(n + 1) * SUP], x.rearrange("p t a -> p (t a)"), x[:, :, 0],
                                         start=True, stop=True)
                    last.then_inc(g_done, 1)

            pe.wait_ge(kq_in[0], 16)
            g_banks(0, 0)
            pe.sem_inc(z_done, NSB)
            pe.wait_ge(start, 5)
            with pe.Fori(0, TURNS) as i:
                for cc in range(LOOP):
                    c = i * LOOP + cc
                    u = cc % 2
                    if cc % CPS == CPS - 1:
                        sup = cc // CPS + 1
                        pe.wait_ge(kq_in[sup % 2], i * (16 * SPT // 2) + 16 * (sup // 2 + 1))
                        g_banks(i * SPT + sup, sup % 2)
                    j1 = (cc + 1) % CPS
                    par1 = ((cc + 1) // CPS) % 2
                    pe.wait_ge(A_in, (c + 1) * 48)
                    for m in range(NSB):
                        if m >= 2:
                            pe.wait_ge(S_dec, c * NSB + m - 1)
                        pe.matmul(pA[m % 2][:, :], ones3[KW:KW + 3, :], A3[:, m * SBLK:(m + 1) * SBLK],
                                  start=True, stop=True).then_inc(A_done, 1)
                    pe.wait_ge(kt_in, c * 96 + 96)
                    pe.wait_ge(w_in, c * 96 + 96)

                    def update(m):
                        if m >= 2:
                            pe.wait_ge(S_done, c * NSB + m - 1)
                        for n in range(NPB):
                            nn = m * NPB + n
                            last = pe.matmul(pU[m % 2][:, n * D:(n + 1) * D], kt[0:KW, nn, :], wt[0:KW, nn, :],
                                             start=True, stop=True)
                        last.then_inc(U_done, 1)

                    def project(m):
                        pe.wait_ge(S_done, c * NSB + m + 1)
                        if m >= 2:
                            pe.wait_ge(zs_done, (c + 1) * NSB + m - 1)
                        else:
                            pe.wait_ge(zs_done, (c + 1) * NSB)
                        for n in range(NPB):
                            nn = m * NPB + n
                            last = pe.matmul(pz[m % 2][0:32, n * D:(n + 1) * D],
                                             kq[par1][:, nn, j1 * CH:(j1 + 1) * CH, :].rearrange("p t a -> p (t a)"), S[:, nn, :],
                                             start=True, stop=True)
                        last.then_inc(z_done, 1)

                    for m in range(NSB + 2):
                        if m < NSB:
                            update(m)
                        if m >= 2:
                            project(m - 2)

        @block.gpsimd
        def _(pool):
            pool.memset(ones3[KW:KW + 3, :], 1.0).then_inc(start, 1)
            pool.wait_ge(start, 1)
            pool.memset(S[:, :, :], 0.0).then_inc(start, 1)
            pool.memset(z[:, :, :, :], 0.0).then_inc(start, 1)
            pool.memset(Ac[:, 0, :], 1.0).then_inc(start, 1)
            pool.wait_ge(start, 4)
            pool.sem_inc(zs_done, NSB)
            pool.sem_inc(z_in, 64)
            pool.sem_inc(start, 1)

            def prepare(turn, u, uses):
                st = Steps(prep, PREP, turn)
                one = Ac[:, 0, :]
                pool.wait_ge(a_in[u], uses * 48)
                st.mark(pool.tensor_tensor(vv[u][:, :, :], vv[u][:, :, :], mid(bt[u][:, 0, :], 2, DH), ALU.mult))
                for t in range(CH):
                    if t:
                        st.wait(pool, n)
                    n = st.mark(pool.tensor_tensor(Ac[:, t + 1, :], Ac[:, t, :], av[u][:, t, :], ALU.mult))
                st.wait(pool, n)
                st.mark(pool.tensor_tensor(nbA[:, :, :], Ac[:, 0:CH, :], mid(bt[u][:, 1, :], 2, DH), ALU.mult))
                n = st.mark(pool.tensor_tensor(a3p[:, 0, :], Ac[:, CH, :], one, ALU.mult))
                st.wait(pool, n)
                n = st.mark(pool.tensor_tensor(r1[:, :], Ac[:, CH, :], a3p[:, 0, :], ALU.subtract))
                st.wait(pool, n)
                n = st.mark(pool.tensor_tensor(a3p[:, 1, :], r1[:, :], one, ALU.mult))
                st.wait(pool, n)
                n = st.mark(pool.tensor_tensor(r1[:, :], r1[:, :], a3p[:, 1, :], ALU.subtract))
                st.wait(pool, n)
                st.mark(pool.tensor_tensor(a3p[:, 2, :], r1[:, :], one, ALU.mult))
                st.end()

            prepare(0, 0, 1)
            with pool.Fori(0, TURNS) as i:
                for cc in range(LOOP):
                    c = i * LOOP + cc
                    nu = (cc + 1) % 2
                    pool.wait_ge(z_in, c * 64 + 64)
                    pool.tensor_tensor(zq[:, :, :], z[:, :, 1, :], Ac[:, 1:CH + 1, :], ALU.mult).then_inc(zq_done, 1)
                    pool.wait_ge(step, c * STEP + 1)
                    pool.wait_ge(A_in, (c + 1) * 48)
                    pool.wait_ge(zq_done, c + 1)
                    prepare(c + 1, nu, i * 4 + (cc + 1) // 2 + 1)
                    pool.wait_ge(step, c * STEP + STEP)
                    pool.tensor_tensor(o[:, :, :], o[:, :, :], zq[:, :, :], ALU.add).then_inc(o_sum, 1)
                    pool.wait_ge(o_sum, c + 1)
                    pool.dma_start(ov_d[:, bass.ds(c * CH, CH), :], o[:, :, :]).then_inc(o_out, 16)
            pool.wait_ge(o_out, 16 * NCH)
            for u in range(2):
                pool.wait_ge(kq_in[u], 16 * (T // SUP // 2 + (u == 0)))
            pool.wait_ge(z_in, 64 * (NCH + 1))
            pool.wait_ge(g2_in[0], 64 * (NCH // 2 + 1))
            pool.wait_ge(gs_out[0], 16 * (GB // 2) * (T // SUP + 1))
            pool.wait_ge(gs_out[1], 16 * (GB // 2) * (T // SUP + 1))

        @block.vector
        def _(dve):
            def beta_g(u):
                g = g2[u][:, 0:CH, 1, :]
                return dve.tensor_tensor(g, g, mid(bt[u][:, 1, :], 2, CH), ALU.mult)

            dve.wait_ge(a_in[0], 48)
            dve.wait_ge(g2_in[0], 64)
            dve.wait_ge(start, 5)
            beta_g(0).then_inc(start, 1)
            dve.wait_ge(start, 6)
            with dve.Fori(0, TURNS) as i:
                for cc in range(LOOP):
                    c = i * LOOP + cc
                    u = cc % 2
                    st = Steps(step, STEP, c)
                    dve.wait_ge(step, c * STEP)
                    dve.wait_ge(z_in, c * 64 + 64)
                    dve.wait_ge(prep, c * PREP + PREP)
                    n = st.mark(dve.tensor_tensor(pk[:, :, :], z[:, :, 0, :], nbA[:, :, :], ALU.mult))
                    st.wait(dve, n)
                    n = st.mark(dve.tensor_tensor(pk[:, :, :], pk[:, :, :], vv[u][:, :, :], ALU.add))
                    for t in range(CH):
                        w = w_at(t)
                        if t:
                            st.mark(dve.tensor_tensor(w[:, 0:t, :], w_at(t - 1), mid(av[u][:, t, :], 1, t), ALU.mult))
                        st.wait(dve, n)
                        n = st.mark(dve.tensor_reduce(w[:, t, :], pk[:, 0:t + 1, :].rearrange("p s d -> p d s"),
                                                      AX.X, ALU.add))
                        st.wait(dve, n)
                        if t < CH - 1:
                            n = st.mark(dve.tensor_tensor(pk[:, 0:t + 1, :], w, mid(g2[u][:, t + 1, 1, 0:t + 1], 2, DH),
                                                          ALU.mult))
                    assert st.n == W_END

                    def bank(m):
                        return S[:, m * NPB:(m + 1) * NPB, :].rearrange("p n d -> p (n d)")

                    def decay(banks):
                        for m in banks:
                            dve.wait_ge(A_done, c * NSB + m + 1)
                            dve.tensor_tensor(bank(m), bank(m), pA[m % 2][:, :], ALU.mult).then_inc(S_dec, 1)

                    decay(range(0, 2))
                    dve.wait_ge(wp_done, c * 2 + 1)
                    st.mark(dve.tensor_tensor(pk[:, :, :], w_at(CH - 1), wp[:, 0, :, :], ALU.subtract))
                    decay(range(2, 4))
                    dve.wait_ge(wp_done, c * 2 + 2)
                    dve.wait_ge(w_out[2], c * 16)
                    st.mark(dve.tensor_tensor(wp[:, 2, :, :], pk[:, :, :], wp[:, 1, :, :], ALU.subtract))
                    decay(range(4, NSB))

                    def q_sum(t):
                        dve.wait_ge(pq_done, c * CH + t + 1)
                        st.mark(dve.tensor_reduce(o[:, t, :], w_at(t).rearrange("p s d -> p d s"), AX.X, ALU.add))

                    sums = [t for t in range(CH - 1, CH - 5, -1)] + list(range(CH // 2 - 1))
                    rest = [t for t in range(CH) if t not in sums]
                    dve.wait_ge(o_out, c * 16)
                    for m in range(NSB):
                        dve.wait_ge(U_done, c * NSB + m + 1)
                        dve.wait_ge(S_dec, c * NSB + m + 1)
                        dve.tensor_tensor(bank(m), bank(m), pU[m % 2][:, :], ALU.add).then_inc(S_done, 1)
                        if m < len(sums):
                            q_sum(sums[m])
                    for t in rest:
                        q_sum(t)
                    nu = (cc + 1) % 2
                    dve.wait_ge(a_in[nu], (i * 4 + (cc + 1) // 2 + 1) * 48)
                    dve.wait_ge(g2_in[nu], (i * 4 + (cc + 1) // 2 + 1) * 64)
                    st.mark(beta_g(nu))
                    st.end()


def attn_out(nc, x1, xnT_d, o_d, x2, Wg, Wo, ln_w, ln_b):
    with ExitStack() as ctx:
        s_ = Space(nc, ctx, "ao")
        wg = s_.sb("wg", [P, KH, C])
        wo = s_.sb("wo", [P, H, HID])
        lnw = s_.sb("lnw", [P, 1])
        lnb = s_.sb("lnb", [P, 1])
        o = s_.sb("o", [P, TT, C])
        oT = s_.sb("oT", [P, H, T])
        xnT = s_.sb("xnT", [P, KH, T])
        x = s_.sb("x", [P, TT, HID])
        st = s_.sb("st", [P, H, 6])
        mv = s_.sb("mv", [P, H, 2])
        ve = s_.sb("ve", [P, H])
        half = s_.sb("half", [P, H])
        rstd = s_.sb("rstd", [P, H])
        hold = s_.sb("hold", [P, 1])
        ident = s_.sb("ident", [P, P])
        gg = s_.sb("g", [P, H, T])
        pg = s_.ps("pg", 2)
        pt = s_.ps("pt", 2)
        po = s_.ps("po", 2)
        consts_done = s_.sem("consts_done")
        wg_in = s_.sems("wg_in", 2)
        wo_in = s_.sem("wo_in")
        o_in = s_.sem("o_in")
        o0_in = s_.sems("o0_in", 2)
        xT_in = s_.sem("xT_in")
        x_in = s_.sem("x_in")
        stats = s_.sem("stats")
        rstd_done = s_.sem("rstd_done")
        on_done = s_.sem("on_done")
        g_done = s_.sem("g_done")
        t_done = s_.sem("t_done")
        sig_done = s_.sem("sig_done")
        aff_done = s_.sem("aff_done")
        gated = s_.sem("gated")
        p_done = s_.sem("p_done")
        y_done = s_.sem("y_done")
        y_out = s_.sem("y_out")
        ov = o_d.rearrange("(t p) b c -> b p t c", p=P)
        xv = x1.rearrange("(b t p) h -> b p t h", t=TT, p=P)
        yv = x2.rearrange("(b t p) h -> b p t h", t=TT, p=P)
        STATS = 2 * H + 1
        block = ctx.enter_context(nc.Block())

        @block.sync
        def _(sp):
            sp.dma_start(o[:, 0, :], o_d[0:P, 0, :]).then_inc(o0_in[0], 16)
            sp.dma_start(xnT[:, :, :], xnT_d[:, :, 0:T]).then_inc(xT_in, 16)
            wgv = Wg.rearrange("(k p) c -> p k c", p=P)
            sp.dma_start(wg[:, :, 0:C // 4], wgv[:, :, 0:C // 4]).then_inc(wg_in[0], 16)
            sp.dma_start(o[:, 1:TT, :], ov[0][:, 1:TT, :]).then_inc(o0_in[1], 16)
            sp.dma_start(wg[:, :, C // 4:C], wgv[:, :, C // 4:C]).then_inc(wg_in[1], 16)
            sp.dma_start(lnw[:, :], ln_w.rearrange("(c o) -> c o", o=1)).then_inc(wo_in, 16)
            sp.dma_start(lnb[:, :], ln_b.rearrange("(c o) -> c o", o=1)).then_inc(wo_in, 16)
            sp.dma_start(x[:, :, :], xv[0]).then_inc(x_in, 16)
            sp.dma_start(wo[:, :, :], Wo.rearrange("(k p) c -> p k c", p=P)).then_inc(wo_in, 16)
            with sp.Fori(1, B) as b:
                sp.wait_ge(g_done, b * H)
                sp.dma_start(xnT[:, :, :], xnT_d[:, :, bass.ds(b * T, T)]).then_inc(xT_in, 16)
                sp.wait_ge(t_done, b * H)
                sp.dma_start(o[:, :, :], ov[b]).then_inc(o_in, 16)
                sp.wait_ge(y_out, b * 16)
                sp.dma_start(x[:, :, :], xv[b]).then_inc(x_in, 16)

        @block.gpsimd
        def _(pool):
            identity_step(pool, ident, consts_done)
            pool.memset(half[:, :], -0.5).then_inc(consts_done, 1)
            pool.wait_ge(consts_done, 3)

            def rstds(b):
                for t in range(TT):
                    pool.wait_ge(stats, b * (TT * STATS) + (t + 1) * STATS)
                    pool.tensor_tensor(rstd[:, :], ve[:, :], half[:, :], ALU.pow).then_inc(rstd_done, 1)

            def store(b):
                pool.wait_ge(y_done, b * TT + TT)
                pool.dma_start(yv[b], x[:, :, :]).then_inc(y_out, 16)

            rstds(0)
            with pool.Fori(0, B - 1) as b:
                rstds(b + 1)
                store(b)
            store(B - 1)
            pool.wait_ge(y_out, 16 * B)

        @block.tensor
        def _(pe):
            def gates(b, waits):
                for h in range(H):
                    if waits and h in (0, H // 4):
                        pe.wait_ge(wg_in[min(h, 1)], 16)
                    pe.wait_ge(sig_done, b * H + h + 1)
                    for k in range(KH):
                        last = pe.matmul(pg[h % 2][:, :], wg[:, k, h * D:(h + 1) * D], xnT[:, k, :],
                                         start=(k == 0), stop=(k == KH - 1))
                    last.then_inc(g_done, 1)

            def project(b):
                pe.wait_ge(on_done, (b * TT + TT) * H)
                for h in range(H):
                    pe.wait_ge(aff_done, b * H + h + 1)
                    for t in range(TT):
                        last = pe.transpose(pt[h % 2][:, t * P:(t + 1) * P], o[:, t, h * D:(h + 1) * D], ident[:, :])
                    last.then_inc(t_done, 1)
                pe.wait_ge(gated, b * H + H)
                for t in range(TT):
                    if t >= 2:
                        pe.wait_ge(y_done, b * TT + t - 1)
                    else:
                        pe.wait_ge(y_done, b * TT)
                    for h in range(H):
                        last = pe.matmul(po[t % 2][:, :], oT[:, h, t * P:(t + 1) * P], wo[:, h, :],
                                         start=(h == 0), stop=(h == H - 1))
                    last.then_inc(p_done, 1)

            pe.sem_inc(sig_done, 2)
            pe.sem_inc(aff_done, 2)
            pe.wait_ge(consts_done, 2)
            pe.wait_ge(xT_in, 16)
            gates(0, True)
            pe.wait_ge(wo_in, 48)
            with pe.Fori(0, B - 1) as b:
                project(b)
                pe.wait_ge(xT_in, b * 16 + 32)
                gates(b + 1, False)
            project(B - 1)

        @block.scalar
        def _(act):
            with act.Fori(0, B) as b:
                for h in range(H):
                    act.wait_ge(g_done, b * H + h + 1)
                    act.wait_ge(gated, b * H)
                    act.activation(gg[:, h, :], pg[h % 2][:, :], ACT.Sigmoid).then_inc(sig_done, 1)
                act.wait_ge(wo_in, 48)
                for h in range(H):
                    act.wait_ge(t_done, b * H + h + 1)
                    act.wait_ge(p_done, b * TT)
                    act.activation(oT[:, h, :], pt[h % 2][:, :], ACT.Identity, bias=lnb[:, 0:1], scale=lnw[:, 0:1])\
                       .then_inc(aff_done, 1)

        @block.vector
        def _(dve):
            def normalise(b, t):
                s = Steps(stats, STATS, b * TT + t)
                for h in range(H):
                    n = s.mark(dve.bn_stats(st[:, h, :], o[:, t, h * D:(h + 1) * D]))
                s.wait(dve, n)
                dve.memset(hold[:, :], 0.0)
                for h in range(H):
                    n = s.mark(dve.bn_aggr(mv[:, h, :], st[:, h, :]))
                s.wait(dve, n)
                s.mark(dve.tensor_scalar(ve[:, :], mv[:, :, 1], EPS / S2, None, ALU.add))
                s.end()
                dve.wait_ge(rstd_done, b * TT + t + 1)
                for h in range(H):
                    blk = o[:, t, h * D:(h + 1) * D]
                    dve.tensor_scalar(blk, blk, mv[:, h, 0:1], rstd[:, h:h + 1], ALU.subtract, ALU.mult)\
                       .then_inc(on_done, 1)

            def gate(b):
                for h in range(H):
                    dve.wait_ge(aff_done, b * H + h + 3)
                    dve.tensor_tensor(oT[:, h, :], oT[:, h, :], gg[:, h, :], ALU.mult).then_inc(gated, 1)
                dve.wait_ge(x_in, b * 16 + 16)

            def residual(b, t):
                dve.wait_ge(p_done, b * TT + t + 1)
                dve.tensor_tensor(x[:, t, :], x[:, t, :], po[t % 2][:, :], ALU.add).then_inc(y_done, 1)

            for t in range(TT):
                if t < 2:
                    dve.wait_ge(o0_in[t], 16)
                normalise(0, t)
            with dve.Fori(0, B - 1) as b:
                gate(b)
                dve.wait_ge(o_in, b * 16 + 16)
                for t in range(TT):
                    normalise(b + 1, t)
                    residual(b, t)
            gate(B - 1)
            for t in range(TT):
                residual(B - 1, t)


def program(nc, t):
    ffn_w = [("wg", [P, KH, INTER]), ("wu", [P, KH, INTER]), ("wd", [P, OT, HID])]

    def scratch(name, shape, dt=F32):
        return nc.dram_tensor(name, tuple(shape), dt, kind="Internal").ap()

    ffn_d = [scratch(n + "_d", s) for n, s in ffn_w]
    x1, x2 = scratch("x1_d", [TOK, HID]), scratch("x2_d", [TOK, HID])
    xnT_d = scratch("xnT_d", [P, KH, TOK])
    a_d, v_d = (scratch(n, [T + CH, B, C]) for n in ("a_d", "v_d"))
    kt_d = scratch("kt_d", [3, T, B, C], BF16)
    o_d = scratch("o_d", [T, B, C])
    beta_d = scratch("beta_d", [NP, 2, T + CH])
    kq_d = scratch("kq_d", [P, N, T + SUP, 2])
    z_d = scratch("z_d", [4, 2 * CH, N * D // 4])
    w_d = scratch("w_d", [3 * CH, N * D], BF16)
    g_d = scratch("g_d", [2, SUP, 2, N, SUP])

    quantised_ffn(nc, t["x"], x1, t["lut"], t["gate_idx"], t["up_idx"], t["down_idx"], *ffn_d)
    decays(nc, x1, xnT_d, a_d, beta_d, t["Wa"], t["ba"], t["Wb"], t["bb"])
    heads(nc, xnT_d, kq_d, kt_d, v_d, t["Wqkv"], t["conv"])
    scan(nc, kq_d, kt_d, v_d, a_d, beta_d, g_d, z_d, w_d, o_d)
    attn_out(nc, x1, xnT_d, o_d, x2, t["Wg"], t["Wo"], t["ln_w"], t["ln_b"])
    ffn(nc, x2, t["out"], *ffn_d)


def kernel(**inputs):
    import numpy as np
    import concourse.bacc as bacc
    from concourse.bass_utils import run_bass_kernel_spmd

    g = {k.split("_", 2)[2]: np.asarray(v) for k, v in inputs.items()}
    per_head = lambda W: W.reshape(H, D, KH, P).transpose(0, 3, 2, 1)
    qkv = np.stack([per_head(g[n]) for n in ("Wk", "Wv", "Wq")], axis=2)
    arrays = {
        "x": g["x"].reshape(TOK, HID),
        "lut": g["lut"],
        "gate_idx": g["gate_idx"].T, "up_idx": g["up_idx"].T, "down_idx": g["down_idx"].T,
        "Wa": g["Wa"].T, "ba": g["ba"],
        "Wb": np.repeat(g["Wb"], 2, axis=0).T, "bb": np.repeat(g["bb"], 2),
        "Wqkv": np.concatenate([qkv, qkv[0:1]]),
        "conv": np.stack([np.concatenate([g[n + "conv_w"], g[n + "conv_b"][:, None]], axis=1).reshape(H, D, K + 1)
                          for n in "kvq"], axis=2),
        "Wg": g["Wg"].T, "Wo": g["Wo"].T, "ln_w": g["ln_w"], "ln_b": g["ln_b"],
    }
    arrays = {f"in_{k}": np.ascontiguousarray(v) for k, v in arrays.items()}
    nc = bacc.Bacc("TRN2", target_bir_lowering=False, num_devices=1)
    t = {k[3:]: nc.dram_tensor(k, v.shape, mybir.dt.from_np(v.dtype), kind="ExternalInput").ap() for k, v in arrays.items()}
    t["out"] = nc.dram_tensor("out", (TOK, HID), F32, kind="ExternalOutput").ap()
    program(nc, t)
    r = run_bass_kernel_spmd(nc, [arrays], core_ids=[0])
    return r.results[0]["out"].reshape(B, T, HID)
```
